# Optimizing a Trainium2 kernel written in Bass

```python
import numpy as np
import jax
import jax.numpy as jnp

def _softmax(x, axis=-1):
    return jax.nn.softmax(x, axis=axis)

def _gelu(x):
    return jax.nn.gelu(x, approximate=True)

def _silu(x):
    return jax.nn.silu(x)

def _sigmoid(x):
    return jax.nn.sigmoid(x)

def _layernorm(x, axis=-1, eps=1e-05):
    m = jnp.mean(x, axis=axis, keepdims=True)
    v = jnp.var(x, axis=axis, keepdims=True)
    return (x - m) / jnp.sqrt(v + eps)

def _scatter_add(tgt, idx, src, axis=0):
    return tgt.at[idx].add(src)

def _segment_sum(src, seg, n):
    return jax.ops.segment_sum(src, seg, n)
kernel_name = 'mk_recurrent_d4_jaxref_r8_dfcc53'

def setup_inputs(seed: int=0):
    np.random.seed(seed)
    _w = jnp.asarray

    def _L0_attn_setup():
        import jax, jax.numpy as jnp
        import numpy as np
        from jax import lax
        HID, STATE, K, EXPAND = (128, 16, 4, 2)
        INNER = EXPAND * HID
        B_SZ, L = (4, 512)

        def _selective_scan(x, dt, A, Bm, Cm, D):

            def step(h, inp):
                x_t, dt_t, B_t, C_t = inp
                dA = jnp.exp(dt_t[:, :, None] * A[None, :, :])
                dB = dt_t[:, :, None] * B_t[:, None, :]
                h = dA * h + dB * x_t[:, :, None]
                y = jnp.einsum('bds,bs->bd', h, C_t) + D * x_t
                return (h, y)
            B_, _, d = x.shape
            h0 = jnp.zeros((B_, d, A.shape[1]), x.dtype)
            xs = (jnp.swapaxes(x, 0, 1), jnp.swapaxes(dt, 0, 1), jnp.swapaxes(Bm, 0, 1), jnp.swapaxes(Cm, 0, 1))
            _, ys = lax.scan(step, h0, xs)
            return jnp.swapaxes(ys, 0, 1)
        key = jax.random.key(seed)
        ks = jax.random.split(key, 16)
        s = 0.02
        return {'x': jax.random.normal(ks[0], (B_SZ, L, HID), dtype=jnp.float32), 'in_proj_w': jax.random.normal(ks[1], (2 * INNER, HID), dtype=jnp.float32) * s, 'in_proj_b': jnp.zeros((2 * INNER,), jnp.float32), 'conv_w': jax.random.normal(ks[2], (INNER, 1, K), dtype=jnp.float32) * s, 'conv_b': jnp.zeros((INNER,), jnp.float32), 'dt_w': jax.random.normal(ks[3], (INNER, INNER), dtype=jnp.float32) * s, 'dt_b': jnp.zeros((INNER,), jnp.float32), 'A_log': jnp.log(jnp.abs(jax.random.normal(ks[4], (INNER, STATE), dtype=jnp.float32)) + 1e-06), 'B_w': jax.random.normal(ks[5], (STATE, INNER), dtype=jnp.float32) * s, 'B_b': jnp.zeros((STATE,), jnp.float32), 'C_w': jax.random.normal(ks[6], (STATE, INNER), dtype=jnp.float32) * s, 'C_b': jnp.zeros((STATE,), jnp.float32), 'D': jnp.ones((INNER,), jnp.float32), 'out_w': jax.random.normal(ks[7], (HID, INNER), dtype=jnp.float32) * s, 'out_b': jnp.zeros((HID,), jnp.float32)}
    _L0_attn_in = _L0_attn_setup()

    def _L0_ffn_setup():
        import jax, jax.numpy as jnp
        import numpy as np
        B, T, D = (2, 256, 128)
        E, K, FF = (8, 2, 512)

        def _reference_tuple_inner(x, gate_w, gate_b, w1, b1, w2, b2):
            n_experts = w1.shape[0]
            gate_logits = x @ gate_w + gate_b
            topk_vals, topk_idx = jax.lax.top_k(gate_logits, K)
            topk_w = jax.nn.softmax(topk_vals, axis=-1)
            onehot = jax.nn.one_hot(topk_idx, n_experts, dtype=x.dtype)
            comb = jnp.sum(onehot * topk_w[..., None], axis=2)
            h = jax.nn.gelu(jnp.einsum('btd,edf->ebtf', x, w1) + b1[:, None, None, :], approximate=False)
            y = jnp.einsum('ebtf,efd->ebtd', h, w2) + b2[:, None, None, :]
            output = jnp.einsum('ebtd,bte->btd', y, comb)
            expert_counts = jnp.sum(onehot, axis=(0, 1, 2)).astype(jnp.float32)
            return (output, gate_logits, topk_idx, expert_counts)
        key = jax.random.key(seed)
        ks = jax.random.split(key, 4)
        scale = 0.02
        return {'x': jax.random.normal(ks[0], (B, T, D), jnp.float32), 'gate_w': jax.random.normal(ks[1], (D, E), jnp.float32) * scale, 'gate_b': jnp.zeros((E,), jnp.float32), 'w1': jax.random.normal(ks[2], (E, D, FF), jnp.float32) * scale, 'b1': jnp.zeros((E, FF), jnp.float32), 'w2': jax.random.normal(ks[3], (E, FF, D), jnp.float32) * scale, 'b2': jnp.zeros((E, D), jnp.float32)}
    _L0_ffn_in = _L0_ffn_setup()

    def _L1_attn_setup():
        import jax, jax.numpy as jnp
        import numpy as np
        B, T, D, H = (4, 256, 128, 16)
        HD = D // H
        EPS = 1e-05
        NEG = 10000000000.0
        key = jax.random.key(seed)
        k1, k2, k3 = jax.random.split(key, 3)
        return {'target': jax.random.normal(k1, (B, T, D), dtype=jnp.float32), 'w_qkv': jax.random.normal(k2, (D, 3 * D), dtype=jnp.float32) * 0.02, 'w_proj': jax.random.normal(k3, (D, D), dtype=jnp.float32) * (0.02 / np.sqrt(24.0)), 'b_proj': jnp.zeros((D,), dtype=jnp.float32), 'ln_gamma': jnp.ones((D,), dtype=jnp.float32), 'ln_beta': jnp.zeros((D,), dtype=jnp.float32)}
    _L1_attn_in = _L1_attn_setup()

    def _L1_ffn_setup():
        import jax, jax.numpy as jnp
        import numpy as np
        B, S, D = (2, 256, 128)
        E, H, K = (8, 704, 2)
        N_RESERVED = 4
        key = jax.random.key(seed)
        ks = jax.random.split(key, 5)
        scale = 0.02
        x = jax.random.normal(ks[0], (B, S, D), dtype=jnp.float32)
        gate_w = jax.random.normal(ks[1], (E, D), dtype=jnp.float32) * scale
        w1 = jax.random.normal(ks[2], (E, D, H), dtype=jnp.float32) * scale
        w3 = jax.random.normal(ks[3], (E, D, H), dtype=jnp.float32) * scale
        w2 = jax.random.normal(ks[4], (E, H, D), dtype=jnp.float32) * scale
        return {'x': x, 'gate_w': gate_w, 'w1': w1, 'w2': w2, 'w3': w3}
    _L1_ffn_in = _L1_ffn_setup()

    def _L2_attn_setup():
        import jax, jax.numpy as jnp
        import numpy as np
        N_HEADS = 16
        LN_EPS = 1e-05

        def _rope_tables(T, d_head, dtype):
            i = jnp.arange(1, d_head // 2 + 1, dtype=dtype)
            thetas = jnp.repeat(1000.0 ** (-2.0 * i / d_head), 2)
            pos = jnp.arange(1, T + 1, dtype=dtype)
            args = pos[:, None] * thetas[None, :]
            return (jnp.sin(args), jnp.cos(args))

        def _apply_rope(x, sin, cos):
            x_odd = x[..., ::2]
            x_even = x[..., 1::2]
            x_sin = jnp.stack([-x_even, x_odd], axis=-1).reshape(x.shape)
            return x * cos + x_sin * sin
        key = jax.random.key(seed)
        k1, k2, k3 = jax.random.split(key, 3)
        B, T, C = (2, 256, 128)
        x = jax.random.normal(k1, (B, T, C), dtype=jnp.float32)
        w_in = jax.random.normal(k2, (3 * C, C), dtype=jnp.float32) * 0.02
        w_out = jax.random.normal(k3, (C, C), dtype=jnp.float32) * 0.02
        ln_gamma = jnp.ones((C,), dtype=jnp.float32)
        ln_beta = jnp.zeros((C,), dtype=jnp.float32)
        return {'x': x, 'w_in': w_in, 'w_out': w_out, 'ln_gamma': ln_gamma, 'ln_beta': ln_beta}
    _L2_attn_in = _L2_attn_setup()

    def _L2_ffn_setup():
        import jax, jax.numpy as jnp
        import numpy as np
        NUM_EXPERTS = 8
        TOP_K = 2
        D_MODEL = 128
        EXPERT_CAP = 64
        B, S = (4, 256)
        key = jax.random.key(seed)
        ks = jax.random.split(key, 4)
        scale = 1.0 / np.sqrt(D_MODEL)
        x = jax.random.normal(ks[0], (B, S, D_MODEL), dtype=jnp.float32)
        gate_w = jax.random.normal(ks[1], (D_MODEL, NUM_EXPERTS), dtype=jnp.float32) * scale
        w1 = jax.random.normal(ks[2], (NUM_EXPERTS, D_MODEL, EXPERT_CAP), dtype=jnp.float32) * scale
        b1 = jnp.zeros((NUM_EXPERTS, EXPERT_CAP), dtype=jnp.float32)
        w2 = jax.random.normal(ks[3], (NUM_EXPERTS, EXPERT_CAP, D_MODEL), dtype=jnp.float32) * (1.0 / np.sqrt(EXPERT_CAP))
        b2 = jnp.zeros((NUM_EXPERTS, D_MODEL), dtype=jnp.float32)
        return {'x': x, 'gate_w': gate_w, 'w1': w1, 'b1': b1, 'w2': w2, 'b2': b2}
    _L2_ffn_in = _L2_ffn_setup()

    def _L3_attn_setup():
        import jax, jax.numpy as jnp
        import numpy as np
        D_MODEL = 128
        N_HEADS = 16
        D_HEAD = D_MODEL // N_HEADS
        M_SLOPE = 0.5
        BATCH = 2
        SEQ = 256

        def _alibi_bias(n_heads, seq_len, m, dtype):
            slopes = m ** jnp.arange(n_heads, dtype=dtype)
            pos = jnp.arange(seq_len, dtype=dtype)
            dist = jnp.abs(pos[:, None] - pos[None, :])
            return -dist[None, :, :] * slopes[:, None, None]
        key = jax.random.key(seed)
        k1, k2, k3 = jax.random.split(key, 3)
        x = jax.random.normal(k1, (BATCH, SEQ, D_MODEL), dtype=jnp.float32)
        qkv_w = jax.random.normal(k2, (3 * D_MODEL, D_MODEL), dtype=jnp.float32) * (1.0 / np.sqrt(D_MODEL))
        qkv_b = jnp.zeros((3 * D_MODEL,), dtype=jnp.float32)
        out_w = jax.random.normal(k3, (D_MODEL, D_MODEL), dtype=jnp.float32) * (1.0 / np.sqrt(D_MODEL))
        out_b = jnp.zeros((D_MODEL,), dtype=jnp.float32)
        return {'x': x, 'qkv_w': qkv_w, 'qkv_b': qkv_b, 'out_w': out_w, 'out_b': out_b}
    _L3_attn_in = _L3_attn_setup()

    def _L3_ffn_setup():
        import math
        import jax, jax.numpy as jnp
        import numpy as np
        B, T, D, N, H = (8, 256, 128, 16, 256)
        CAP_FACTOR = 1.25
        key = jax.random.key(seed)
        ks = jax.random.split(key, 4)
        x = jax.random.normal(ks[0], (B, T, D), jnp.float32)
        Wg = jax.random.normal(ks[1], (D, N), jnp.float32) * D ** (-0.5)
        W1 = jax.random.normal(ks[2], (N, D, H), jnp.float32) * D ** (-0.5)
        b1 = jnp.zeros((N, H), jnp.float32)
        W2 = jax.random.normal(ks[3], (N, H, D), jnp.float32) * H ** (-0.5)
        b2 = jnp.zeros((N, D), jnp.float32)
        return {'x': x, 'Wg': Wg, 'W1': W1, 'b1': b1, 'W2': W2, 'b2': b2}
    _L3_ffn_in = _L3_ffn_setup()
    _d = {'L0_attn_x': _L0_attn_in['x'], 'L0_attn_in_proj_w': _L0_attn_in['in_proj_w'], 'L0_attn_in_proj_b': _L0_attn_in['in_proj_b'], 'L0_attn_conv_w': _L0_attn_in['conv_w'], 'L0_attn_conv_b': _L0_attn_in['conv_b'], 'L0_attn_dt_w': _L0_attn_in['dt_w'], 'L0_attn_dt_b': _L0_attn_in['dt_b'], 'L0_attn_A_log': _L0_attn_in['A_log'], 'L0_attn_B_w': _L0_attn_in['B_w'], 'L0_attn_B_b': _L0_attn_in['B_b'], 'L0_attn_C_w': _L0_attn_in['C_w'], 'L0_attn_C_b': _L0_attn_in['C_b'], 'L0_attn_D': _L0_attn_in['D'], 'L0_attn_out_w': _L0_attn_in['out_w'], 'L0_attn_out_b': _L0_attn_in['out_b'], 'L0_ffn_gate_w': _L0_ffn_in['gate_w'], 'L0_ffn_gate_b': _L0_ffn_in['gate_b'], 'L0_ffn_w1': _L0_ffn_in['w1'], 'L0_ffn_b1': _L0_ffn_in['b1'], 'L0_ffn_w2': _L0_ffn_in['w2'], 'L0_ffn_b2': _L0_ffn_in['b2'], 'L1_attn_w_qkv': _L1_attn_in['w_qkv'], 'L1_attn_w_proj': _L1_attn_in['w_proj'], 'L1_attn_b_proj': _L1_attn_in['b_proj'], 'L1_attn_ln_gamma': _L1_attn_in['ln_gamma'], 'L1_attn_ln_beta': _L1_attn_in['ln_beta'], 'L1_ffn_gate_w': _L1_ffn_in['gate_w'], 'L1_ffn_w1': _L1_ffn_in['w1'], 'L1_ffn_w2': _L1_ffn_in['w2'], 'L1_ffn_w3': _L1_ffn_in['w3'], 'L2_attn_w_in': _L2_attn_in['w_in'], 'L2_attn_w_out': _L2_attn_in['w_out'], 'L2_attn_ln_gamma': _L2_attn_in['ln_gamma'], 'L2_attn_ln_beta': _L2_attn_in['ln_beta'], 'L2_ffn_gate_w': _L2_ffn_in['gate_w'], 'L2_ffn_w1': _L2_ffn_in['w1'], 'L2_ffn_b1': _L2_ffn_in['b1'], 'L2_ffn_w2': _L2_ffn_in['w2'], 'L2_ffn_b2': _L2_ffn_in['b2'], 'L3_attn_qkv_w': _L3_attn_in['qkv_w'], 'L3_attn_qkv_b': _L3_attn_in['qkv_b'], 'L3_attn_out_w': _L3_attn_in['out_w'], 'L3_attn_out_b': _L3_attn_in['out_b'], 'L3_ffn_Wg': _L3_ffn_in['Wg'], 'L3_ffn_W1': _L3_ffn_in['W1'], 'L3_ffn_b1': _L3_ffn_in['b1'], 'L3_ffn_W2': _L3_ffn_in['W2'], 'L3_ffn_b2': _L3_ffn_in['b2']}
    _x0 = _d['L0_attn_x']
    _d['L0_attn_x'] = jax.random.normal(jax.random.fold_in(jax.random.key(seed), 1), (4, 512, 128), dtype=_x0.dtype)
    del _x0
    return _d

def reference(L0_attn_x, L0_attn_in_proj_w, L0_attn_in_proj_b, L0_attn_conv_w, L0_attn_conv_b, L0_attn_dt_w, L0_attn_dt_b, L0_attn_A_log, L0_attn_B_w, L0_attn_B_b, L0_attn_C_w, L0_attn_C_b, L0_attn_D, L0_attn_out_w, L0_attn_out_b, L0_ffn_gate_w, L0_ffn_gate_b, L0_ffn_w1, L0_ffn_b1, L0_ffn_w2, L0_ffn_b2, L1_attn_w_qkv, L1_attn_w_proj, L1_attn_b_proj, L1_attn_ln_gamma, L1_attn_ln_beta, L1_ffn_gate_w, L1_ffn_w1, L1_ffn_w2, L1_ffn_w3, L2_attn_w_in, L2_attn_w_out, L2_attn_ln_gamma, L2_attn_ln_beta, L2_ffn_gate_w, L2_ffn_w1, L2_ffn_b1, L2_ffn_w2, L2_ffn_b2, L3_attn_qkv_w, L3_attn_qkv_b, L3_attn_out_w, L3_attn_out_b, L3_ffn_Wg, L3_ffn_W1, L3_ffn_b1, L3_ffn_W2, L3_ffn_b2):

    def _L0_attn_ref(x, in_proj_w, in_proj_b, conv_w, conv_b, dt_w, dt_b, A_log, B_w, B_b, C_w, C_b, D, out_w, out_b):
        import jax, jax.numpy as jnp
        import numpy as np
        from jax import lax
        HID, STATE, K, EXPAND = (128, 16, 4, 2)
        INNER = EXPAND * HID
        B_SZ, L = (4, 512)

        def _selective_scan(x, dt, A, Bm, Cm, D):

            def step(h, inp):
                x_t, dt_t, B_t, C_t = inp
                dA = jnp.exp(dt_t[:, :, None] * A[None, :, :])
                dB = dt_t[:, :, None] * B_t[:, None, :]
                h = dA * h + dB * x_t[:, :, None]
                y = jnp.einsum('bds,bs->bd', h, C_t) + D * x_t
                return (h, y)
            B_, _, d = x.shape
            h0 = jnp.zeros((B_, d, A.shape[1]), x.dtype)
            xs = (jnp.swapaxes(x, 0, 1), jnp.swapaxes(dt, 0, 1), jnp.swapaxes(Bm, 0, 1), jnp.swapaxes(Cm, 0, 1))
            _, ys = lax.scan(step, h0, xs)
            return jnp.swapaxes(ys, 0, 1)
        xz = x @ in_proj_w.T + in_proj_b
        x_part, z = jnp.split(xz, 2, axis=-1)
        xc = lax.conv_general_dilated(jnp.swapaxes(x_part, 1, 2), conv_w, window_strides=(1,), padding=[(K - 1, 0)], dimension_numbers=('NCH', 'OIH', 'NCH'), feature_group_count=INNER) + conv_b[None, :, None]
        x_conv = jax.nn.silu(jnp.swapaxes(xc, 1, 2))
        A = -jnp.exp(A_log)
        dt = jax.nn.softplus(x_conv @ dt_w.T + dt_b)
        Bm = x_conv @ B_w.T + B_b
        Cm = x_conv @ C_w.T + C_b
        y = _selective_scan(x_conv, dt, A, Bm, Cm, D)
        y = y * jax.nn.silu(z)
        return y @ out_w.T + out_b

    def _L0_ffn_ref(x, gate_w, gate_b, w1, b1, w2, b2):
        import jax, jax.numpy as jnp
        import numpy as np
        B, T, D = (2, 256, 128)
        E, K, FF = (8, 2, 512)

        def _reference_tuple_inner(x, gate_w, gate_b, w1, b1, w2, b2):
            n_experts = w1.shape[0]
            gate_logits = x @ gate_w + gate_b
            topk_vals, topk_idx = jax.lax.top_k(gate_logits, K)
            topk_w = jax.nn.softmax(topk_vals, axis=-1)
            onehot = jax.nn.one_hot(topk_idx, n_experts, dtype=x.dtype)
            comb = jnp.sum(onehot * topk_w[..., None], axis=2)
            h = jax.nn.gelu(jnp.einsum('btd,edf->ebtf', x, w1) + b1[:, None, None, :], approximate=False)
            y = jnp.einsum('ebtf,efd->ebtd', h, w2) + b2[:, None, None, :]
            output = jnp.einsum('ebtd,bte->btd', y, comb)
            expert_counts = jnp.sum(onehot, axis=(0, 1, 2)).astype(jnp.float32)
            return (output, gate_logits, topk_idx, expert_counts)
        return _reference_tuple_inner(x, gate_w, gate_b, w1, b1, w2, b2)[0]

    def _L1_attn_ref(target, w_qkv, w_proj, b_proj, ln_gamma, ln_beta):
        import jax, jax.numpy as jnp
        import numpy as np
        B, T, D, H = (4, 256, 128, 16)
        HD = D // H
        EPS = 1e-05
        NEG = 10000000000.0
        b, t, d = target.shape
        resid = target
        qkv = target @ w_qkv
        q, k, v = jnp.split(qkv, 3, axis=-1)
        q = q.reshape(b, t, H, HD).transpose(0, 2, 1, 3)
        k = k.reshape(b, t, H, HD).transpose(0, 2, 1, 3)
        v = v.reshape(b, t, H, HD).transpose(0, 2, 1, 3)
        scores = jnp.einsum('bhqd,bhkd->bhqk', q, k) * (1.0 / np.sqrt(HD))
        causal = (jnp.arange(t)[:, None] >= jnp.arange(t)[None, :]).astype(scores.dtype)
        scores = scores * causal - (1.0 - causal) * NEG
        attn = jax.nn.softmax(scores, axis=-1)
        out = jnp.einsum('bhqk,bhkd->bhqd', attn, v)
        out = out.transpose(0, 2, 1, 3).reshape(b, t, d)
        proj = out @ w_proj + b_proj
        x = proj + resid
        mu = jnp.mean(x, axis=-1, keepdims=True)
        var = jnp.var(x, axis=-1, keepdims=True)
        return (x - mu) * jax.lax.rsqrt(var + EPS) * ln_gamma + ln_beta

    def _L1_ffn_ref(x, gate_w, w1, w2, w3):
        import jax, jax.numpy as jnp
        import numpy as np
        B, S, D = (2, 256, 128)
        E, H, K = (8, 704, 2)
        N_RESERVED = 4
        b, s, d = x.shape
        T = b * s
        xf = x.reshape(T, d)
        logits = xf @ gate_w.T
        expert_ids = jnp.arange(E)
        logits = jnp.where(expert_ids[None, :] >= E - N_RESERVED, -jnp.inf, logits)
        weights = jax.nn.softmax(logits, axis=-1)
        top_w, top_idx = jax.lax.top_k(weights, K)
        top_w = top_w / jnp.sum(top_w, axis=-1, keepdims=True)
        cw = jnp.zeros((T, E), dtype=x.dtype).at[jnp.arange(T)[:, None], top_idx].add(top_w)
        h = jax.nn.silu(jnp.einsum('td,edh->teh', xf, w1)) * jnp.einsum('td,edh->teh', xf, w3)
        y = jnp.einsum('teh,ehd->ted', h, w2)
        out = jnp.einsum('te,ted->td', cw, y)
        return out.reshape(b, s, d)

    def _L2_attn_ref(x, w_in, w_out, ln_gamma, ln_beta):
        import jax, jax.numpy as jnp
        import numpy as np
        N_HEADS = 16
        LN_EPS = 1e-05

        def _rope_tables(T, d_head, dtype):
            i = jnp.arange(1, d_head // 2 + 1, dtype=dtype)
            thetas = jnp.repeat(1000.0 ** (-2.0 * i / d_head), 2)
            pos = jnp.arange(1, T + 1, dtype=dtype)
            args = pos[:, None] * thetas[None, :]
            return (jnp.sin(args), jnp.cos(args))

        def _apply_rope(x, sin, cos):
            x_odd = x[..., ::2]
            x_even = x[..., 1::2]
            x_sin = jnp.stack([-x_even, x_odd], axis=-1).reshape(x.shape)
            return x * cos + x_sin * sin
        B, T, C = x.shape
        H = N_HEADS
        d_head = C // H
        scale = 1.0 / jnp.sqrt(jnp.asarray(d_head, dtype=x.dtype))
        qkv = jnp.einsum('btc,oc->bto', x, w_in)
        q, k, v = jnp.split(qkv, 3, axis=-1)
        q = q.reshape(B, T, H, d_head).transpose(0, 2, 1, 3)
        k = k.reshape(B, T, H, d_head).transpose(0, 2, 1, 3)
        v = v.reshape(B, T, H, d_head).transpose(0, 2, 1, 3)
        sin, cos = _rope_tables(T, d_head, x.dtype)
        q_rope = _apply_rope(q, sin, cos)
        k_rope = _apply_rope(k, sin, cos)
        att_num = jnp.exp(jnp.einsum('bhqd,bhkd->bhqk', q_rope, k_rope) * scale)
        att_den = jnp.sum(jnp.exp(jnp.einsum('bhqd,bhkd->bhqk', q, k) * scale), axis=-1, keepdims=True)
        att = att_num / att_den
        y = jnp.einsum('bhqk,bhkd->bhqd', att, v)
        y = y.transpose(0, 2, 1, 3).reshape(B, T, C)
        y = jnp.einsum('btc,oc->bto', y, w_out)
        h = y + x
        mu = jnp.mean(h, axis=-1, keepdims=True)
        var = jnp.var(h, axis=-1, keepdims=True)
        return (h - mu) / jnp.sqrt(var + LN_EPS) * ln_gamma + ln_beta

    def _L2_ffn_ref(x, gate_w, w1, b1, w2, b2):
        import jax, jax.numpy as jnp
        import numpy as np
        NUM_EXPERTS = 8
        TOP_K = 2
        D_MODEL = 128
        EXPERT_CAP = 64
        B, S = (4, 256)
        Bx, Sx, D = x.shape
        xt = x.reshape(-1, D)
        gates = jax.nn.softmax(xt @ gate_w, axis=-1)
        topk_g, topk_i = jax.lax.top_k(gates, TOP_K)
        tok_w = topk_g.sum(axis=-1)
        sel = (topk_i[:, :, None] == jnp.arange(NUM_EXPERTS)[None, None, :]).any(axis=1)
        h = jax.nn.gelu(jnp.einsum('nd,edh->enh', xt, w1) + b1[:, None, :], approximate=False)
        y = jnp.einsum('enh,ehd->end', h, w2) + b2[:, None, :]
        out = jnp.einsum('end,ne,n->nd', y, sel.astype(x.dtype), tok_w)
        return out.reshape(Bx, Sx, D)

    def _L3_attn_ref(x, qkv_w, qkv_b, out_w, out_b):
        import jax, jax.numpy as jnp
        import numpy as np
        D_MODEL = 128
        N_HEADS = 16
        D_HEAD = D_MODEL // N_HEADS
        M_SLOPE = 0.5
        BATCH = 2
        SEQ = 256

        def _alibi_bias(n_heads, seq_len, m, dtype):
            slopes = m ** jnp.arange(n_heads, dtype=dtype)
            pos = jnp.arange(seq_len, dtype=dtype)
            dist = jnp.abs(pos[:, None] - pos[None, :])
            return -dist[None, :, :] * slopes[:, None, None]
        batch, seq_len, d_model = x.shape
        qkv = x @ qkv_w.T + qkv_b
        qkv = qkv.reshape(batch, seq_len, N_HEADS, 3 * D_HEAD).transpose(0, 2, 1, 3)
        q, k, v = jnp.split(qkv, 3, axis=-1)
        scale = jnp.sqrt(jnp.asarray(D_HEAD, dtype=x.dtype))
        scores = jnp.einsum('bhid,bhjd->bhij', q, k) / scale
        scores = scores + _alibi_bias(N_HEADS, seq_len, M_SLOPE, x.dtype)[None]
        attn = jax.nn.softmax(scores, axis=-1)
        out = jnp.einsum('bhij,bhjd->bhid', attn, v)
        out = out.transpose(0, 2, 1, 3).reshape(batch, seq_len, d_model)
        return out @ out_w.T + out_b

    def _L3_ffn_ref(x, Wg, W1, b1, W2, b2):
        import math
        import jax, jax.numpy as jnp
        import numpy as np
        B, T, D, N, H = (8, 256, 128, 16, 256)
        CAP_FACTOR = 1.25
        b, t, d = x.shape
        n = Wg.shape[1]
        bt = b * t
        cap = math.ceil(CAP_FACTOR * bt / n)
        logits = jnp.einsum('btd,dn->btn', x, Wg)
        probs = jax.nn.softmax(logits, axis=-1)
        top1_val = probs.max(axis=-1).reshape(bt)
        top1_idx = probs.argmax(axis=-1).reshape(bt)
        x_flat = x.reshape(bt, d)
        masked = jnp.where(top1_idx[None, :] == jnp.arange(n)[:, None], top1_val[None, :], -jnp.inf)
        vals, idx = jax.lax.top_k(masked, cap)
        valid = jnp.isfinite(vals)
        xe = x_flat[idx]
        h = jax.nn.gelu(jnp.einsum('ncd,ndh->nch', xe, W1) + b1[:, None, :])
        out = jnp.einsum('nch,nhd->ncd', h, W2) + b2[:, None, :]
        safe_idx = jnp.where(valid, idx, bt)
        y_flat = x_flat.at[safe_idx.reshape(-1)].set(out.reshape(-1, d), mode='drop')
        return y_flat.reshape(b, t, d)
    x = L0_attn_x
    xn = _layernorm(x, axis=-1)
    s = _L0_attn_ref(xn, L0_attn_in_proj_w, L0_attn_in_proj_b, L0_attn_conv_w, L0_attn_conv_b, L0_attn_dt_w, L0_attn_dt_b, L0_attn_A_log, L0_attn_B_w, L0_attn_B_b, L0_attn_C_w, L0_attn_C_b, L0_attn_D, L0_attn_out_w, L0_attn_out_b)
    g = _silu(_L0_ffn_ref(xn, L0_ffn_gate_w, L0_ffn_gate_b, L0_ffn_w1, L0_ffn_b1, L0_ffn_w2, L0_ffn_b2))
    x = x + s * g
    xn = _layernorm(x, axis=-1)
    s = _L1_attn_ref(xn, L1_attn_w_qkv, L1_attn_w_proj, L1_attn_b_proj, L1_attn_ln_gamma, L1_attn_ln_beta)
    g = _silu(_L1_ffn_ref(xn, L1_ffn_gate_w, L1_ffn_w1, L1_ffn_w2, L1_ffn_w3))
    x = x + s * g
    xn = _layernorm(x, axis=-1)
    s = _L2_attn_ref(xn, L2_attn_w_in, L2_attn_w_out, L2_attn_ln_gamma, L2_attn_ln_beta)
    g = _silu(_L2_ffn_ref(xn, L2_ffn_gate_w, L2_ffn_w1, L2_ffn_b1, L2_ffn_w2, L2_ffn_b2))
    x = x + s * g
    xn = _layernorm(x, axis=-1)
    s = _L3_attn_ref(xn, L3_attn_qkv_w, L3_attn_qkv_b, L3_attn_out_w, L3_attn_out_b)
    g = _silu(_L3_ffn_ref(xn, L3_ffn_Wg, L3_ffn_W1, L3_ffn_b1, L3_ffn_W2, L3_ffn_b2))
    x = x + s * g
    return x

_drawn_inputs = setup_inputs


def setup_inputs(seed=0):
    import zlib

    import numpy as np

    out = dict(_drawn_inputs(seed))
    spreads = {'L0_attn_in_proj_b': (0.0, 0.1),
     'L0_attn_conv_b': (0.0, 0.1),
     'L0_attn_dt_b': (0.0, 0.1),
     'L0_attn_B_b': (0.0, 0.1),
     'L0_attn_C_b': (0.0, 0.1),
     'L0_attn_D': (1.0, 0.2),
     'L0_attn_out_b': (0.0, 0.1),
     'L0_ffn_gate_b': (0.0, 0.1),
     'L0_ffn_b1': (0.0, 0.1),
     'L0_ffn_b2': (0.0, 0.1),
     'L1_attn_b_proj': (0.0, 0.1),
     'L1_attn_ln_gamma': (1.0, 0.2),
     'L1_attn_ln_beta': (0.0, 0.1),
     'L2_attn_ln_gamma': (1.0, 0.2),
     'L2_attn_ln_beta': (0.0, 0.1),
     'L2_ffn_b1': (0.0, 0.1),
     'L2_ffn_b2': (0.0, 0.1),
     'L3_attn_qkv_b': (0.0, 0.1),
     'L3_attn_out_b': (0.0, 0.1),
     'L3_ffn_b1': (0.0, 0.1),
     'L3_ffn_b2': (0.0, 0.1)}
    factors = {}
    for name, (base, spread) in spreads.items():
        noise = np.random.default_rng([zlib.crc32(name.encode()), seed]).standard_normal(out[name].shape)
        drawn = base * np.exp(spread * noise) if base else spread * noise
        out[name] = jnp.asarray(drawn.astype(out[name].dtype))
    for name, factor in factors.items():
        out[name] = (out[name] * factor).astype(out[name].dtype)
    return out
```

```python
from contextlib import ExitStack

import numpy as np

import concourse.bass as bass
from concourse import mybir

F32 = mybir.dt.float32
BF16 = mybir.dt.bfloat16
I32 = mybir.dt.int32
U32 = mybir.dt.uint32
ALU = mybir.AluOpType
ACT = mybir.ActivationFunctionType
AX = mybir.AxisListType

P = 128
NB = 4
T = 512
TB = T // P
NT = NB * TB
D = 128
INNER = 256
NST = 16
KC = 4
NH = 16
DH = D // NH
QUADS = NH // 4
EPS = 1e-5
E0, FF0 = 8, 512
E1, FF1 = 4, 704
E2, FF2 = 8, 64
E3, FF3 = 16, 256
CAP = 160
SLOTS = E3 * CAP
ST = SLOTS // P
NEG = -1e30
VW = DH + 1
SLOPE_AT = 2 * ST * P + NT * P

QPARTS = (0, 0, 1, 1, 0, 2)
KPARTS = (0, 1, 0, 1, 2, 0)
NG = len(QPARTS)
KROWS = NG * DH
AROW = KROWS
MROW = KROWS + 4
KALL = MROW + 2


def blob(pieces):
    at, cols, out = {}, 0, []
    for name, a in pieces:
        a = np.asarray(a)
        a = a.reshape(a.shape[0], -1)
        if a.shape[0] < P:
            a = np.concatenate([a, np.zeros((P - a.shape[0], a.shape[1]), a.dtype)])
        at[name] = (cols, a.shape[1])
        cols += a.shape[1]
        out.append(a)
    return at, np.ascontiguousarray(np.concatenate(out, axis=1))


def rows(v):
    return np.repeat(np.asarray(v).reshape(1, -1), P, axis=0)


def padded_heads(w):
    n = w.shape[1]
    out = np.zeros((QUADS, 4, 32, n), w.dtype)
    out[:, :, :DH] = w.reshape(QUADS, 4, DH, n)
    return out.transpose(1, 2, 0, 3).reshape(P, QUADS * n)


def chunks1():
    full = FF1 // P
    out = []
    for e in range(0, E1, 2):
        out += [[(e, c * P, 0, P)] for c in range(full)]
        out += [[(e, full * P, 0, FF1 - full * P), (e + 1, full * P, FF1 - full * P, FF1 - full * P)]]
        out += [[(e + 1, c * P, 0, P)] for c in range(full)]
    return out


CH1 = chunks1()


def up1(w):
    return np.concatenate([np.concatenate([w[e][:, o:o + n] for e, o, _, n in ch], axis=1) for ch in CH1], axis=1)


def down1(w):
    return np.concatenate([np.concatenate([w[e][o:o + n] for e, o, _, n in ch], axis=0) for ch in CH1], axis=1)


def layouts(a):
    t = np.transpose
    d = {}
    d["l0"] = blob([
        ("in_w", t(a["L0_attn_in_proj_w"])), ("in_b", t(a["L0_attn_in_proj_b"].reshape(4, P))),
        ("conv_w", t(a["L0_attn_conv_w"].reshape(2, P, KC), (1, 0, 2))),
        ("conv_b", t(a["L0_attn_conv_b"].reshape(2, P))),
        ("dt_w", t(t(a["L0_attn_dt_w"]).reshape(2, P, INNER), (1, 0, 2))),
        ("dt_b", t(a["L0_attn_dt_b"].reshape(2, P))),
        ("a_log", t(a["L0_attn_A_log"].reshape(2, P, NST), (1, 0, 2))),
        ("bc_w", t(np.concatenate([t(a["L0_attn_B_w"]), t(a["L0_attn_C_w"])], axis=1).reshape(2, P, 2 * NST), (1, 0, 2))),
        ("bc_b", np.concatenate([a["L0_attn_B_b"], a["L0_attn_C_b"]]).reshape(-1, 1)),
        ("d", t(a["L0_attn_D"].reshape(2, P))),
        ("out_w", t(t(a["L0_attn_out_w"]).reshape(2, P, D), (1, 0, 2))), ("out_b", rows(a["L0_attn_out_b"])),
        ("gate_w", a["L0_ffn_gate_w"]), ("gate_b", rows(a["L0_ffn_gate_b"])),
        ("b1", t(a["L0_ffn_b1"].reshape(E0 * 4, P))), ("b2", a["L0_ffn_b2"]),
        ("w1", t(a["L0_ffn_w1"], (1, 0, 2))),
        ("w2", t(a["L0_ffn_w2"].reshape(E0 * 4, P, D), (1, 0, 2))),
    ])
    q = a["L1_attn_w_qkv"]
    d["l1"] = blob([
        ("wq", q[:, :D]), ("wk", q[:, D:2 * D]), ("wv", q[:, 2 * D:]),
        ("wp", padded_heads(a["L1_attn_w_proj"])), ("bp", rows(a["L1_attn_b_proj"])),
        ("gamma", rows(a["L1_attn_ln_gamma"])), ("beta", rows(a["L1_attn_ln_beta"])),
        ("gate_w", t(a["L1_ffn_gate_w"])[:, :E1]),
        ("w1", up1(a["L1_ffn_w1"])), ("w3", up1(a["L1_ffn_w3"])), ("w2", down1(a["L1_ffn_w2"])),
    ])
    wi = t(a["L2_attn_w_in"])
    swap = np.arange(D) ^ 1
    d["l2"] = blob([
        ("wq", wi[:, :D]), ("wqs", wi[:, :D][:, swap]), ("wk", wi[:, D:2 * D]), ("wks", wi[:, D:2 * D][:, swap]),
        ("wv", wi[:, 2 * D:]), ("wp", padded_heads(t(a["L2_attn_w_out"]))),
        ("gamma", rows(a["L2_attn_ln_gamma"])), ("beta", rows(a["L2_attn_ln_beta"])),
        ("gate_w", a["L2_ffn_gate_w"]), ("b1", t(a["L2_ffn_b1"].reshape(4, P))), ("b2", a["L2_ffn_b2"]),
        ("w1", t(a["L2_ffn_w1"], (1, 0, 2))),
        ("w2", t(a["L2_ffn_w2"].reshape(4, P, D), (1, 0, 2))),
    ])
    qw = t(a["L3_attn_qkv_w"]).reshape(D, NH, 3, DH)
    qb = a["L3_attn_qkv_b"].reshape(NH, 3, DH)
    d["l3"] = blob([
        ("wq", qw[:, :, 0].reshape(D, D)), ("wk", qw[:, :, 1].reshape(D, D)), ("wv", qw[:, :, 2].reshape(D, D)),
        ("bq", qb[:, 0].reshape(D, 1)), ("bk", qb[:, 1].reshape(D, 1)), ("bv", rows(qb[:, 2])),
        ("wp", padded_heads(t(a["L3_attn_out_w"]))), ("bp", rows(a["L3_attn_out_b"])),
        ("gate_w", a["L3_ffn_Wg"]), ("b1", t(a["L3_ffn_b1"].reshape(E3 * 2, P))), ("b2", t(a["L3_ffn_b2"])),
        ("w1", t(a["L3_ffn_W1"], (1, 0, 2))),
        ("w2", t(a["L3_ffn_W2"].reshape(E3 * 2, P, D), (1, 0, 2))),
    ])
    return d


def constants():
    f, bf = np.float32, mybir.dt.np(BF16)
    i = np.arange(P)
    eye = np.eye(P, dtype=f)
    seld = np.zeros((P, P), f)
    for g in range(4):
        seld[32 * g + DH, 32 * g:32 * g + 32] = 1
    k = np.arange(1, DH // 2 + 1, dtype=f)
    thetas = np.repeat(np.power(f(1000.0), (f(-2.0) * k / f(DH))).astype(f), 2)
    args = (np.arange(1, T + 1, dtype=f)[:, None] * thetas[None, :]).astype(f)
    sign = np.where(np.arange(DH) % 2 == 0, f(-1), f(1))
    cos = np.tile(np.cos(args).astype(f).T, (NH, 1))
    sin = np.tile((np.sin(args).astype(f) * sign).T, (NH, 1))
    c32 = blob([
        ("eye", eye), ("seld", seld),         ("iota", rows(np.arange(16, dtype=f))),
        ("drop", (SLOTS + i[:, None] + P * np.arange(NT)[None, :]).astype(f)),
        ("lower", (i[None, :] < i[:, None]).astype(f)),
    ])
    after = (i[None, :] > i[:, None]).astype(f)
    back = -2.0 * np.maximum(i[None, :] - i[:, None], 0)
    slope = 0.5 ** np.arange(NH)
    sel = np.zeros((P, 2 * NST, P), f)
    for s in range(2 * NST):
        sel[[s, 2 * NST + s, 4 * NST + s], s] = 1
    c16 = blob([
        ("eye", eye), ("mask_a", NEG * after), ("mask_b", NEG * after.T),
        ("back_a", back), ("back_b", back.T),
    ])
    slopes = (slope[None, :, None] * eye[:, None, :]).reshape(P, -1).astype(bf)
    c16 = (c16[0], c16[1].astype(bf))
    sel = sel.reshape(P, -1).astype(bf)
    pos = np.arange(T)
    ph, pl = (pos // 16) * 16, pos % 16
    r = np.zeros((5, 2, 6, NH // 2, T), f)
    for h in range(NH):
        par, s = h % 2, h // 2
        m = slope[h]
        r[0, par, :, s] = 0
        r[1, par, 4:, s] = 1
        r[2, par, 0:2, s] = 1
        r[2, par, 2, s], r[2, par, 3, s] = -m * ph, -m * pl
        r[3, par, 0, s], r[3, par, 1, s], r[3, par, 2:, s] = m * ph, m * pl, 1
        r[4, par, 0, s], r[4, par, 1, s], r[4, par, 2:4, s] = -m * ph, -m * pl, -1
        r[4, par, 4:, s] = 1
    rope = blob([("cos", cos), ("sin", sin)])
    return {"rope": rope, "c32": c32, "c16": c16, "slope": (None, slopes), "sel": (None, sel), "rows": (None, r.astype(bf))}


def by_parity(hs):
    return [h for h in hs if h % 2 == 0] + [h for h in hs if h % 2]


def score_units(kind):
    units_a, units_b, stages = [], [], []
    for g in range(QUADS):
        hs = range(4 * g, 4 * g + 4)
        if kind == "causal":
            for h in hs:
                units_a.append([(h, 3, 0, 512), (h, 2, 512, 384), (h, 0, 896, 128)])
                units_b.append((0, [(h, 0, 0, 512), (h, 1, 512, 384), (h, 3, 896, 128)]))
            stages.append((g, "x", len(units_b)))
            units_a.append([(h, 1, 256 * n, 256) for n, h in enumerate(by_parity(hs))])
            units_b.append((0, [(h, 2, 256 * n, 256) for n, h in enumerate(by_parity(hs))]))
            stages.append((g, "y", len(units_b)))
        else:
            for plain in ((0, 1) if kind == "rope" else (0,)):
                for cp in range(2):
                    for h in hs:
                        unit = [(h, 2 * cp, 0, 512), (h, 2 * cp + 1, 512, 512)]
                        if not plain:
                            units_a.append(unit)
                        units_b.append((plain, unit))
                    stages.append((g, (plain, cp), len(units_b)))
    return units_a, units_b, stages


def b_items(kind, lag=2):
    _, units, stages = score_units(kind)
    after = {}
    for s, (g, _, end) in enumerate(stages):
        after.setdefault(end + lag, []).append(("pv", s))
        if s + 1 == len(stages) or stages[s + 1][0] != g:
            after.setdefault(end + lag + 2, []).append(("bc", g))
    out = []
    for u in range(len(units) + 5):
        out += after.get(u, [])
        if u < len(units):
            out.append(("b", u))
    return out


def spread(main, extra):
    out, done = [], 0
    for n, item in enumerate(main):
        out.append(item)
        want = (n + 1) * len(extra) // len(main)
        out += extra[done:want]
        done = want
    return out


class Links:

    def __init__(self, eng, sem):
        self.eng, self.sem, self.done, self.n, self.base = eng, sem, 0, 0, 0

    def enter(self, b, key):
        self.base, self.n = self.done + b * LINKS[key], 0

    def close(self, key):
        if self.n != LINKS[key]:
            WRONG_LINKS[key] = self.n
        self.done += self.n * NB
        self.base, self.n = self.done, 0

    def straight(self):
        self.done += self.n
        self.base, self.n = self.done, 0

    def add(self, ins):
        ins.then_inc(self.sem, 1)
        self.n += 1
        return ins

    def wait(self, n=None):
        self.eng.wait_ge(self.sem, self.base + (self.n if n is None else n))

    def link(self, ins):
        self.add(ins)
        self.wait()


KIND = {1: "causal", 2: "rope", 3: "alibi"}
NF = {0: E0 * 4, 1: len(CH1), 2: E2 * FF2 // P}
OPERANDS = {1: ("q", "k"), 2: ("q", "k", "qr", "kr"), 3: ("q", "k")}
LINKS = {"pre": 8, 0: 76, 1: 67, 2: 56, 3: 8, "act0": 5, "pool1": 1, "pool2": 2}
WRONG_LINKS = {}


def down_groups(l):
    if l == 0:
        return [[(f // 4, 0, P, f, f % 4 == 0, f % 4 == 3)] for f in range(NF[0])]
    if l == 2:
        return [[(2 * f, 0, FF2, f, True, True), (2 * f + 1, FF2, FF2, f, True, True)] for f in range(NF[2])]
    full, out = FF1 // P, []
    half = FF1 - full * P
    for pair in range(E1 // 2):
        at = pair * (2 * full + 1)
        out += [[(2 * pair, 0, P, at + c, c == 0, False)] for c in range(full)]
        out += [[(2 * pair, 0, half, at + full, False, True)]]
        out += [[(2 * pair + 1, 0, P, at + full + 1 + c, c == 0, False)] for c in range(full - 1)]
        out += [[(2 * pair + 1, 0, P, at + 2 * full, False, False),
                 (2 * pair + 1, half, half, at + full, False, True)]]
    return out


def schedule(l):
    f = [("f", n) for n in range(NF.get(l, 0))]
    if l == 0:
        out = []
        for s in range(NST):
            out.append(("s", s))
            if s % 2:
                out += f[2 * (s - 1):2 * (s - 1) + 4]
        return out + [("fl", 0)]
    a = [("a", u) for u in range(len(score_units(KIND[l])[0]))]
    b = b_items(KIND[l])
    if l == 1:
        return f[:3] + spread(a, f[3:12]) + [("mx", 0)] + f[12:15] + spread(b, f[15:]) + [("fl", 0)]
    if l == 2:
        return f + [("fl", 0)] + b
    return a + [("mx", 0)] + b


def program(nc, x_in, blobs, at, out, layers=(0, 1, 2, 3)):
    ctx = ExitStack()
    with ctx:
        def sb(name, shape, dt=F32):
            return ctx.enter_context(nc.sbuf_tensor(name, shape, dt))

        def sem(name):
            return ctx.enter_context(nc.semaphore(name))

        wide = {n: blobs[n].shape[1] for n in blobs if n != "rows"}
        wa = sb("weights_even", [P, max(wide["l0"], wide["l2"] + 2 * T, SLOPE_AT + NH * P // 2)])
        wb = sb("weights_odd", [P, max(wide["l1"], wide["l3"])])
        c32 = sb("consts", [P, wide["c32"]])
        c16 = sb("consts16", [P, wide["c16"]], BF16)
        x = sb("x", [P, NT, D])
        xn = sb("xn", [P, NT, D])
        xnt = sb("xnt", [P, NT * P])
        xb = sb("xnt_sequence", [P, T])
        scratch = sb("scratch", [P, 17408])
        facc = sb("mixture_sum", [P, TB, D])
        sa = sb("branch", [P, TB, D])
        xs = sa
        hid = sb("hidden", [P, 2, T])
        hidh = sb("hidden_shared", [P, T])
        act_t = sb("tanh", [P, T])
        act_g = sb("gated", [P, T])
        stat = sb("stat", [P, TB, 6])
        mv = sb("mean_var", [P, TB, 2])
        rstd = sb("rstd", [P, TB])
        vare = sb("variance_eps", [P, TB])
        half = sb("minus_half", [P, TB])
        lg = sb("logits", [P, TB, 16])
        m8 = sb("top_values", [P, TB, 8])
        i8 = sb("top_index", [P, TB, 8], U32)
        fi = sb("top_index_f", [P, TB, 8])
        gd = sb("gate_small", [P, 6, TB])
        cw = sb("combine", [P, TB, 16])
        cw2 = sb("combine_second", [P, TB, 16])
        cwt = sb("combine_t", [16, T])
        small = sb("small_l0", [P, 64])
        junk = sb("junk", [P, 8])
        ps = ctx.enter_context(nc.psum_tensor("ps", [P, 8, 512], F32))
        PV, UP, YB, MI = 4, 5, 6, 7

        def W(l, name, shape=None):
            base = {0: wa, 2: wa, 1: wb, 3: wb, "c32": c32, "c16": c16}[l]
            a, n = at[{0: "l0", 1: "l1", 2: "l2", 3: "l3"}.get(l, l)][name]
            return base[:, a:a + n]

        eye, seld, iota = W("c32", "eye"), W("c32", "seld"), W("c32", "iota")
        eyeb = W("c16", "eye")
        rope = [wa[:, wide["l2"] + T * n:wide["l2"] + T * (n + 1)] for n in range(2)]
        slope = wa[:, SLOPE_AT:SLOPE_AT + NH * P // 2].bitcast(BF16)

        stack = [scratch[:, 2048 * n:2048 * (n + 1)].bitcast(BF16).rearrange("p (s t) -> p s t", t=T)
                 for n in range(4)]
        pt = [scratch[:, 8192 + 4096 * n:8192 + 4096 * (n + 1)].rearrange("p (i c) -> p i c", i=4) for n in range(2)]
        pty = scratch[:, 16384:17408].rearrange("p (i c) -> p i c", i=4)
        vf = [scratch[:, 8192 + 512 * n:8192 + 512 * (n + 1)] for n in range(4)]
        part = [scratch[:, 10240 + 768 * n:10240 + 768 * (n + 1)].bitcast(BF16).rearrange("p (k t) -> p k t", t=T)
                for n in range(4)]
        nm = scratch[0:16, 13312:13824].bitcast(BF16).rearrange("p (k t) -> p k t", t=T)
        vx = sb("values", [P, TB, NH * VW + 32])
        onesv = sb("ones_column", [P, 32])
        ot = sb("head_out", [P, T])
        rc = sb("reciprocals", [P, T])
        on = sb("heads_out", [P, QUADS, T])
        mx = sb("neg_max", [P, TB, NH])
        o = 0

        def take(n):
            nonlocal o
            o += n
            return scratch[:, o - n:o]

        l0 = {"xp": take(2 * (T + KC - 1)).rearrange("p (g t) -> p g t", g=2)}
        for n in ("xc", "xconv", "dt", "dtx", "zs", "y", "da0", "da1", "ub", "hs", "hc", "tmp"):
            l0[n] = take(2 * T).rearrange("p (g t) -> p g t", g=2)
        l0["bcf"] = take(T)
        l0["bcm"] = take(T // 2).bitcast(BF16)
        l0["bcs"] = take(T // 2).bitcast(BF16)
        l0["sel"] = take(2 * NST * P // 2).bitcast(BF16).rearrange("p (s m) -> p s m", m=P)
        assert o <= 17408, o

        parts_d = nc.dram_tensor("parts_scratch", [4, NH, NG, DH, T], BF16, kind="Internal").ap()
        max_d = nc.dram_tensor("max_scratch", [2, 2, NH // 2, T], BF16, kind="Internal").ap()
        slots_d = nc.dram_tensor("slots_scratch", [SLOTS + NT * P, D], F32, kind="Internal").ap()

        xe = wa[:, 0:SLOTS].rearrange("p (n d) -> p n d", d=P)
        xet = wa[:, SLOTS:2 * SLOTS]
        gs = wa[:, 2 * SLOTS:2 * SLOTS + NT * P].rearrange("p (n d) -> p n d", d=P)
        PART = 32
        ro = 0

        def route(*shape, rows_=P, dt=F32):
            nonlocal ro
            n = int(np.prod(shape)) * (2 if dt == BF16 else 4) // 4
            v = scratch[0:rows_, ro:ro + n]
            ro += n
            v = v if dt == F32 else v.bitcast(dt)
            return v if len(shape) == 1 else v.rearrange("p (a b) -> p a b", b=shape[1])

        r_parts = route(NT, 3 * PART)
        r_hot = route(NT, 3 * PART)
        r_partst = route(NT * P, rows_=3 * PART, dt=BF16)
        r_hott = route(NT * P, rows_=3 * PART, dt=BF16)
        r_lg, r_w, r_hot1 = route(NT, E3), route(NT, E3), route(NT, E3)
        r_b16 = route(2, NT * E3, dt=BF16)
        r_m8, r_fi = route(NT, 8), route(NT, 8)
        r_i8 = route(NT, 8, dt=U32)
        r_junk = route((NT + 1) * P, dt=BF16)
        r_v = route(9, NT)
        r_idx = route(NT, dt=I32)

        x_in_v = x_in.rearrange("b (n p) d -> p (b n) d", p=P)
        out_v = out.rearrange("b (n p) d -> p (b n) d", p=P)

        s_x, s_c32, s_c16 = sem("x_in"), sem("consts_in"), sem("consts16_in")
        s_w = [sem(f"weights_in{l}") for l in range(4)]
        s_sel = sem("selectors_in")
        s_out = sem("out_written")
        eps_ready = sem("pool_constants_ready")
        dl = sem("vector_own")
        pl = sem("pool_own")
        alone = [sem("waits_alone_vector"), sem("waits_alone_pool"), sem("waits_alone_sync")]

        def wait_done(eng, n):
            eng.sem_inc(alone[n], 1)

        dn_set = sem("vector_constants_ready")
        first = layers[0]
        var_ready = {n: sem(f"variance_ready_{n}") for n in ("pre",) + tuple(layers)}
        rstd_ready = {n: sem(f"rstd_ready_{n}") for n in ("pre",) + tuple(layers)}
        xn_ready = {n: sem(f"xn_ready_{n}") for n in ("pre",) + tuple(layers)}
        xn_turned = {n: sem(f"xn_turned_{n}") for n in ("pre",) + tuple(layers)}
        xnt_ready = {n: sem(f"xnt_ready_{n}") for n in ("pre",) + tuple(layers)}
        before = {l: ("pre" if l == first else l - 1) for l in layers}
        units = {l: score_units(KIND[l]) for l in layers if l}
        NUA = {l: len(units[l][0]) for l in units}
        NUB = {l: len(units[l][1]) for l in units}
        NS = {l: len(units[l][2]) for l in units}
        DG = {l: down_groups(l) for l in (0, 1, 2)}
        NE = {0: E0, 1: E1, 2: E2}
        KA = {1: KROWS, 3: MROW}
        NY = {l: sum(len(g) for g in DG[l]) for l in DG}
        NPROJ = {0: 5, 1: 4, 2: 6, 3: 3}
        NSTK = {1: 2, 2: 4, 3: 3}
        NROWS = {1: 4, 3: 7}
        EV = {1: 2, 2: 4, 3: 2}
        mixed, with_bias, with_heads, with_max = (0, 1, 2), (0, 2), (1, 2, 3), (1, 3)
        per_turn = {}
        for names, counts in (
                ("xb_ready tail_done attn_ready", {l: 1 for l in range(4)}),
                ("gate_diff gate_exp gate_seen cw_ready fgate_ready", {l: 1 for l in mixed}),
                ("cwt_turned cwt_ready bias_ready bias_seen", {l: 1 for l in with_bias}),
                ("proj_ready", NPROJ), ("evac_done", EV), ("up_ready hidden_ready", NF), ("y_ready", NY),
                ("y_free", NE), ("values_ready", {l: 1 for l in with_heads}),
                ("parts_ready", {l: len(OPERANDS[l]) for l in with_heads}),
                ("parts_out", {l: 16 * NG * len(OPERANDS[l]) for l in with_heads}),
                ("stacks_ready", {l: 16 * 2 * NSTK[l] for l in with_heads}),
                ("a_ready a_free", {l: NUA.get(l, 0) for l in with_max}),
                ("max_turned max_parts", {l: 1 for l in with_max}),
                ("max_out", {l: 16 for l in with_max}), ("max_in", {l: 32 for l in with_max}),
                ("b_ready exp_done", NUB), ("pv_done", NS),
                ("head_copied den_ready pv_free on_ready", {l: QUADS for l in with_heads})):
            for name in names.split():
                per_turn[name] = counts

        class Signals(dict):

            def __missing__(self, key):
                l, name = key
                if name in per_turn:
                    if name not in self:
                        self[name] = sem(name)
                    return self[name]
                self[key] = sem("l%d_%s" % key)
                return self[key]

        q = Signals()
        start = {(l, name): NB * sum(counts.get(m, 0) for m in layers[:i])
              for i, l in enumerate(layers) for name, counts in per_turn.items()}
        block = ctx.enter_context(nc.Block())

        def upto(l, f):
            return sum(len(g) for g in DG[l][:f + 1])

        def span(b, n=T):
            return bass.ds(b * n, n)

        def head(h):
            return 64 * (h % 2), h // 2

        @block.tensor
        def _(pe):
            def turn_xn(l, b):
                pe.wait_ge(xnt_ready[l], b + 1)
                pe.wait_ge(xn_ready[l], b + 1)
                for j in range(TB):
                    mm = pe.transpose(ps[:, MI, P * j:P * (j + 1)], xs[:, j, :], eye)
                mm.then_inc(xn_turned[l], 1)

            def gate(l, bank, b, ready):
                n = {0: E0, 1: E1, 2: E2}[l]
                for j in range(TB):
                    mm = pe.matmul(ps[:, bank, 16 * j:16 * j + n], xb[:, P * j:P * (j + 1)], W(l, "gate_w"),
                                   start=(j == 0), stop=True, skip_group_check=True)
                mm.then_inc(ready, 1)

            def mixture_bias(l, b):
                n = NE[l]
                pe.wait_ge(q[l, "cw_ready"], start[l, "cw_ready"] + b + 1)
                for j in range(TB):
                    mm = pe.transpose(ps[0:n, MI, P * j:P * (j + 1)], cw[:, j, 0:n], eye)
                mm.then_inc(q[l, "cwt_turned"], 1)
                pe.wait_ge(q[l, "cwt_ready"], start[l, "cwt_ready"] + b + 1)
                for j in range(TB):
                    mm = pe.matmul(ps[:, MI, P * j:P * (j + 1)], cwt[0:n, P * j:P * (j + 1)], W(l, "b2")[0:n, :],
                                   start=(j == 0), stop=True, skip_group_check=True)
                mm.then_inc(q[l, "bias_ready"], 1)

            def up(l, b, f):
                pe.wait_ge(q[l, "hidden_ready"], start[l, "hidden_ready"] + b * NF[l] + f + 1)
                w1 = W(l, "w1")[:, P * f:P * (f + 1)]
                if l == 1:
                    pe.matmul(ps[:, MI, :], W(l, "w3")[:, P * f:P * (f + 1)], xb[:, :], start=True, stop=True)
                pe.matmul(ps[:, UP, :], w1, xb[:, :], start=True, stop=True).then_inc(q[l, "up_ready"], 1)

            def down(l, b, f):
                pe.wait_ge(q[l, "hidden_ready"], start[l, "hidden_ready"] + b * NF[l] + f + 2)
                if f == 0:
                    pe.wait_ge(q[l, "gate_seen"], start[l, "gate_seen"] + b + 1)
                for e, lo, n, src, one, last in DG[l][f]:
                    if one:
                        pe.wait_ge(q[l, "y_free"], start[l, "y_free"] + b * NE[l] + e + 1)
                    buf = hidh[:, :] if l == 1 and len(CH1[src]) == 2 else hid[:, src % 2, :]
                    for j in range(TB):
                        mm = pe.matmul(ps[:, YB, P * j:P * (j + 1)], buf[lo:lo + n, P * j:P * (j + 1)],
                                       W(l, "w2")[lo:lo + n, P * src:P * (src + 1)],
                                       start=(one and j == 0), stop=True, skip_group_check=True)
                    mm.then_inc(q[l, "y_ready"], 1)

            def layer0():
                l = 0
                pe.wait_ge(s_w[0], 32)
                pe.wait_ge(s_sel, 16)
                pe.wait_ge(xnt_ready[before[l]], NB + 1)
                pe.sem_inc(q[l, "y_ready0"], 2)
                with pe.Fori(0, NB) as b:
                    pe.wait_ge(q[l, "xb_ready"], start[l, "xb_ready"] + b + 1)
                    pe.wait_ge(q[l, "tail_done"], start[l, "tail_done"] + b + 1)
                    if l != layers[-1]:
                        pe.wait_ge(xnt_ready[l], b + 1)
                    for c in range(4):
                        pe.matmul(ps[:, c, :], W(l, "in_w")[:, P * c:P * (c + 1)], xb[:, :],
                                  start=True, stop=True).then_inc(q[l, "proj_ready"], 1)
                    gate(l, YB, b, q[l, "proj_ready"])
                    mixture_bias(l, b)
                    pe.wait_ge(q[l, "xconv_ready"], 2 * b + 2)
                    pe.wait_ge(q[l, "xp_ready"], 2 * b + 2)
                    pe.wait_ge(q[l, "zbias_ready"], 2 * b + 2)
                    for g in range(2):
                        for k in range(2):
                            mm = pe.matmul(ps[:, g, :], W(l, "dt_w")[:, INNER * k + P * g:INNER * k + P * (g + 1)],
                                           l0["xconv"][:, k, :], start=(k == 0), stop=(k == 1))
                        mm.then_inc(q[l, "dtbc_ready"], 1)
                    for k in range(2):
                        mm = pe.matmul(ps[0:2 * NST, 2, :], W(l, "bc_w")[:, 2 * NST * k:2 * NST * (k + 1)],
                                       l0["xconv"][:, k, :], start=(k == 0), stop=(k == 1))
                    mm.then_inc(q[l, "dtbc_ready"], 1)
                    pe.wait_ge(q[l, "dt_ready"], b + 1)
                    pe.wait_ge(q[l, "bcs_ready"], b + 1)
                    pe.wait_ge(q[l, "bias_seen"], start[l, "bias_seen"] + b + 1)

                    def state_rows(s):
                        pe.wait_ge(q[l, "hc_ready"], 2 * NST * b + 2 * s + 2)
                        for n in range(2):
                            mm = pe.matmul(ps[:, 2 * (s % 2) + n, :], l0["sel"][0:6 * NST, s + NST * n, :],
                                           l0["bcs"][0:6 * NST, :], start=True, stop=True)
                        mm.then_inc(q[l, "bc_rows"], 1)

                    def state_sum(s):
                        for g in range(2):
                            pe.wait_ge(q[l, "hc_ready"], 2 * NST * b + 2 * s + g + 5)
                            mm = pe.matmul(ps[:, (PV, MI)[g], :], eye, l0["hc"][:, g, :],
                                           start=(s == 0), stop=(s == NST - 1), skip_group_check=True)
                            mm.then_inc(q[l, "y_ready0"], 1)

                    for kind, n in schedule(l):
                        if kind == "s":
                            state_rows(n)
                            if n:
                                state_sum(n - 1)
                        elif kind == "f":
                            up(l, b, n)
                            if n:
                                down(l, b, n - 1)
                        else:
                            state_sum(NST - 1)
                            down(l, b, NF[l] - 1)
                    pe.wait_ge(q[l, "yg_ready"], b + 1)
                    for j in range(TB):
                        for k in range(2):
                            mm = pe.matmul(ps[:, PV, P * j:P * (j + 1)], l0["y"][:, k, P * j:P * (j + 1)],
                                           W(l, "out_w")[:, D * k:D * (k + 1)],
                                           start=(j == 0 and k == 0), stop=True, skip_group_check=True)
                    mm.then_inc(q[l, "attn_ready"], 1)
                    if l != layers[-1]:
                        turn_xn(l, b)

            def pe_route():
                l = 3
                pe.wait_ge(s_w[l], 32)
                pe.wait_ge(xnt_ready[before[l]], NB + 1)
                for i in range(NT):
                    mm = pe.matmul(ps[:, YB, E3 * i:E3 * (i + 1)], xnt[:, P * i:P * (i + 1)], W(l, "gate_w"),
                                   start=(i == 0), stop=True, skip_group_check=True)
                mm.then_inc(q[l, "logits_ready"], 1)
                pe.wait_ge(q[l, "stack_built"], 1)
                for k, src in enumerate((r_parts, r_hot)):
                    for i in range(NT):
                        mm = pe.transpose(ps[0:3 * PART, 4 * k + i // 4, P * (i % 4):P * (i % 4 + 1)], src[:, i, :],
                                          eye)
                    mm.then_inc(q[l, "stack_turned"], 1)
                pe.wait_ge(q[l, "stack_parts"], 1)
                pe.wait_ge(q[l, "stack_hot"], 1)
                for i in range(NT):
                    if i >= 2:
                        pe.wait_ge(q[l, "ranked"], i - 1)
                    for c in range(TB):
                        mm = pe.matmul(ps[:, 4 * (i % 2) + c, :], r_hott[:, P * i:P * (i + 1)],
                                       r_partst[:, T * c:T * (c + 1)], start=True, stop=True)
                    mm.then_inc(q[l, "row_ready"], 1)
                pe.wait_ge(q[l, "slots_in"], 16)
                for n in range(ST // 4):
                    if n == 4:
                        pe.wait_ge(q[l, "slots_turned"], 1)
                    for k in range(4):
                        mm = pe.transpose(ps[:, n % 4, P * k:P * (k + 1)], xe[:, 4 * n + k, :], eye)
                    mm.then_inc(q[l, "slots_turning"], 1)
                pe.wait_ge(q[l, "slots_turned"], ST // 4)

                def expert_up(e):
                    if e >= 2:
                        pe.wait_ge(q[l, "expert_hidden"], e - 1)
                    for c in range(2):
                        mm = pe.matmul(ps[:, 4 + e % 2, CAP * c:CAP * (c + 1)],
                                       W(l, "w1")[:, FF3 * e + P * c:FF3 * e + P * (c + 1)],
                                       xet[:, CAP * e:CAP * (e + 1)], start=(c == 0), stop=True, skip_group_check=True)
                    mm.then_inc(q[l, "expert_up"], 1)

                def expert_down(e):
                    pe.wait_ge(q[l, "expert_hidden"], e + 1)
                    if e >= 2:
                        pe.wait_ge(q[l, "expert_out"], e - 1)
                    for c in range(2):
                        mm = pe.matmul(ps[:, 6 + e % 2, 0:CAP], W(l, "w2")[:, P * (2 * e + c):P * (2 * e + c + 1)],
                                       hid[:, e % 2, CAP * c:CAP * (c + 1)], start=(c == 0), stop=(c == 1))
                    mm.then_inc(q[l, "expert_down"], 1)

                for e in range(E3):
                    expert_up(e)
                    if e:
                        expert_down(e - 1)
                expert_down(E3 - 1)
                pe.wait_ge(q[l, "expert_out"], E3)
                for n in range(ST // 4):
                    if n == 4:
                        pe.wait_ge(q[l, "slots_turned"], ST // 4 + 1)
                    for k in range(4):
                        mm = pe.transpose(ps[:, n % 4, P * k:P * (k + 1)], xet[:, P * (4 * n + k):P * (4 * n + k + 1)],
                                          eye)
                    mm.then_inc(q[l, "slots_turning"], 1)
                pe.wait_ge(q[l, "slots_turned"], 2 * (ST // 4))

            def attention_layer(l):
                kind = KIND[l]
                ua, ub, st = units[l]
                pe.wait_ge(s_w[l], 48 if l == 2 else 32)
                pe.wait_ge(xnt_ready[before[l]], NB + 1)
                with pe.Fori(0, NB) as b:
                    pe.wait_ge(q[l, "xb_ready"], start[l, "xb_ready"] + b + 1)
                    pe.wait_ge(q[l, "tail_done"], start[l, "tail_done"] + b + 1)
                    if l != layers[-1]:
                        pe.wait_ge(xnt_ready[l], b + 1)
                    pe.wait_ge(q[l, "exp_done"], start[l, "exp_done"] + b * NUB[l] + 2)
                    names = {1: ("wq", "wk"), 2: ("wq", "wqs", "wk", "wks"), 3: ("wq", "wk")}[l]
                    for c, n in enumerate(names):
                        pe.matmul(ps[:, c, :], W(l, n), xb[:, :], start=True, stop=True)\
                          .then_inc(q[l, "proj_ready"], 1)
                    for j in range(TB):
                        mm = pe.matmul(ps[:, PV, P * j:P * (j + 1)], xb[:, P * j:P * (j + 1)], W(l, "wv"),
                                       start=(j == 0), stop=True, skip_group_check=True)
                    mm.then_inc(q[l, "proj_ready"], 1)
                    if l != 3:
                        gate(l, YB, b, q[l, "proj_ready"])
                    if l == 2:
                        mixture_bias(l, b)
                        pe.wait_ge(q[l, "bias_seen"], start[l, "bias_seen"] + b + 1)

                    def scores_a(u):
                        if u == 0:
                            pe.wait_ge(q[l, "stacks_ready"], start[l, "stacks_ready"] + 16 * 2 * NSTK[l] * (b + 1))
                            if l in (1, 3):
                                pe.wait_ge(q[l, "rows_ready"], 16 * NROWS[l])
                            pe.wait_ge(q[l, "evac_done"], start[l, "evac_done"] + len(names) * (b + 1))
                        pe.wait_ge(q[l, "a_free"], start[l, "a_free"] + b * NUA[l] + u + 1)
                        base, begun = 2 * (u % 2), set()
                        for h, j, col, n in ua[u]:
                            p0, s = head(h)
                            bank, c0 = base + col // 512, col % 512
                            o_ = ps[:, bank, c0:c0 + n]
                            lhs = stack[0][p0:p0 + KA[l], s, P * j:P * (j + 1)]
                            first_ = bank not in begun
                            begun.add(bank)
                            if l == 1:
                                pe.matmul(o_, lhs, stack[1][p0:p0 + KA[l], s, 0:n], start=first_, stop=True,
                                          skip_group_check=True)
                                mm = pe.matmul(o_[:, n - P:n], eyeb, W("c16", "mask_a"), start=False, stop=True,
                                               skip_group_check=True)
                            else:
                                cut = P * (j + 1)
                                mm = pe.matmul(o_[:, 0:cut], lhs, stack[1][p0:p0 + KA[l], s, 0:cut], start=first_,
                                               stop=True, skip_group_check=True)
                                if cut < T:
                                    pe.matmul(o_[:, cut:T], lhs, stack[2][p0:p0 + KA[l], s, cut:T], start=False,
                                              stop=True, skip_group_check=True)
                                mm = pe.matmul(o_[:, cut - P:cut], slope[:, P * h:P * (h + 1)],
                                               W("c16", "back_a"), start=False, stop=True, skip_group_check=True)
                        mm.then_inc(q[l, "a_ready"], 1)

                    def turn_max():
                        pe.wait_ge(q[l, "a_free"], start[l, "a_free"] + NUA[l] * (b + 1) + 2)
                        for j in range(TB):
                            mm = pe.transpose(ps[0:NH, 0, P * j:P * (j + 1)], mx[:, j, :], eye)
                        mm.then_inc(q[l, "max_turned"], 1)

                    def scores_b(u):
                        if u == 0:
                            if l == 2:
                                pe.wait_ge(q[l, "stacks_ready"], start[l, "stacks_ready"] + 16 * 2 * NSTK[l] * (b + 1))
                                pe.wait_ge(q[l, "evac_done"], start[l, "evac_done"] + len(names) * (b + 1))
                                pe.wait_ge(q[l, "parts_ready"], start[l, "parts_ready"] + 4 * (b + 1))
                            else:
                                pe.wait_ge(q[l, "max_in"], start[l, "max_in"] + 32 * (b + 1))
                                pe.wait_ge(q[l, "max_parts"], start[l, "max_parts"] + b + 1)
                        pe.wait_ge(q[l, "exp_done"], start[l, "exp_done"] + b * NUB[l] + u + 1)
                        base, begun = 2 * (u % 2), set()
                        plain, regions = ub[u]
                        for h, c, col, n in regions:
                            p0, s = head(h)
                            bank, c0 = base + col // 512, col % 512
                            o_ = ps[:, bank, c0:c0 + n]
                            first_ = bank not in begun
                            begun.add(bank)
                            rows_ = KROWS if l == 2 else KALL
                            qs = stack[2 if (l == 2 and not plain) else 0][p0:p0 + rows_, s, :]
                            ks = stack[3 if (l == 2 and not plain) else 1][p0:p0 + rows_, s, P * c:P * (c + 1)]
                            if l == 1:
                                pe.matmul(o_, ks, qs[:, P * c:T], start=first_, stop=True, skip_group_check=True)
                                mm = pe.matmul(o_[:, 0:P], eyeb, W("c16", "mask_b"), start=False, stop=True,
                                               skip_group_check=True)
                            elif l == 2:
                                mm = pe.matmul(o_, ks, qs, start=True, stop=True)
                            else:
                                pe.matmul(o_[:, P * c:T], ks, qs[:, P * c:T], start=True, stop=True,
                                          skip_group_check=True)
                                if c:
                                    kn = stack[2][p0:p0 + rows_, s, P * c:P * (c + 1)]
                                    pe.matmul(o_[:, 0:P * c], kn, qs[:, 0:P * c], start=False, stop=True,
                                              skip_group_check=True)
                                mm = pe.matmul(o_[:, P * c:P * (c + 1)], slope[:, P * h:P * (h + 1)],
                                               W("c16", "back_b"), start=False, stop=True, skip_group_check=True)
                        mm.then_inc(q[l, "b_ready"], 1)

                    def values(s):
                        g, what, end = st[s]
                        pe.wait_ge(q[l, "exp_done"], start[l, "exp_done"] + b * NUB[l] + end + 2)
                        first_ = s == 0 or st[s - 1][0] != g
                        if first_:
                            pe.wait_ge(q[l, "pv_free"], start[l, "pv_free"] + b * QUADS + g + 1)
                            if s == 0:
                                pe.wait_ge(q[l, "values_ready"], start[l, "values_ready"] + b + 1)
                        if what == "x":
                            regions = [(0, 0, 0, 512, pt[g % 2]), (1, 128, 512, 384, pt[g % 2]), (3, 384, 896, 128, pt[g % 2])]
                        elif what == "y":
                            regions = [(2, 256, 0, 256, pty)]
                        else:
                            regions = [(2 * what[1] + n, 0, 512 * n, 512, pt[s % 2]) for n in range(2)]
                        for k, (c, q0, col, n, buf) in enumerate(regions):
                            for i in range(4):
                                h = 4 * g + i
                                plain = what not in ("x", "y") and what[0]
                                lhs = onesv[:, :] if plain else vx[:, c, VW * h:VW * h + 32]
                                slot = by_parity(range(4)).index(i) if what == "y" else i
                                mm = pe.matmul(ps[32 * i:32 * i + 32, PV, q0:q0 + n], lhs, buf[:, slot, col:col + n],
                                               start=(first_ and k == 0), stop=True, skip_group_check=True)
                        mm.then_inc(q[l, "pv_done"], 1)

                    def denominators(g):
                        pe.wait_ge(q[l, "head_copied"], start[l, "head_copied"] + b * QUADS + g + 1)
                        pe.matmul(ps[:, PV, :], seld, ot[:, :], start=True, stop=True)\
                          .then_inc(q[l, "den_ready"], 1)

                    for what, n in schedule(l):
                        if what == "f":
                            up(l, b, n)
                            if n:
                                down(l, b, n - 1)
                        elif what == "fl":
                            down(l, b, NF[l] - 1)
                        elif what == "a":
                            scores_a(n)
                        elif what == "mx":
                            turn_max()
                        elif what == "b":
                            scores_b(n)
                        elif what == "pv":
                            values(n)
                        else:
                            denominators(n)
                    pe.wait_ge(q[l, "on_ready"], start[l, "on_ready"] + QUADS * (b + 1))
                    for j in range(TB):
                        for g in range(QUADS):
                            mm = pe.matmul(ps[:, PV, P * j:P * (j + 1)], on[:, g, P * j:P * (j + 1)],
                                           W(l, "wp")[:, D * g:D * (g + 1)], start=(j == 0 and g == 0), stop=True,
                                           skip_group_check=True)
                    mm.then_inc(q[l, "attn_ready"], 1)
                    if l != layers[-1]:
                        turn_xn(l, b)

            pe.sem_inc(q[0, "y_ready"], 1)
            pe.sem_inc(q[0, "pv_done"], 2)
            pe.wait_ge(s_c32, 16)
            pe.wait_ge(s_c16, 16)
            with pe.Fori(0, NB) as b:
                turn_xn("pre", b)
            for l in layers:
                if l == 0:
                    layer0()
                else:
                    if l == 3:
                        pe_route()
                    attention_layer(l)

        @block.scalar
        def _(act):
            al = sem("scalar_own")
            own = Links(act, al)

            def take_xnt(l, b):
                act.wait_ge(xn_turned[l], b + 1)
                act.activation(xnt[:, span(b)], ps[:, MI, :], ACT.Copy).then_inc(xnt_ready[l], 1)

            def gate_exp(l, b):
                act.wait_ge(q[l, "gate_diff"], start[l, "gate_diff"] + b + 1)
                if l == 2:
                    act.activation(cw2[:, :, 0:9], cw[:, :, 0:9], ACT.Exp).then_inc(q[l, "gate_exp"], 1)
                else:
                    act.activation(gd[:, 1, :], gd[:, 0, :], ACT.Exp).then_inc(q[l, "gate_exp"], 1)

            def hidden(l, b, f):
                act.wait_ge(q[l, "up_ready"], start[l, "up_ready"] + b * NF[l] + f + 1)
                if l == 1:
                    act.activation(act_t[:, :], ps[:, UP, :], ACT.Tanh, scale=0.5).then_inc(q[l, "tanh_done"], 1)
                    return
                act.wait_ge(q[l, "y_ready"], start[l, "y_ready"] + b * NY[l] + (upto(l, f - 2) if f >= 2 else 0) + 1)
                act.activation(hid[:, f % 2, :], ps[:, UP, :], ACT.Gelu, bias=W(l, "b1")[:, f:f + 1])\
                   .then_inc(q[l, "hidden_ready"], 1)

            def gate_tanh(l, b):
                act.wait_ge(q[l, "y_free"], start[l, "y_free"] + NE[l] * (b + 1) + 1)
                act.activation(act_t[:, :], facc[:, :, :], ACT.Tanh, scale=0.5).then_inc(q[l, "fgate_ready"], 1)

            def layer0():
                l = 0
                act.wait_ge(s_w[0], 32)
                act.activation(small[:, 16:48], W(l, "a_log"), ACT.Exp).then_inc(q[l, "a_exp"], 1)
                act.wait_ge(dn_set, 1)
                with act.Fori(0, NB) as b:
                    own.enter(b, "act0")
                    for g in range(2):
                        act.wait_ge(q[l, "proj_ready"], start[l, "proj_ready"] + NPROJ[l] * b + g + 1)
                        act.activation(l0["xp"][:, g, KC - 1:], ps[:, g, :], ACT.Identity,
                                       bias=W(l, "in_b")[:, g:g + 1]).then_inc(q[l, "xp_ready"], 1)
                    for g in range(2):
                        act.wait_ge(q[l, "proj_ready"], start[l, "proj_ready"] + NPROJ[l] * b + g + 3)
                        act.activation(l0["zs"][:, g, :], ps[:, 2 + g, :], ACT.Identity,
                                       bias=small[:, 10 + g:11 + g], scale=0.5).then_inc(q[l, "zbias_ready"], 1)
                    act.wait_ge(q[l, "zbias_ready"], 2 * b + 2)
                    act.activation(l0["tmp"][:, :, :], l0["zs"][:, :, :], ACT.Tanh).then_inc(q[l, "z_tanh"], 1)
                    for g in range(2):
                        act.wait_ge(q[l, "conv_ready"], 2 * b + g + 1)
                        act.activation(l0["xconv"][:, g, :], l0["xc"][:, g, :], ACT.Tanh)\
                           .then_inc(q[l, "conv_tanh"], 1)
                    gate_exp(l, b)
                    for g in range(2):
                        act.wait_ge(q[l, "dt_abs"], 2 * b + g + 1)
                        own.add(act.activation(l0["dtx"][:, g, :], l0["dt"][:, g, :], ACT.Abs))
                    own.wait(1)
                    own.add(act.activation(l0["dtx"][:, 0, :], l0["dtx"][:, 0, :], ACT.Exp, scale=-1.0))
                    own.wait(2)
                    own.add(act.activation(l0["dtx"][:, 1, :], l0["dtx"][:, 1, :], ACT.Exp, scale=-1.0))
                    own.wait(3)
                    own.add(act.activation(l0["dtx"][:, 0, :], l0["dtx"][:, 0, :], ACT.Ln, bias=1.0))
                    own.wait(4)
                    act.activation(l0["dtx"][:, 1, :], l0["dtx"][:, 1, :], ACT.Ln, bias=1.0)\
                       .then_inc(q[l, "dt_ln"], 1)
                    act.wait_ge(q[l, "dt_ready"], b + 1)

                    def decay(s):
                        for g in range(2):
                            act.wait_ge(q[l, "da_free"], 2 * NST * b + 2 * s + g + 1)
                            act.activation(l0[f"da{s % 2}"][:, g, :], l0["dt"][:, g, :], ACT.Exp,
                                           scale=small[:, 16 + NST * g + s:17 + NST * g + s])\
                               .then_inc(q[l, "da_ready"], 1)

                    decay(0)
                    for what, n in schedule(l):
                        if what == "s" and n + 1 < NST:
                            decay(n + 1)
                        elif what == "f":
                            hidden(l, b, n)
                    gate_tanh(l, b)
                    if l != layers[-1]:
                        take_xnt(l, b)
                    own.close("act0")

            def act_route():
                l = 3
                act.wait_ge(q[l, "logits_shifted"], 1)
                act.activation(r_w[:, :, :], r_w[:, :, :], ACT.Exp).then_inc(q[l, "logits_exp"], 1)
                act.wait_ge(q[l, "stack_turned"], 1)
                act.activation(r_partst, ps[0:3 * PART, 0:4, :], ACT.Copy).then_inc(q[l, "stack_parts"], 1)
                for n in range(ST // 4):
                    act.wait_ge(q[l, "slots_turning"], n + 1)
                    act.activation(xet[:, T * n:T * (n + 1)], ps[:, n % 4, :], ACT.Copy)\
                       .then_inc(q[l, "slots_turned"], 1)
                for e in range(E3):
                    act.wait_ge(q[l, "expert_up"], e + 1)
                    if e >= 2:
                        act.wait_ge(q[l, "expert_down"], e - 1)
                    for c in range(2):
                        ins = act.activation(hid[:, e % 2, CAP * c:CAP * (c + 1)],
                                             ps[:, 4 + e % 2, CAP * c:CAP * (c + 1)], ACT.Gelu_apprx_tanh,
                                             bias=W(l, "b1")[:, 2 * e + c:2 * e + c + 1])
                    ins.then_inc(q[l, "expert_hidden"], 1)
                for n in range(ST // 4):
                    act.wait_ge(q[l, "slots_turning"], ST // 4 + n + 1)
                    act.activation(xe[:, 4 * n:4 * n + 4, :], ps[:, n % 4, :], ACT.Copy)\
                       .then_inc(q[l, "slots_turned"], 1)
                act.wait_ge(q[l, "gathered"], 16 * NT)
                act.activation(xe[:, 0:NT, :], gs[:, :, :], ACT.Tanh, scale=0.5).then_inc(q[l, "mixture_tanh"], 1)

            def attention_layer(l):
                rs = float(DH) ** -0.5
                _, ub, st = units[l]
                act.wait_ge(s_w[l], 48 if l == 2 else 32)
                stage_of = {}
                lo = 0
                for s, (g, what, end) in enumerate(st):
                    for u in range(lo, end):
                        stage_of[u] = (s, g, what, u - lo)
                    lo = end
                if l == 3:
                    act_route()
                with act.Fori(0, NB) as b:
                    for c in range(EV[l]):
                        act.wait_ge(q[l, "proj_ready"], start[l, "proj_ready"] + NPROJ[l] * b + c + 1)
                        isq = c < EV[l] // 2
                        if l == 3:
                            ins = act.activation(vf[c], ps[:, c, :], ACT.Identity, scale=rs if isq else 1.0,
                                                 bias=small[:, 48:49] if isq else W(l, "bk"))
                        else:
                            ins = act.activation(vf[c], ps[:, c, :], ACT.Copy, scale=rs if isq else 1.0)
                        ins.then_inc(q[l, "evac_done"], 1)
                    if l != 3:
                        gate_exp(l, b)

                    def probabilities(u):
                        s, g, what, n = stage_of[u]
                        act.wait_ge(q[l, "b_ready"], start[l, "b_ready"] + b * NUB[l] + u + 1)
                        if n == 0:
                            act.wait_ge(q[l, "pv_done"], start[l, "pv_done"] + b * NS[l] + s + 1)
                        src = ps[:, 2 * (u % 2):2 * (u % 2) + 2, :]
                        if what == "y":
                            dst, src = pty[:, :, :], src.rearrange("p k (i c) -> p (k i) c", c=256)
                        elif what == "x":
                            dst = pt[g % 2][:, n, :].rearrange("p (k c) -> p k c", k=2)
                        else:
                            dst = pt[s % 2][:, n, :].rearrange("p (k c) -> p k c", k=2)
                        act.activation(dst, src, ACT.Exp).then_inc(q[l, "exp_done"], 1)

                    for what, n in schedule(l):
                        if what == "f":
                            hidden(l, b, n)
                        elif what == "b":
                            probabilities(n)
                    if l != 3:
                        gate_tanh(l, b)
                    if l != layers[-1]:
                        take_xnt(l, b)

            act.sem_inc(q[0, "hidden_ready"], 1)
            act.sem_inc(q[0, "exp_done"], 2)
            for n in ("pre",) + tuple(layers):
                act.sem_inc(xnt_ready[n], 1)
            with act.Fori(0, NB) as b:
                take_xnt("pre", b)
            for l in layers:
                layer0() if l == 0 else attention_layer(l)

        @block.vector
        def _(dve):
            own = Links(dve, dl)
            tt, stt, ts, cp = dve.tensor_tensor, dve.scalar_tensor_tensor, dve.tensor_scalar, dve.tensor_copy

            def moments(src, l, n):
                wait_done(dve, 0)
                for j in range(TB):
                    own.add(dve.bn_stats(stat[:, j, :], src(j)))
                own.wait()
                wait_done(dve, 0)
                for j in range(TB):
                    ins = dve.bn_aggr(mv[:, j, :], stat[:, j, :])
                ins.then_inc(var_ready[l], 1)
                dve.wait_ge(rstd_ready[l], n)

            def normed(b, l, n):
                moments(lambda j: x[:, bass.ds(b * TB + j, 1), :].rearrange("p o d -> p (o d)"), l, n)
                for j in range(TB):
                    own.add(ts(xn[:, bass.ds(b * TB + j, 1), :].rearrange("p o d -> p (o d)"),
                               x[:, bass.ds(b * TB + j, 1), :].rearrange("p o d -> p (o d)"),
                               mv[:, j, 0:1], rstd[:, j:j + 1], ALU.subtract, ALU.mult))
                own.wait()
                ts(xs[:, :, :], xn[:, bass.ds(b * TB, TB), :], 1.0, None, ALU.mult).then_inc(xn_ready[l], 1)

            def gates(l, b, count):
                n = NE[l]
                dve.wait_ge(q[l, "proj_ready"], start[l, "proj_ready"] + count)
                src = ps[:, YB, 0:16 * TB].rearrange("p (j e) -> p j e", e=16)[:, :, 0:n]
                if l == 0:
                    tt(lg[:, :, 0:n], src, W(l, "gate_b").unsqueeze(1).to_broadcast([P, TB, n]), ALU.add)\
                        .then_inc(q[l, "gate_seen"], 1)
                else:
                    cp(lg[:, :, 0:n], src).then_inc(q[l, "gate_seen"], 1)
                dve.wait_ge(q[l, "gate_seen"], start[l, "gate_seen"] + b + 1)
                wait_done(dve, 0)
                for j in range(TB):
                    own.add(dve.max(m8[:, j, :], lg[:, j, 0:8]))
                own.wait()
                wait_done(dve, 0)
                for j in range(TB):
                    own.add(dve.max_index(i8[:, j, :], m8[:, j, :], lg[:, j, 0:8]))
                if l == 2:
                    own.add(tt(cw[:, :, 0:8], lg[:, :, 0:8], m8[:, :, 0:1].to_broadcast([P, TB, 8]), ALU.subtract))
                    tt(cw[:, :, 8:9], m8[:, :, 1:2], m8[:, :, 0:1], ALU.subtract).then_inc(q[l, "gate_diff"], 1)
                else:
                    tt(gd[:, 0, :], m8[:, :, 1], m8[:, :, 0], ALU.subtract).then_inc(q[l, "gate_diff"], 1)
                own.wait()
                own.link(cp(fi[:, :, :], i8[:, :, :]))

            def weights(l, b):
                n = NE[l]
                dve.wait_ge(q[l, "gate_exp"], start[l, "gate_exp"] + b + 1)
                io = iota[:, 0:n].unsqueeze(1).to_broadcast([P, TB, n])
                if l == 2:
                    own.add(dve.tensor_reduce(gd[:, 1, :], cw2[:, :, 0:8], AX.X, ALU.add))
                    own.add(ts(gd[:, 2, :], cw2[:, :, 8], 1.0, None, ALU.add))
                    own.wait()
                    own.link(dve.reciprocal(gd[:, 3, :], gd[:, 1, :]))
                    own.add(tt(gd[:, 4, :], gd[:, 2, :], gd[:, 3, :], ALU.mult))
                    own.add(tt(cw[:, :, 0:n], io, fi[:, :, 0:1].to_broadcast([P, TB, n]), ALU.is_equal))
                    own.link(tt(cw2[:, :, 0:n], io, fi[:, :, 1:2].to_broadcast([P, TB, n]), ALU.is_equal))
                    own.link(tt(cw[:, :, 0:n], cw[:, :, 0:n], cw2[:, :, 0:n], ALU.add))
                    tt(cw[:, :, 0:n], cw[:, :, 0:n], gd[:, 4, :].unsqueeze(2).to_broadcast([P, TB, n]), ALU.mult)\
                        .then_inc(q[l, "cw_ready"], 1)
                else:
                    own.add(tt(cw[:, :, 0:n], io, fi[:, :, 0:1].to_broadcast([P, TB, n]), ALU.is_equal))
                    own.add(tt(cw2[:, :, 0:n], io, fi[:, :, 1:2].to_broadcast([P, TB, n]), ALU.is_equal))
                    own.link(ts(gd[:, 2, :], gd[:, 1, :], 1.0, None, ALU.add))
                    own.link(dve.reciprocal(gd[:, 3, :], gd[:, 2, :]))
                    own.add(tt(cw[:, :, 0:n], cw[:, :, 0:n], gd[:, 3, :].unsqueeze(2).to_broadcast([P, TB, n]), ALU.mult))
                    own.link(tt(gd[:, 4, :], gd[:, 1, :], gd[:, 3, :], ALU.mult))
                    own.link(tt(cw2[:, :, 0:n], cw2[:, :, 0:n], gd[:, 4, :].unsqueeze(2).to_broadcast([P, TB, n]), ALU.mult))
                    tt(cw[:, :, 0:n], cw[:, :, 0:n], cw2[:, :, 0:n], ALU.add).then_inc(q[l, "cw_ready"], 1)
                if l == 1:
                    return
                dve.wait_ge(q[l, "cwt_turned"], start[l, "cwt_turned"] + b + 1)
                cp(cwt[0:n, :], ps[0:n, MI, :]).then_inc(q[l, "cwt_ready"], 1)
                dve.wait_ge(q[l, "bias_ready"], start[l, "bias_ready"] + b + 1)
                cp(facc[:, :, :], ps[:, MI, :].rearrange("p (j d) -> p j d", j=TB)).then_inc(q[l, "bias_seen"], 1)

            def gated(b, f):
                l = 1
                dve.wait_ge(q[l, "tanh_done"], b * NF[l] + f + 1)
                own.link(stt(act_g[:, :], act_t[:, :], 1.0, ps[:, UP, :], ALU.add, ALU.mult))
                dve.wait_ge(q[l, "y_ready"], start[l, "y_ready"] + b * NY[l] + (upto(l, f - 2) if f >= 2 else 0) + 1)
                dst = hidh[:, :] if len(CH1[f]) == 2 else hid[:, f % 2, :]
                stt(dst, act_g[:, :], 0.5, ps[:, MI, :], ALU.mult, ALU.mult).then_inc(q[l, "hidden_ready"], 1)

            def mix(l, b, f):
                for n, (e, _, _, _, _, last) in enumerate(DG[l][f]):
                    if not last:
                        continue
                    dve.wait_ge(q[l, "y_ready"], start[l, "y_ready"] + b * NY[l] + upto(l, f - 1) + n + 2)
                    if l == 1 and e == 0:
                        pass
                    elif e == 0:
                        dve.wait_ge(q[l, "bias_seen"], start[l, "bias_seen"] + b + 1)
                    else:
                        dve.wait_ge(q[l, "y_free"], start[l, "y_free"] + b * NE[l] + e + 1)
                    if e == 0:
                        dve.wait_ge(q[l, "cw_ready"], start[l, "cw_ready"] + b + 1)
                    for j in range(TB):
                        yj = ps[:, YB, P * j:P * (j + 1)]
                        if l == 1 and e == 0:
                            ins = ts(facc[:, j, :], yj, cw[:, j, e:e + 1], None, ALU.mult)
                        else:
                            ins = stt(facc[:, j, :], yj, cw[:, j, e:e + 1], facc[:, j, :], ALU.mult, ALU.add)
                    ins.then_inc(q[l, "y_free"], 1)

            def combine(l, b):
                if l != 3:
                    dve.wait_ge(q[l, "fgate_ready"], start[l, "fgate_ready"] + b + 1)
                    own.link(stt(facc[:, :, :], act_t[:, :].rearrange("p (j d) -> p j d", j=TB), 1.0, facc[:, :, :],
                                 ALU.add, ALU.mult))
                    own.link(tt(sa[:, :, :], sa[:, :, :], facc[:, :, :], ALU.mult))
                else:
                    own.link(tt(sa[:, :, :], sa[:, :, :], gs[:, bass.ds(b * TB, TB), :], ALU.mult))
                xv = x[:, bass.ds(b * TB, TB), :]
                ins = stt(xv, sa[:, :, :], 0.5, xv, ALU.mult, ALU.add)
                if l != layers[-1]:
                    own.link(ins)
                    normed(b, l, (b + 1) if l == 0 else 2 * b + 2)
                else:
                    ins.then_inc(q[l, "layer_done"], 1)

            def spread_rows(v):
                return v.unsqueeze(1).to_broadcast([P, TB, v.shape[1]])

            def layer0():
                l = 0
                dve.wait_ge(s_w[0], 32)
                dve.sem_inc(q[l, "da_free"], 4)
                dve.sem_inc(q[l, "hc_ready"], 4)
                own.add(dve.memset(l0["xp"][:, :, 0:KC - 1], 0.0))
                own.add(ts(small[:, 0:8], W(l, "conv_w"), 0.5, None, ALU.mult))
                own.add(ts(small[:, 8:10], W(l, "conv_b"), 0.5, None, ALU.mult))
                own.add(ts(small[:, 10:12], W(l, "in_b")[:, 2:4], 0.5, None, ALU.mult))
                dve.wait_ge(q[l, "a_exp"], 1)
                ts(small[:, 16:48], small[:, 16:48], -1.0, None, ALU.mult).then_inc(dn_set, 1)
                own.straight()
                with dve.Fori(0, NB) as b:
                    own.enter(b, 0)
                    dve.wait_ge(xnt_ready[before[l]], b + 2)
                    ts(xb[:, :], xnt[:, span(b)], 1.0, None, ALU.mult).then_inc(q[l, "xb_ready"], 1)
                    for g in range(2):
                        dve.wait_ge(q[l, "xp_ready"], 2 * b + g + 1)
                        own.add(ts(l0["xc"][:, g, :], l0["xp"][:, g, 0:T], small[:, KC * g:KC * g + 1],
                                   small[:, 8 + g:9 + g], ALU.mult, ALU.add))
                    n0 = own.n
                    for k in range(1, KC):
                        for g in range(2):
                            own.wait(n0 + 2 * (k - 1) - 1 + g)
                            ins = stt(l0["xc"][:, g, :], l0["xp"][:, g, k:k + T], small[:, KC * g + k:KC * g + k + 1],
                                      l0["xc"][:, g, :], ALU.mult, ALU.add)
                            if k == KC - 1:
                                ins.then_inc(q[l, "conv_ready"], 1)
                            else:
                                own.add(ins)
                    gates(l, b, NPROJ[l] * (b + 1))
                    for g in range(2):
                        dve.wait_ge(q[l, "conv_tanh"], 2 * b + g + 1)
                        stt(l0["xconv"][:, g, :], l0["xconv"][:, g, :], 1.0, l0["xc"][:, g, :], ALU.add, ALU.mult)\
                            .then_inc(q[l, "xconv_ready"], 1)
                    weights(l, b)
                    dve.wait_ge(q[l, "z_tanh"], b + 1)
                    own.add(stt(l0["zs"][:, :, :], l0["tmp"][:, :, :], 1.0, l0["zs"][:, :, :], ALU.add, ALU.mult))
                    for g in range(2):
                        dve.wait_ge(q[l, "dtbc_ready"], 3 * b + g + 1)
                        ts(l0["dt"][:, g, :], ps[:, g, :], W(l, "dt_b")[:, g:g + 1], None, ALU.add)\
                            .then_inc(q[l, "dt_abs"], 1)
                    dve.wait_ge(q[l, "dtbc_ready"], 3 * b + 3)
                    n = 2 * NST
                    own.link(ts(l0["bcf"][0:n, :], ps[0:n, 2, :], W(l, "bc_b")[0:n, :], None, ALU.add))
                    own.link(cp(l0["bcs"][0:n, :], l0["bcf"][0:n, :]))
                    own.link(tt(l0["bcf"][0:n, :], l0["bcf"][0:n, :], l0["bcs"][0:n, :], ALU.subtract))
                    own.link(cp(l0["bcm"][0:n, :], l0["bcf"][0:n, :]))
                    own.add(cp(l0["bcs"][n:2 * n, :], l0["bcm"][0:n, :]))
                    tt(l0["bcs"][2 * n:3 * n, :], l0["bcf"][0:n, :], l0["bcm"][0:n, :], ALU.subtract)\
                        .then_inc(q[l, "bcs_ready"], 1)
                    dve.wait_ge(q[l, "dt_ln"], b + 1)
                    for g in range(2):
                        own.add(stt(l0["dt"][:, g, :], l0["dt"][:, g, :], 0.0, l0["dtx"][:, g, :], ALU.max, ALU.add))
                    own.wait()
                    own.add(tt(l0["dtx"][:, 0, :], l0["dt"][:, 0, :], l0["xconv"][:, 0, :], ALU.mult))
                    tt(l0["dtx"][:, 1, :], l0["dt"][:, 1, :], l0["xconv"][:, 1, :], ALU.mult)\
                        .then_inc(q[l, "dt_ready"], 1)
                    dve.wait_ge(q[l, "dt_ready"], b + 1)

                    def step(s):
                        dve.wait_ge(q[l, "bc_rows"], b * NST + s + 1)
                        k = 2 * (s % 2)
                        for g in range(2):
                            own.add(tt(l0["ub"][:, g, :], l0["dtx"][:, g, :], ps[:, k, :], ALU.mult))
                        n0 = own.n
                        at_ = 2 * NST * b + 2 * s
                        for g in range(2):
                            dve.wait_ge(q[l, "da_ready"], at_ + g + 1)
                            own.wait(n0 - 1 + g)
                            dve.tensor_tensor_scan(l0["hs"][:, g, :], l0[f"da{s % 2}"][:, g, :], l0["ub"][:, g, :],
                                                   0.0, ALU.mult, ALU.add).then_inc(q[l, "da_free"], 1)
                        for g in range(2):
                            dve.wait_ge(q[l, "y_ready0"], at_ + g + 1)
                            dve.wait_ge(q[l, "da_free"], at_ + g + 5)
                            tt(l0["hc"][:, g, :], l0["hs"][:, g, :], ps[:, k + 1, :], ALU.mult)\
                                .then_inc(q[l, "hc_ready"], 1)

                    for what, n in schedule(l):
                        if what == "s":
                            step(n)
                        elif what == "f":
                            if n:
                                mix(l, b, n - 1)
                        else:
                            mix(l, b, NF[l] - 1)
                    dve.wait_ge(q[l, "y_ready0"], 2 * NST * (b + 1) + 2)
                    for g in range(2):
                        own.add(stt(l0["y"][:, g, :], l0["xconv"][:, g, :], W(l, "d")[:, g:g + 1],
                                    ps[:, (PV, MI)[g], :], ALU.mult, ALU.add))
                    own.wait()
                    tt(l0["y"][:, :, :], l0["y"][:, :, :], l0["zs"][:, :, :], ALU.mult).then_inc(q[l, "yg_ready"], 1)
                    dve.wait_ge(q[l, "attn_ready"], start[l, "attn_ready"] + b + 1)
                    tt(sa[:, :, :], ps[:, PV, :].rearrange("p (j d) -> p j d", j=TB), spread_rows(W(l, "out_b")),
                       ALU.add).then_inc(q[l, "tail_done"], 1)
                    dve.wait_ge(q[l, "tail_done"], start[l, "tail_done"] + b + 2)
                    combine(l, b)
                    own.close(0)

            def dve_route():
                l = 3
                own.add(dve.memset(r_parts[:, :, :], 0.0))
                own.add(dve.memset(r_hot[:, :, :], 0.0))
                own.add(dve.memset(r_v[:, 1, :], 0.0))
                dve.wait_ge(q[l, "logits_ready"], 1)
                own.link(cp(r_lg[:, :, :], ps[:, YB, 0:NT * E3].rearrange("p (i e) -> p i e", e=E3)))
                for i in range(NT):
                    own.add(dve.max(r_m8[:, i, :], r_lg[:, i, :]))
                own.wait()
                for i in range(NT):
                    own.add(dve.max_index(r_i8[:, i, :], r_m8[:, i, :], r_lg[:, i, :]))
                tt(r_w[:, :, :], r_lg[:, :, :], r_m8[:, :, 0:1].to_broadcast([P, NT, E3]), ALU.subtract)\
                    .then_inc(q[l, "logits_shifted"], 1)
                own.wait()
                own.link(cp(r_fi[:, :, :], r_i8[:, :, :]))
                io = iota[:, 0:E3].unsqueeze(1).to_broadcast([P, NT, E3])
                own.add(tt(r_hot1[:, :, :], io, r_fi[:, :, 0:1].to_broadcast([P, NT, E3]), ALU.is_equal))
                dve.wait_ge(q[l, "logits_exp"], 1)
                own.link(dve.tensor_reduce(r_v[:, 8, :], r_w[:, :, :], AX.X, ALU.add))
                own.link(dve.reciprocal(r_v[:, 0, :], r_v[:, 8, :]))
                for k in range(3):
                    own.add(cp(r_hot[:, :, PART * k:PART * k + E3], r_hot1[:, :, :]))
                own.link(tt(r_w[:, :, :], r_hot1[:, :, :], r_v[:, 0, :].unsqueeze(2).to_broadcast([P, NT, E3]),
                            ALU.mult))
                high = r_b16[:, 0, :].rearrange("p (i e) -> p i e", e=E3)
                mid = r_b16[:, 1, :].rearrange("p (i e) -> p i e", e=E3)
                own.link(cp(high, r_w[:, :, :]))
                own.add(cp(r_parts[:, :, 0:E3], high))
                own.link(tt(r_w[:, :, :], r_w[:, :, :], high, ALU.subtract))
                own.link(cp(mid, r_w[:, :, :]))
                own.add(cp(r_parts[:, :, PART:PART + E3], mid))
                own.wait()
                tt(r_parts[:, :, 2 * PART:2 * PART + E3], r_w[:, :, :], mid, ALU.subtract)\
                    .then_inc(q[l, "stack_built"], 1)
                dve.wait_ge(q[l, "stack_turned"], 2)
                cp(r_hott.rearrange("p (k c) -> p k c", k=4), ps[0:3 * PART, 4:8, :]).then_inc(q[l, "stack_hot"], 1)
                for i in range(NT):
                    dve.wait_ge(q[l, "row_ready"], i + 1)
                    if i:
                        dve.wait_ge(q[l, "ranked"], i)
                    row = ps[:, 4 * (i % 2):4 * (i % 2) + 4, :].rearrange("p k c -> p (k c)")
                    mine = r_v[:, 0, i:i + 1]
                    if i:
                        own.add(ts(r_junk[:, 0:P * i], row[:, 0:P * i], mine, 0.0, ALU.is_ge, ALU.add,
                                   accum_out=r_v[:, 1, i:i + 1]))
                    own.add(ts(r_junk[:, P * i:NT * P], row[:, P * i:NT * P], mine, 0.0, ALU.is_gt, ALU.add,
                               accum_out=r_v[:, 2, i:i + 1]))
                    own.wait()
                    stt(r_junk[:, NT * P:], row[:, P * i:P * (i + 1)], mine, W("c32", "lower"), ALU.is_equal, ALU.mult,
                        accum_out=r_v[:, 3, i:i + 1]).then_inc(q[l, "ranked"], 1)
                dve.wait_ge(q[l, "ranked"], NT)
                own.add(tt(r_v[:, 4, :], r_v[:, 1, :], r_v[:, 2, :], ALU.add))
                own.link(stt(r_v[:, 5, :], r_fi[:, :, 0], float(CAP), W("c32", "drop"), ALU.mult, ALU.subtract))
                own.link(tt(r_v[:, 4, :], r_v[:, 4, :], r_v[:, 3, :], ALU.add))
                own.add(tt(r_v[:, 5, :], r_v[:, 5, :], r_v[:, 4, :], ALU.add))
                own.link(ts(r_v[:, 6, :], r_v[:, 4, :], float(CAP), None, ALU.is_lt))
                own.link(tt(r_v[:, 5, :], r_v[:, 5, :], r_v[:, 6, :], ALU.mult))
                own.link(tt(r_v[:, 5, :], r_v[:, 5, :], W("c32", "drop"), ALU.add))
                cp(r_idx, r_v[:, 5, :]).then_inc(q[l, "index_ready"], 1)
                for e in range(E3):
                    dve.wait_ge(q[l, "expert_down"], e + 1)
                    ts(xet[:, CAP * e:CAP * (e + 1)], ps[:, 6 + e % 2, 0:CAP], W(l, "b2")[:, e:e + 1], None, ALU.add)\
                        .then_inc(q[l, "expert_out"], 1)
                dve.wait_ge(q[l, "mixture_tanh"], 1)
                own.link(stt(gs[:, :, :], xe[:, 0:NT, :], 1.0, gs[:, :, :], ALU.add, ALU.mult))
                own.straight()

            def attention_layer(l):
                ua, ub, st = units[l]
                dve.wait_ge(s_w[l], 48 if l == 2 else 32)
                if l == 1:
                    own.add(dve.memset(lg[:, :, E1:8], NEG))
                if l == first:
                    own.add(dve.memset(vx[:, :, :], 0.0))
                    own.add(dve.memset(onesv[:, :], 0.0))
                    own.wait()
                elif l == 1:
                    own.add(dve.memset(vx[:, :, :], 0.0))
                    own.add(dve.memset(onesv[:, :], 0.0))
                    own.wait()
                own.add(dve.memset(vx[:, :, 0:NH * VW].rearrange("p j (h d) -> p j h d", d=VW)[:, :, :, DH:VW],
                                   0.0 if l == 2 else 1.0))
                own.add(dve.memset(onesv[:, DH:DH + 1], 1.0))
                if l == 3:
                    own.add(ts(small[:, 48:49], W(l, "bq"), float(DH) ** -0.5, None, ALU.mult))
                own.wait()
                own.straight()
                if l == 3:
                    dve_route()
                with dve.Fori(0, NB) as b:
                    own.enter(b, l)
                    dve.wait_ge(xnt_ready[before[l]], b + 2)
                    ts(xb[:, :], xnt[:, span(b)], 1.0, None, ALU.mult).then_inc(q[l, "xb_ready"], 1)

                    def parts(v, k):
                        own.link(cp(part[k][:, 0, :], vf[v]))
                        own.link(tt(vf[v], vf[v], part[k][:, 0, :], ALU.subtract))
                        own.link(cp(part[k][:, 1, :], vf[v]))
                        tt(part[k][:, 2, :], vf[v], part[k][:, 1, :], ALU.subtract).then_inc(q[l, "parts_ready"], 1)

                    if l == 2:
                        for v, k in ((0, 0), (2, 1)):
                            dve.wait_ge(q[l, "evac_done"], start[l, "evac_done"] + EV[l] * b + v + 2)
                            own.add(tt(act_g[:, :], vf[v], rope[0], ALU.mult))
                            own.link(tt(vf[v + 1], vf[v + 1], rope[1], ALU.mult))
                            own.link(tt(vf[v + 1], vf[v + 1], act_g[:, :], ALU.add))
                            parts(v, k)
                            parts(v + 1, k + 2)
                    else:
                        for k in range(2):
                            dve.wait_ge(q[l, "evac_done"], start[l, "evac_done"] + EV[l] * b + k + 1)
                            parts(k, k)
                    dve.wait_ge(q[l, "proj_ready"], start[l, "proj_ready"] + NPROJ[l] * b + EV[l] + 1)
                    pv_in = ps[:, PV, :].rearrange("p (j h d) -> p j h d", j=TB, d=DH)
                    for j in range(TB):
                        if l == 3:
                            ins = tt(vx[:, j, 0:NH * VW].rearrange("p (h d) -> p h d", d=VW)[:, :, 0:DH], pv_in[:, j], W(l, "bv").rearrange("p (h d) -> p h d", d=DH),
                                     ALU.add)
                        else:
                            ins = cp(vx[:, j, 0:NH * VW].rearrange("p (h d) -> p h d", d=VW)[:, :, 0:DH], pv_in[:, j])
                        if j == TB - 1:
                            ins.then_inc(q[l, "values_ready"], 1)
                    if l != 3:
                        gates(l, b, NPROJ[l] * (b + 1))
                        weights(l, b)

                    def column(h):
                        return (h % 2) * (NH // 2) + h // 2

                    def maxima(u):
                        dve.wait_ge(q[l, "a_ready"], start[l, "a_ready"] + b * NUA[l] + u + 1)
                        base = 2 * (u % 2)
                        flat = ps[:, base:base + 2, :].rearrange("p k c -> p (k c)")
                        if l == 3:
                            h, j = ua[u][0][0], ua[u][0][1]
                            ins = dve.tensor_reduce(mx[:, j:j + 2, column(h)], ps[:, base:base + 2, :], AX.X, ALU.max,
                                                    negate=True)
                        elif len(ua[u]) == 4:
                            g = ua[u][0][0] // 4
                            dst = mx[:, 1, :].rearrange("p (a s) -> p a s", a=2)[:, :, 2 * g:2 * g + 2]
                            ins = dve.tensor_reduce(dst, ps[:, base:base + 2, :].rearrange("p k (i c) -> p k i c", c=256),
                                                    AX.X, ALU.max, negate=True)
                        else:
                            for h, j, col, n in ua[u]:
                                c = column(h)
                                ins = dve.tensor_reduce(mx[:, j, c:c + 1], flat[:, col:col + n], AX.X, ALU.max,
                                                        negate=True)
                        ins.then_inc(q[l, "a_free"], 1)

                    for what, n in schedule(l):
                        if what == "f":
                            if l == 1:
                                gated(b, n)
                            if n:
                                mix(l, b, n - 1)
                        elif what == "fl":
                            mix(l, b, NF[l] - 1)
                        elif what == "a":
                            maxima(n)
                        elif what == "mx":
                            dve.wait_ge(q[l, "max_turned"], start[l, "max_turned"] + b + 1)
                            own.link(cp(nm[:, 0, :], ps[0:NH, 0, :]))
                            tt(nm[:, 1, :], ps[0:NH, 0, :], nm[:, 0, :], ALU.subtract).then_inc(q[l, "max_parts"], 1)
                        elif what == "pv":
                            if n + 1 == NS[l] or st[n + 1][0] != st[n][0]:
                                dve.wait_ge(q[l, "pv_done"], start[l, "pv_done"] + b * NS[l] + n + 3)
                                if st[n][0]:
                                    dve.wait_ge(q[l, "on_ready"], start[l, "on_ready"] + b * QUADS + st[n][0])
                                cp(ot[:, :], ps[:, PV, :]).then_inc(q[l, "head_copied"], 1)
                        elif what == "bc":
                            dve.wait_ge(q[l, "den_ready"], start[l, "den_ready"] + b * QUADS + n + 1)
                            if n:
                                dve.wait_ge(q[l, "on_ready"], start[l, "on_ready"] + b * QUADS + n)
                            dve.reciprocal(rc[:, :], ps[:, PV, :]).then_inc(q[l, "pv_free"], 1)
                            dve.wait_ge(q[l, "pv_free"], start[l, "pv_free"] + b * QUADS + n + 2)
                            tt(on[:, n, :], ot[:, :], rc[:, :], ALU.mult).then_inc(q[l, "on_ready"], 1)
                    dve.wait_ge(q[l, "attn_ready"], start[l, "attn_ready"] + b + 1)
                    pj = ps[:, PV, :].rearrange("p (j d) -> p j d", j=TB)
                    xv = xn[:, bass.ds(b * TB, TB), :]
                    tt(sa[:, :, :], pj, xv if l == 2 else spread_rows(W(l, "bp")), ALU.add)\
                        .then_inc(q[l, "tail_done"], 1)
                    dve.wait_ge(q[l, "tail_done"], start[l, "tail_done"] + b + 2)
                    if l == 1:
                        own.link(tt(sa[:, :, :], sa[:, :, :], xv, ALU.add))
                    if l != 3:
                        moments(lambda j: sa[:, j, :], l, 2 * b + 1 if l != layers[-1] else b + 1)
                        for j in range(TB):
                            own.add(ts(sa[:, j, :], sa[:, j, :], mv[:, j, 0:1], rstd[:, j:j + 1], ALU.subtract, ALU.mult))
                        own.wait()
                        own.link(tt(sa[:, :, :], sa[:, :, :], spread_rows(W(l, "gamma")), ALU.mult))
                        own.link(tt(sa[:, :, :], sa[:, :, :], spread_rows(W(l, "beta")), ALU.add))
                    combine(l, b)
                    own.close(l)

            dve.sem_inc(q[0, "tail_done"], 1)
            dve.sem_inc(q[0, "y_free"], 1)
            dve.sem_inc(q[0, "pv_free"], 1)
            dve.sem_inc(q[0, "a_free"], 2)
            dve.wait_ge(s_x, 16)
            with dve.Fori(0, NB) as b:
                own.enter(b, "pre")
                dve.wait_ge(xnt_ready["pre"], b + 1)
                normed(b, "pre", b + 1)
                own.close("pre")
            for l in layers:
                layer0() if l == 0 else attention_layer(l)

        @block.gpsimd
        def _(pool):
            own = Links(pool, pl)
            own.add(pool.memset(half[:, :], -0.5))

            def serve(l, n, key):
                pool.wait_ge(var_ready[l], n)
                wait_done(pool, 1)
                own.link(pool.tensor_scalar(vare[:, :], mv[:, :, 1], EPS, None, ALU.add))
                pool.tensor_tensor(rstd[:, :], vare[:, :], half[:, :], ALU.pow).then_inc(rstd_ready[l], 1)

            def pool_route():
                l = 3
                pool.wait_ge(xnt_ready[before[l]], NB + 1)
                pool.memset(xe[:, :, :], 0.0).then_inc(q[l, "zeros_ready"], 1)
                pool.wait_ge(q[l, "zeros_out"], 32)
                pool.wait_ge(q[l, "index_ready"], 1)
                for i in range(NT):
                    pool.indirect_dma_start(slots_d, bass.IndirectOffsetOnAxis(ap=r_idx[:, i:i + 1], axis=0),
                                            xn[:, i, :], None).then_inc(q[l, "scattered"], 16)
                pool.wait_ge(q[l, "slots_out"], 16)
                for i in range(NT):
                    pool.indirect_dma_start(gs[:, i, :], None, slots_d,
                                            bass.IndirectOffsetOnAxis(ap=r_idx[:, i:i + 1], axis=0))\
                        .then_inc(q[l, "gathered"], 16)
                pool.wait_ge(q[l, "gathered"], 16 * NT)

            own.wait()
            own.straight()
            for l in ("pre",) + tuple(layers):
                n = (l in (1, 2)) + (l != layers[-1])
                if l == 3:
                    pool_route()
                if n:
                    with pool.Fori(0, NB) as b:
                        own.enter(b, "pool%d" % n)
                        for k in range(n):
                            serve(l, n * b + k + 1, "pool")
                        own.close("pool%d" % n)

        @block.sync
        def _(sp):
            def load_weights(l):
                base = wb if l % 2 else wa
                cut = at[f"l{l}"]["w1"][0]
                n = wide[f"l{l}"]
                src = blobs[f"l{l}"]
                sp.dma_start(base[:, 0:cut], src[:, 0:cut]).then_inc(s_w[l], 16)
                sp.dma_start(base[:, cut:n], src[:, cut:n]).then_inc(s_w[l], 16)
                if l == 2:
                    sp.dma_start(wa[:, n:n + 2 * T], blobs["rope"]).then_inc(s_w[l], 16)

            def sp_route():
                l = 3
                slots = slots_d[0:SLOTS, :].rearrange("(n p) d -> p n d", p=P)
                sp.wait_ge(q[l, "zeros_ready"], 1)
                sp.dma_start(slots, xe[:, :, :]).then_inc(q[l, "zeros_out"], 16)
                sp.wait_ge(xn_ready[before[l]], NB)
                sp.dma_start(slots_d[SLOTS:, :].rearrange("(n p) d -> p n d", p=P), xn[:, :, :])\
                  .then_inc(q[l, "zeros_out"], 16)
                sp.wait_ge(q[l, "scattered"], 16 * NT)
                sp.dma_start(xe[:, :, :], slots).then_inc(q[l, "slots_in"], 16)
                sp.wait_ge(q[l, "slots_turned"], 2 * (ST // 4))
                sp.dma_start(slots, xe[:, :, :]).then_inc(q[l, "slots_out"], 16)

            sp.dma_start(x[:, :, :], x_in_v).then_inc(s_x, 16)
            sp.dma_start(c32[:, :], blobs["c32"]).then_inc(s_c32, 16)
            if 0 in layers:
                sp.dma_start(l0["sel"], blobs["sel"].rearrange("p (s m) -> p s m", m=P)).then_inc(s_sel, 16)
            load_weights(layers[0])
            sp.dma_start(c16[:, :], blobs["c16"]).then_inc(s_c16, 16)
            if len(layers) > 1:
                load_weights(layers[1])
            for i, l in enumerate(layers):
                if i:
                    sp.wait_ge(xn_ready[l - 1], NB)
                    if i + 1 < len(layers):
                        load_weights(l + 1)
                if l == 3:
                    sp_route()
                if l in (1, 3):
                    for s, k in ((0, 0), (1, 1)) if l == 1 else ((0, 2), (1, 3), (2, 4)):
                        for par in range(2):
                            sp.dma_start(stack[s][64 * par + AROW:64 * par + AROW + 6, :, :], blobs["rows"][k, par])\
                              .then_inc(q[l, "rows_ready"], 16)
                if l == 3:
                    sp.dma_start(slope, blobs["slope"]).then_inc(q[l, "rows_ready"], 16)
                if l == 0 and l != layers[-1]:
                    continue
                with sp.Fori(0, NB) as b:
                    if l:
                        order = (0, 2, 1, 3) if l == 2 else (0, 1)
                        reads = 0
                        for n, k in enumerate(order):
                            sp.wait_ge(q[l, "parts_ready"], start[l, "parts_ready"] + len(order) * b + n + 1)
                            for j, pn in enumerate(KPARTS if k % 2 else QPARTS):
                                sp.dma_start(parts_d[k, :, j], part[k][:, pn, :]).then_inc(q[l, "parts_out"], 16)
                            sp.wait_ge(q[l, "parts_out"], start[l, "parts_out"] + 16 * NG * (len(order) * b + n + 1))
                            for s in ((1, 2) if (l == 3 and k == 1) else (k,)):
                                for par in range(2):
                                    sp.dma_start(stack[s][64 * par:64 * par + KROWS, :, :],
                                                 parts_d[k, par::2].rearrange("p j d t -> (j d) p t"))\
                                      .then_inc(q[l, "stacks_ready"], 16)
                                    reads += 1
                        assert reads == 2 * NSTK[l]
                        sp.wait_ge(q[l, "stacks_ready"], start[l, "stacks_ready"] + 16 * 2 * NSTK[l] * (b + 1))
                        wait_done(sp, 2)
                        if l != 2:
                            sp.wait_ge(q[l, "max_parts"], start[l, "max_parts"] + b + 1)
                            sp.dma_start(max_d.rearrange("k a s t -> (a s) k t"), nm[:, :, :])\
                              .then_inc(q[l, "max_out"], 16)
                            sp.wait_ge(q[l, "max_out"], start[l, "max_out"] + 16 * (b + 1))
                            for par in range(2):
                                sp.dma_start(stack[0][64 * par + MROW:64 * par + KALL, :, :], max_d[:, par])\
                                  .then_inc(q[l, "max_in"], 16)
                            sp.wait_ge(q[l, "max_in"], start[l, "max_in"] + 32 * (b + 1))
                        wait_done(sp, 2)
                    if l == layers[-1]:
                        sp.wait_ge(q[l, "layer_done"], b + 1)
                        sp.dma_start(out_v[:, bass.ds(b * TB, TB), :], x[:, bass.ds(b * TB, TB), :])\
                          .then_inc(s_out, 16)
            sp.wait_ge(s_out, 16 * NB)


def kernel(**inputs):
    import concourse.bacc as bacc
    from concourse.bass_utils import run_bass_kernel_spmd

    host = {n: np.ascontiguousarray(a) for n, a in inputs.items()}
    packed = layouts(host)
    packed.update(constants())
    at = {n: where for n, (where, _) in packed.items()}
    arrays = {f"in_{n}": a for n, (_, a) in packed.items()}
    arrays["in_x"] = host["L0_attn_x"]
    nc = bacc.Bacc("TRN2", target_bir_lowering=False, num_devices=1)
    aps = {n: nc.dram_tensor(n, a.shape, mybir.dt.from_np(a.dtype), kind="ExternalInput").ap()
           for n, a in arrays.items()}
    shape = host["L0_attn_x"].shape
    out = nc.dram_tensor("out_x", shape, F32, kind="ExternalOutput").ap()
    program(nc, aps["in_x"], {n[3:]: v for n, v in aps.items() if n != "in_x"}, at, out)
    r = run_bass_kernel_spmd(nc, [arrays], core_ids=[0])
    return r.results[0]["out_x"]
```

```python
from contextlib import ExitStack

import numpy as np

import concourse.bass as bass
from concourse import mybir

F32 = mybir.dt.float32
BF16 = mybir.dt.bfloat16
I32 = mybir.dt.int32
U32 = mybir.dt.uint32
ALU = mybir.AluOpType
ACT = mybir.ActivationFunctionType
AX = mybir.AxisListType

P = 128
NB = 4
T = 512
TB = T // P
NT = NB * TB
D = 128
INNER = 256
NST = 16
KC = 4
NH = 16
DH = D // NH
QUADS = NH // 4
EPS = 1e-5
E0, FF0 = 8, 512
E1, FF1 = 4, 704
E2, FF2 = 8, 64
E3, FF3 = 16, 256
CAP = 160
SLOTS = E3 * CAP
ST = SLOTS // P
NEG = -1e30
VW = DH + 1
SLOPE_AT = 2 * ST * P + NT * P

QPARTS = (0, 0, 1, 1, 0, 2)
KPARTS = (0, 1, 0, 1, 2, 0)
NG = len(QPARTS)
KROWS = NG * DH
AROW = KROWS
MROW = KROWS + 4
KALL = MROW + 2


def blob(pieces):
    at, cols, out = {}, 0, []
    for name, a in pieces:
        a = np.asarray(a)
        a = a.reshape(a.shape[0], -1)
        if a.shape[0] < P:
            a = np.concatenate([a, np.zeros((P - a.shape[0], a.shape[1]), a.dtype)])
        at[name] = (cols, a.shape[1])
        cols += a.shape[1]
        out.append(a)
    return at, np.ascontiguousarray(np.concatenate(out, axis=1))


def rows(v):
    return np.repeat(np.asarray(v).reshape(1, -1), P, axis=0)


def chunks1():
    full = FF1 // P
    out = []
    for e in range(0, E1, 2):
        out += [[(e, c * P, 0, P)] for c in range(full)]
        out += [[(e, full * P, 0, FF1 - full * P), (e + 1, full * P, FF1 - full * P, FF1 - full * P)]]
        out += [[(e + 1, c * P, 0, P)] for c in range(full)]
    return out


CH1 = chunks1()


def up1(w):
    return np.concatenate([np.concatenate([w[e][:, o:o + n] for e, o, _, n in ch], axis=1) for ch in CH1], axis=1)


def down1(w):
    return np.concatenate([np.concatenate([w[e][o:o + n] for e, o, _, n in ch], axis=0) for ch in CH1], axis=1)


def layouts(a):
    t = np.transpose
    d = {}
    d["l0"] = blob([
        ("in_w", t(a["L0_attn_in_proj_w"])), ("in_b", t(a["L0_attn_in_proj_b"].reshape(4, P))),
        ("conv_w", t(a["L0_attn_conv_w"].reshape(2, P, KC), (1, 0, 2))),
        ("conv_b", t(a["L0_attn_conv_b"].reshape(2, P))),
        ("dt_w", t(t(a["L0_attn_dt_w"]).reshape(2, P, INNER), (1, 0, 2))),
        ("dt_b", t(a["L0_attn_dt_b"].reshape(2, P))),
        ("a_log", t(a["L0_attn_A_log"].reshape(2, P, NST), (1, 0, 2))),
        ("bc_w", t(np.concatenate([t(a["L0_attn_B_w"]), t(a["L0_attn_C_w"])], axis=1).reshape(2, P, 2 * NST), (1, 0, 2))),
        ("bc_b", np.concatenate([a["L0_attn_B_b"], a["L0_attn_C_b"]]).reshape(-1, 1)),
        ("d", t(a["L0_attn_D"].reshape(2, P))),
        ("out_w", t(t(a["L0_attn_out_w"]).reshape(2, P, D), (1, 0, 2))), ("out_b", rows(a["L0_attn_out_b"])),
        ("gate_w", a["L0_ffn_gate_w"]), ("gate_b", rows(a["L0_ffn_gate_b"])),
        ("b1", t(a["L0_ffn_b1"].reshape(E0 * 4, P))), ("b2", a["L0_ffn_b2"]),
        ("w1", t(a["L0_ffn_w1"], (1, 0, 2))),
        ("w2", t(a["L0_ffn_w2"].reshape(E0 * 4, P, D), (1, 0, 2))),
    ])
    q = a["L1_attn_w_qkv"]
    d["l1"] = blob([
        ("wq", q[:, :D]), ("wk", q[:, D:2 * D]), ("wv", q[:, 2 * D:]),
        ("wp", a["L1_attn_w_proj"]), ("bp", rows(a["L1_attn_b_proj"])),
        ("gamma", rows(a["L1_attn_ln_gamma"])), ("beta", rows(a["L1_attn_ln_beta"])),
        ("gate_w", t(a["L1_ffn_gate_w"])[:, :E1]),
        ("w1", up1(a["L1_ffn_w1"])), ("w3", up1(a["L1_ffn_w3"])), ("w2", down1(a["L1_ffn_w2"])),
    ])
    wi = t(a["L2_attn_w_in"])
    swap = np.arange(D) ^ 1
    d["l2"] = blob([
        ("wq", wi[:, :D]), ("wqs", wi[:, :D][:, swap]), ("wk", wi[:, D:2 * D]), ("wks", wi[:, D:2 * D][:, swap]),
        ("wv", wi[:, 2 * D:]), ("wp", t(a["L2_attn_w_out"])),
        ("gamma", rows(a["L2_attn_ln_gamma"])), ("beta", rows(a["L2_attn_ln_beta"])),
        ("gate_w", a["L2_ffn_gate_w"]), ("b1", t(a["L2_ffn_b1"].reshape(4, P))), ("b2", a["L2_ffn_b2"]),
        ("w1", t(a["L2_ffn_w1"], (1, 0, 2))),
        ("w2", t(a["L2_ffn_w2"].reshape(4, P, D), (1, 0, 2))),
    ])
    qw = t(a["L3_attn_qkv_w"]).reshape(D, NH, 3, DH)
    qb = a["L3_attn_qkv_b"].reshape(NH, 3, DH)
    d["l3"] = blob([
        ("wq", qw[:, :, 0].reshape(D, D)), ("wk", qw[:, :, 1].reshape(D, D)), ("wv", qw[:, :, 2].reshape(D, D)),
        ("bq", qb[:, 0].reshape(D, 1)), ("bk", qb[:, 1].reshape(D, 1)), ("bv", rows(qb[:, 2])),
        ("wp", t(a["L3_attn_out_w"])), ("bp", rows(a["L3_attn_out_b"])),
        ("gate_w", a["L3_ffn_Wg"]), ("b1", t(a["L3_ffn_b1"].reshape(E3 * 2, P))), ("b2", t(a["L3_ffn_b2"])),
        ("w1", t(a["L3_ffn_W1"], (1, 0, 2))),
        ("w2", t(a["L3_ffn_W2"].reshape(E3 * 2, P, D), (1, 0, 2))),
    ])
    return d


def constants():
    f, bf = np.float32, mybir.dt.np(BF16)
    i = np.arange(P)
    eye = np.eye(P, dtype=f)
    k = np.arange(1, DH // 2 + 1, dtype=f)
    thetas = np.repeat(np.power(f(1000.0), (f(-2.0) * k / f(DH))).astype(f), 2)
    args = (np.arange(1, T + 1, dtype=f)[:, None] * thetas[None, :]).astype(f)
    sign = np.where(np.arange(DH) % 2 == 0, f(-1), f(1))
    cos = np.tile(np.cos(args).astype(f).T, (NH, 1))
    sin = np.tile((np.sin(args).astype(f) * sign).T, (NH, 1))
    c32 = blob([
        ("eye", eye), ("iota", rows(np.arange(16, dtype=f))),
        ("drop", (SLOTS + i[:, None] + P * np.arange(NT)[None, :]).astype(f)),
        ("lower", (i[None, :] < i[:, None]).astype(f)),
    ])
    after = (i[None, :] > i[:, None]).astype(f)
    back = -2.0 * np.maximum(i[None, :] - i[:, None], 0)
    slope = 0.5 ** np.arange(NH)
    sel = np.zeros((P, 2 * NST, P), f)
    for s in range(2 * NST):
        sel[[s, 2 * NST + s, 4 * NST + s], s] = 1
    c16 = blob([
        ("eye", eye), ("mask_a", NEG * after), ("mask_b", NEG * after.T),
        ("back_a", back), ("back_b", back.T),
    ])
    slopes = (slope[None, :, None] * eye[:, None, :]).reshape(P, -1).astype(bf)
    c16 = (c16[0], c16[1].astype(bf))
    sel = sel.reshape(P, -1).astype(bf)
    pos = np.arange(T)
    ph, pl = (pos // 16) * 16, pos % 16
    r = np.zeros((5, 2, 6, NH // 2, T), f)
    for h in range(NH):
        par, s = h % 2, h // 2
        m = slope[h]
        r[0, par, :, s] = 0
        r[1, par, 4:, s] = 1
        r[2, par, 0:2, s] = 1
        r[2, par, 2, s], r[2, par, 3, s] = -m * ph, -m * pl
        r[3, par, 0, s], r[3, par, 1, s], r[3, par, 2:, s] = m * ph, m * pl, 1
        r[4, par, 0, s], r[4, par, 1, s], r[4, par, 2:4, s] = -m * ph, -m * pl, -1
        r[4, par, 4:, s] = 1
    rope = blob([("cos", cos), ("sin", sin)])
    return {"rope": rope, "c32": c32, "c16": c16, "slope": (None, slopes), "sel": (None, sel), "rows": (None, r.astype(bf))}


def by_parity(hs):
    return [h for h in hs if h % 2 == 0] + [h for h in hs if h % 2]


def score_units(kind):
    units_a, units_b, stages = [], [], []
    for g in range(QUADS):
        hs = range(4 * g, 4 * g + 4)
        if kind == "causal":
            for n, h in enumerate(hs):
                units_a.append([(h, 3, 0, 512), (h, 2, 512, 384), (h, 0, 896, 128)])
                units_b.append((len(stages), n, [(h, 0, 0, 512), (h, 1, 512, 384), (h, 3, 896, 128)]))
            stages.append((g, "x", len(units_b), 3))
            units_a.append([(h, 1, 256 * n, 256) for n, h in enumerate(by_parity(hs))])
            units_b.append((len(stages), 0, [(h, 2, 256 * n, 256) for n, h in enumerate(by_parity(hs))]))
            stages.append((g, "y", len(units_b), 1))
        else:
            sums = [[(h, 2 * jp, 0, 512), (h, 2 * jp + 1, 512, 512)] for h in hs for jp in range(2)]
            if kind == "rope" and g == 0:
                units_b += [(None, 0, unit) for unit in sums]
            for cp in range(2):
                for n, h in enumerate(hs):
                    unit = [(h, 2 * cp, 0, 512), (h, 2 * cp + 1, 512, 512)]
                    units_a.append(unit)
                    if kind == "rope" and g:
                        units_b.append((None, 0, sums[4 * cp + n]))
                    units_b.append((len(stages), n, unit))
                stages.append((g, cp, len(units_b), 2))
    return units_a, units_b, stages


def b_items(kind, lag=2):
    _, units, stages = score_units(kind)
    out, waiting, u = [], [], 0
    while u < len(units) or waiting:
        if u < len(units):
            out.append(("b", u))
        u += 1
        for s, (g, _, end, parts) in enumerate(stages):
            if end == u:
                waiting += [(u + lag, ("pv", (s, k, k == parts - 1))) for k in range(parts)]
                if s + 1 == len(stages) or stages[s + 1][0] != g:
                    waiting.append((u + lag + 2, ("bc", g)))
        if waiting and (waiting[0][0] <= u or u > len(units)):
            out.append(waiting.pop(0)[1])
    return out


def spread(main, extra):
    out, done = [], 0
    for n, item in enumerate(main):
        out.append(item)
        want = (n + 1) * len(extra) // len(main)
        out += extra[done:want]
        done = want
    return out


class Links:

    def __init__(self, eng, sem):
        self.eng, self.sem, self.done, self.n, self.base = eng, sem, 0, 0, 0

    def enter(self, b, key):
        self.base, self.n = self.done + b * LINKS[key], 0

    def close(self, key, turns=NB):
        assert self.n == LINKS[key], (key, self.n)
        self.done += self.n * turns
        self.base, self.n = self.done, 0

    def straight(self):
        self.done += self.n
        self.base, self.n = self.done, 0

    def add(self, ins):
        ins.then_inc(self.sem, 1)
        self.n += 1
        return ins

    def wait(self, n=None):
        self.eng.wait_ge(self.sem, self.base + (self.n if n is None else n))

    def link(self, ins):
        self.add(ins)
        self.wait()


KIND = {1: "causal", 2: "rope", 3: "alibi"}
NF = {0: E0 * 4, 1: len(CH1), 2: E2 * FF2 // P}
OPERANDS = {1: ("q", "k"), 2: ("q", "k", "qr", "kr"), 3: ("q", "k")}
LINKS = {0: 74, 1: 71, 2: 60, 3: 13, "act0": 5, "pool0": 0, "pool1": 1, "pool2": 2}


def down_groups(l):
    if l == 0:
        return [[(f // 4, 0, P, f, f % 4 == 0, f % 4 == 3)] for f in range(NF[0])]
    if l == 2:
        return [[(2 * f, 0, FF2, f, True, True), (2 * f + 1, FF2, FF2, f, True, True)] for f in range(NF[2])]
    full, out = FF1 // P, []
    half = FF1 - full * P
    for pair in range(E1 // 2):
        at = pair * (2 * full + 1)
        out += [[(2 * pair, 0, P, at + c, c == 0, False)] for c in range(full)]
        out += [[(2 * pair, 0, half, at + full, False, True)]]
        out += [[(2 * pair + 1, 0, P, at + full + 1 + c, c == 0, False)] for c in range(full - 1)]
        out += [[(2 * pair + 1, 0, P, at + 2 * full, False, False),
                 (2 * pair + 1, half, half, at + full, False, True)]]
    return out


AHEAD = (3, 6)
LAG = {0: 3, 1: 1, 2: 1}


def schedule(l):
    f = [("f", n) for n in range(NF.get(l, 0))]
    if l == 0:
        out, done = [], AHEAD[1]
        for s in range(NST):
            out.append(("s", s))
            want = AHEAD[1] + (NF[0] - AHEAD[1]) * (s + 1) // NST
            out += f[done:want]
            done = want
        return out + [("fl", 0)]
    a = [("a", u) for u in range(len(score_units(KIND[l])[0]))]
    b = b_items(KIND[l])
    if l == 1:
        return f[:2] + spread(a, f[2:13]) + [("mx", 0)] + f[13:15] + spread(b, f[15:]) + [("fl", 0)]
    if l == 2:
        return b[:4] + f[:1] + spread(b[4:-16], f[1:]) + [("fl", 0)] + b[-16:]
    return a + [("mx", 0)] + b


def program(nc, x_in, blobs, at, out, layers=(0, 1, 2, 3)):
    ctx = ExitStack()
    with ctx:
        def sb(name, shape, dt=F32):
            return ctx.enter_context(nc.sbuf_tensor(name, shape, dt))

        def sem(name):
            return ctx.enter_context(nc.semaphore(name))

        wide = {n: blobs[n].shape[1] for n in blobs if n != "rows"}
        wa = sb("weights_even", [P, max(wide["l0"], wide["l2"] + 2 * T, SLOPE_AT + NH * P // 2)])
        wb = sb("weights_odd", [P, max(wide["l1"], wide["l3"])])
        c32 = sb("consts", [P, wide["c32"]])
        c16 = sb("consts16", [P, wide["c16"]], BF16)
        x = sb("x", [P, NT, D])
        xn = sb("xn", [P, NT, D])
        xnt = sb("xnt", [P, NT * P])
        xb = sb("xnt_sequence", [P, T])
        scratch = sb("scratch", [P, 17408])
        facc = sb("mixture_sum", [P, TB, D])
        sa = sb("branch", [P, TB, D])
        xs = sa
        hid = sb("hidden", [P, 2, T])
        hidh = sb("hidden_shared", [P, T])
        act_t = sb("tanh", [P, T])
        act_g = sb("gated", [P, T])
        stat = sb("stat", [P, TB, 6])
        mv = sb("mean_var", [P, TB, 2])
        rstd = sb("rstd", [P, TB])
        vare = sb("variance_eps", [P, TB])
        half = sb("minus_half", [P, TB])
        stat0 = hid[:, 0, 0:6 * NT].rearrange("p (i k) -> p i k", k=6)
        mv0 = hid[:, 0, 6 * NT:8 * NT].rearrange("p (i k) -> p i k", k=2)
        vare0, rstd0 = hid[:, 0, 8 * NT:9 * NT], hid[:, 0, 9 * NT:10 * NT]
        lg = sb("logits", [P, TB, 16])
        m8 = sb("top_values", [P, TB, 8])
        i8 = sb("top_index", [P, TB, 8], U32)
        fi = sb("top_index_f", [P, TB, 8])
        gd = sb("gate_small", [P, 6, TB])
        cw = sb("combine", [P, TB, 16])
        cw2 = sb("combine_second", [P, TB, 16])
        cwt = sb("combine_t", [16, T])
        small = sb("small_l0", [P, 64])
        ps = ctx.enter_context(nc.psum_tensor("ps", [P, 8, 512], F32))
        PV, UP, YB, MI = 4, 5, 6, 7

        def W(l, name, shape=None):
            base = {0: wa, 2: wa, 1: wb, 3: wb, "c32": c32, "c16": c16}[l]
            a, n = at[{0: "l0", 1: "l1", 2: "l2", 3: "l3"}.get(l, l)][name]
            return base[:, a:a + n]

        eye, iota = W("c32", "eye"), W("c32", "iota")
        eyeb = W("c16", "eye")
        rope = [wa[:, wide["l2"] + T * n:wide["l2"] + T * (n + 1)] for n in range(2)]
        slope = wa[:, SLOPE_AT:SLOPE_AT + NH * P // 2].bitcast(BF16)

        stack = [scratch[:, 2048 * n:2048 * (n + 1)].bitcast(BF16).rearrange("p (s t) -> p s t", t=T)
                 for n in range(4)]
        pt = [scratch[:, 8192 + 4096 * n:8192 + 4096 * (n + 1)].rearrange("p (i c) -> p i c", i=4) for n in range(2)]
        pty = scratch[:, 16384:17408].rearrange("p (i c) -> p i c", i=4)
        vf = [scratch[:, 8192 + 512 * n:8192 + 512 * (n + 1)] for n in range(4)]
        part = [scratch[:, 10240 + 768 * n:10240 + 768 * (n + 1)].bitcast(BF16).rearrange("p (k t) -> p k t", t=T)
                for n in range(4)]
        nm = scratch[0:16, 13312:13824].bitcast(BF16).rearrange("p (k t) -> p k t", t=T)
        vx = sb("values", [P, TB, NH * VW + 32])
        ot = sb("head_out", [P, T])
        rcp = sb("reciprocals", [P, TB, 4])
        dens = sb("denominators", [P, TB, NH])
        on = sb("heads_out", [P, TB, D])
        mx = sb("neg_max", [P, TB, NH])
        o = 0

        def take(n):
            nonlocal o
            o += n
            return scratch[:, o - n:o]

        l0 = {"xp": take(2 * (T + KC - 1)).rearrange("p (g t) -> p g t", g=2)}
        for n in ("xc", "xconv", "dt", "dtx", "zs", "y", "da0", "da1", "ub", "hs", "hc", "tmp"):
            l0[n] = take(2 * T).rearrange("p (g t) -> p g t", g=2)
        l0["bcf"] = take(T)
        l0["bcm"] = take(T // 2).bitcast(BF16)
        l0["bcs"] = take(T // 2).bitcast(BF16)
        l0["sel"] = take(2 * NST * P // 2).bitcast(BF16).rearrange("p (s m) -> p s m", m=P)
        assert o <= 17408, o

        parts_d = nc.dram_tensor("parts_scratch", [4, NH, NG, DH, T], BF16, kind="Internal").ap()
        max_d = nc.dram_tensor("max_scratch", [2, 2, NH // 2, T], BF16, kind="Internal").ap()
        slots_d = nc.dram_tensor("slots_scratch", [SLOTS + NT * P, D], F32, kind="Internal").ap()

        xe = wa[:, 0:SLOTS].rearrange("p (n d) -> p n d", d=P)
        xet = wa[:, SLOTS:2 * SLOTS]
        gs = wa[:, 2 * SLOTS:2 * SLOTS + NT * P].rearrange("p (n d) -> p n d", d=P)
        PART = 32
        ro = 0

        def route(*shape, rows_=P, dt=F32):
            nonlocal ro
            n = int(np.prod(shape)) * (2 if dt == BF16 else 4) // 4
            v = scratch[0:rows_, ro:ro + n]
            ro += n
            v = v if dt == F32 else v.bitcast(dt)
            return v if len(shape) == 1 else v.rearrange("p (a b) -> p a b", b=shape[1])

        r_parts = route(NT, 3 * PART)
        r_hot = route(NT, 3 * PART)
        r_partst = route(NT * P, rows_=3 * PART, dt=BF16)
        r_hott = route(NT * P, rows_=3 * PART, dt=BF16)
        r_lg, r_w, r_hot1 = route(NT, E3), route(NT, E3), route(NT, E3)
        r_b16 = route(2, NT * E3, dt=BF16)
        r_m8, r_fi = route(NT, 8), route(NT, 8)
        r_i8 = route(NT, 8, dt=U32)
        r_junk = route((NT + 1) * P, dt=BF16)
        r_v = route(9, NT)
        r_idx = route(NT, dt=I32)

        x_in_v = x_in.rearrange("b (n p) d -> p (b n) d", p=P)
        out_v = out.rearrange("b (n p) d -> p (b n) d", p=P)

        s_x, s_c32, s_c16 = sem("x_in"), sem("consts_in"), sem("consts16_in")
        s_w = [sem(f"weights_in{l}") for l in range(4)]
        s_sel = sem("selectors_in")
        s_out = sem("out_written")
        dl = sem("vector_own")
        pl = sem("pool_own")
        alone = [sem("waits_alone_vector"), sem("waits_alone_pool"), sem("waits_alone_sync")]

        def wait_done(eng, n):
            eng.sem_inc(alone[n], 1)

        dn_set = sem("vector_constants_ready")
        first = layers[0]
        var_ready = {n: sem(f"variance_ready_{n}") for n in ("pre",) + tuple(layers)}
        rstd_ready = {n: sem(f"rstd_ready_{n}") for n in ("pre",) + tuple(layers)}
        xn_ready = {n: sem(f"xn_ready_{n}") for n in ("pre",) + tuple(layers)}
        xn_turned = {n: sem(f"xn_turned_{n}") for n in ("pre",) + tuple(layers)}
        xnt_ready = {n: sem(f"xnt_ready_{n}") for n in ("pre",) + tuple(layers)}
        before = {l: ("pre" if l == first else l - 1) for l in layers}
        units = {l: score_units(KIND[l]) for l in layers if l}
        NUA = {l: len(units[l][0]) for l in units}
        NUB = {l: len(units[l][1]) for l in units}
        NS = {l: len(units[l][2]) for l in units}
        DG = {l: down_groups(l) for l in (0, 1, 2)}
        NE = {0: E0, 1: E1, 2: E2}
        KA = {1: KROWS, 3: MROW}
        NY = {l: sum(len(g) for g in DG[l]) for l in DG}
        NPROJ = {0: 5, 1: 4, 2: 6, 3: 3}
        NSTK = {1: 2, 2: 2, 3: 3}
        NROWS = {1: 4, 3: 7}
        EV = {1: 2, 2: 4, 3: 2}
        mixed, with_bias, with_heads, with_max = (0, 1, 2), (0, 2), (1, 2, 3), (1, 3)
        per_turn = {}
        for names, counts in (
                ("xb_ready tail_done attn_ready fgate_ready", {l: 1 for l in range(4)}),
                ("gate_diff gate_exp gate_seen cw_ready", {l: 1 for l in mixed}),
                ("cwt_turned cwt_ready bias_ready bias_seen", {l: 1 for l in with_bias}),
                ("proj_ready", NPROJ), ("evac_done", EV), ("up_ready hidden_ready", NF), ("y_ready", NY),
                ("y_free", NE), ("values_ready", {l: 1 for l in with_heads}),
                ("parts_ready", {l: len(OPERANDS[l]) for l in with_heads}),
                ("parts0_out parts1_out", {l: 16 * NG for l in with_heads}),
                ("parts2_out parts3_out", {2: 16 * NG}),
                ("stacks_ready", {l: 16 * 2 * NSTK[l] for l in with_heads}),
                ("a_ready a_free", {l: NUA.get(l, 0) for l in with_max}),
                ("max_turned max_parts", {l: 1 for l in with_max}),
                ("max_out", {l: 16 for l in with_max}), ("max_in", {l: 32 for l in with_max}),
                ("b_ready exp_done", NUB), ("pv_done", NS),
                ("head_copied den_ready pv_free", {l: QUADS for l in with_heads}),
                ("heads_turned heads_ready", {l: 1 for l in with_heads})):
            for name in names.split():
                per_turn[name] = counts

        class Signals(dict):

            def __missing__(self, key):
                l, name = key
                if name in per_turn:
                    if name not in self:
                        self[name] = sem(name)
                    return self[name]
                self[key] = sem("l%d_%s" % key)
                return self[key]

        q = Signals()
        start = {(l, name): NB * sum(counts.get(m, 0) for m in layers[:i])
              for i, l in enumerate(layers) for name, counts in per_turn.items()}
        block = ctx.enter_context(nc.Block())

        def upto(l, f):
            return sum(len(g) for g in DG[l][:f + 1])

        def up_bank(l, f):
            return (UP, PV, MI)[f % 3] if l == 0 else UP

        def hidden_buffer(l, f):
            if l == 0 and f % 3 == 2 or l == 1 and len(CH1[f]) == 2:
                return hidh[:, :]
            return hid[:, f % (3 if l == 0 else 2), :]

        def span(b, n=T):
            return bass.ds(b * n, n)

        def head(h):
            return 64 * (h % 2), h // 2

        @block.tensor
        def _(pe):
            def turn_xn(l, b):
                pe.wait_ge(xnt_ready[l], b + 1)
                pe.wait_ge(xn_ready[l], b + 1)
                for j in range(TB):
                    mm = pe.transpose(ps[:, MI, P * j:P * (j + 1)], xs[:, j, :], eye)
                mm.then_inc(xn_turned[l], 1)

            def gate(l, bank, b, ready):
                n = {0: E0, 1: E1, 2: E2}[l]
                for j in range(TB):
                    mm = pe.matmul(ps[:, bank, 16 * j:16 * j + n], xb[:, P * j:P * (j + 1)], W(l, "gate_w"),
                                   start=(j == 0), stop=True, skip_group_check=True)
                mm.then_inc(ready, 1)

            def mixture_bias(l, b):
                n = NE[l]
                pe.wait_ge(q[l, "cw_ready"], start[l, "cw_ready"] + b + 1)
                for j in range(TB):
                    mm = pe.transpose(ps[0:n, MI, P * j:P * (j + 1)], cw[:, j, 0:n], eye)
                mm.then_inc(q[l, "cwt_turned"], 1)
                pe.wait_ge(q[l, "cwt_ready"], start[l, "cwt_ready"] + b + 1)
                for j in range(TB):
                    mm = pe.matmul(ps[:, MI, P * j:P * (j + 1)], cwt[0:n, P * j:P * (j + 1)], W(l, "b2")[0:n, :],
                                   start=(j == 0), stop=True, skip_group_check=True)
                mm.then_inc(q[l, "bias_ready"], 1)

            def up(l, b, f):
                if l:
                    pe.wait_ge(q[l, "hidden_ready"], start[l, "hidden_ready"] + b * NF[l] + f + 1)
                elif f >= LAG[0]:
                    pe.wait_ge(q[l, "hidden_ready"], start[l, "hidden_ready"] + b * NF[l] + f - LAG[0] + 2)
                    if f == 5:
                        pe.wait_ge(q[l, "bias_seen"], start[l, "bias_seen"] + b + 1)
                w1 = W(l, "w1")[:, P * f:P * (f + 1)]
                if l == 1:
                    pe.matmul(ps[:, MI, :], W(l, "w3")[:, P * f:P * (f + 1)], xb[:, :], start=True, stop=True)
                pe.matmul(ps[:, up_bank(l, f), :], w1, xb[:, :], start=True, stop=True)\
                  .then_inc(q[l, "up_ready"], 1)

            def down(l, b, f):
                pe.wait_ge(q[l, "hidden_ready"], start[l, "hidden_ready"] + b * NF[l] + f + 2)
                if f == 0:
                    pe.wait_ge(q[l, "gate_seen"], start[l, "gate_seen"] + b + 1)
                for e, lo, n, src, one, last in DG[l][f]:
                    if one:
                        pe.wait_ge(q[l, "y_free"], start[l, "y_free"] + b * NE[l] + e + 1)
                    buf = hidden_buffer(l, src)
                    for j in range(TB):
                        mm = pe.matmul(ps[:, YB, P * j:P * (j + 1)], buf[lo:lo + n, P * j:P * (j + 1)],
                                       W(l, "w2")[lo:lo + n, P * src:P * (src + 1)],
                                       start=(one and j == 0), stop=True, skip_group_check=True)
                    mm.then_inc(q[l, "y_ready"], 1)

            def layer0():
                l = 0
                pe.wait_ge(s_w[0], 32)
                pe.wait_ge(s_sel, 16)
                pe.wait_ge(xnt_ready[before[l]], NB + 1)
                with pe.Fori(0, NB) as b:
                    def ffn(n):
                        up(l, b, n)
                        if n >= LAG[l]:
                            down(l, b, n - LAG[l])

                    pe.wait_ge(q[l, "xb_ready"], start[l, "xb_ready"] + b + 1)
                    pe.wait_ge(q[l, "tail_done"], start[l, "tail_done"] + b + 1)
                    if l != layers[-1]:
                        pe.wait_ge(xnt_ready[l], b + 1)
                    for c in range(4):
                        pe.matmul(ps[:, c, :], W(l, "in_w")[:, P * c:P * (c + 1)], xb[:, :],
                                  start=True, stop=True).then_inc(q[l, "proj_ready"], 1)
                    gate(l, YB, b, q[l, "proj_ready"])
                    for n in range(AHEAD[0]):
                        ffn(n)
                    pe.wait_ge(q[l, "hidden_ready"], start[l, "hidden_ready"] + b * NF[l] + 4)
                    mixture_bias(l, b)
                    pe.wait_ge(q[l, "xconv_ready"], 2 * b + 2)
                    pe.wait_ge(q[l, "xp_ready"], 2 * b + 2)
                    pe.wait_ge(q[l, "zbias_ready"], 2 * b + 2)
                    for g in range(2):
                        for k in range(2):
                            mm = pe.matmul(ps[:, g, :], W(l, "dt_w")[:, INNER * k + P * g:INNER * k + P * (g + 1)],
                                           l0["xconv"][:, k, :], start=(k == 0), stop=(k == 1))
                        mm.then_inc(q[l, "dtbc_ready"], 1)
                    for k in range(2):
                        mm = pe.matmul(ps[0:2 * NST, 2, :], W(l, "bc_w")[:, 2 * NST * k:2 * NST * (k + 1)],
                                       l0["xconv"][:, k, :], start=(k == 0), stop=(k == 1))
                    mm.then_inc(q[l, "dtbc_ready"], 1)
                    for n in range(*AHEAD):
                        ffn(n)
                    pe.wait_ge(q[l, "dt_ready"], b + 1)
                    pe.wait_ge(q[l, "bcs_ready"], b + 1)

                    def state_rows(s):
                        pe.wait_ge(q[l, "hc_ready"], 2 * NST * b + 2 * s + 2)
                        for n in range(2):
                            mm = pe.matmul(ps[:, 2 * (s % 2) + n, :], l0["sel"][0:6 * NST, s + NST * n, :],
                                           l0["bcs"][0:6 * NST, :], start=True, stop=True)
                        mm.then_inc(q[l, "bc_rows"], 1)

                    state_rows(0)
                    for kind, n in schedule(l):
                        if kind == "s":
                            if n + 1 < NST:
                                state_rows(n + 1)
                        elif kind == "f":
                            ffn(n)
                        else:
                            for f in range(NF[l] - LAG[l], NF[l]):
                                down(l, b, f)
                    pe.wait_ge(q[l, "yg_ready"], b + 1)
                    for j in range(TB):
                        for k in range(2):
                            mm = pe.matmul(ps[:, PV, P * j:P * (j + 1)], l0["y"][:, k, P * j:P * (j + 1)],
                                           W(l, "out_w")[:, D * k:D * (k + 1)],
                                           start=(j == 0 and k == 0), stop=True, skip_group_check=True)
                    mm.then_inc(q[l, "attn_ready"], 1)
                    if l != layers[-1]:
                        turn_xn(l, b)

            def pe_route():
                l = 3
                pe.wait_ge(s_w[l], 32)
                pe.wait_ge(xnt_ready[before[l]], NB + 1)
                for i in range(NT):
                    mm = pe.matmul(ps[:, YB, E3 * i:E3 * (i + 1)], xnt[:, P * i:P * (i + 1)], W(l, "gate_w"),
                                   start=(i == 0), stop=True, skip_group_check=True)
                mm.then_inc(q[l, "logits_ready"], 1)
                pe.wait_ge(q[l, "stack_built"], 1)
                for k, src in enumerate((r_parts, r_hot)):
                    for i in range(NT):
                        mm = pe.transpose(ps[0:3 * PART, 4 * k + i // 4, P * (i % 4):P * (i % 4 + 1)], src[:, i, :],
                                          eye)
                    mm.then_inc(q[l, "stack_turned"], 1)
                pe.wait_ge(q[l, "stack_parts"], 1)
                pe.wait_ge(q[l, "stack_hot"], 1)
                for i in range(NT):
                    if i >= 2:
                        pe.wait_ge(q[l, "ranked"], i - 1)
                    for c in range(TB):
                        mm = pe.matmul(ps[:, 4 * (i % 2) + c, :], r_hott[:, P * i:P * (i + 1)],
                                       r_partst[:, T * c:T * (c + 1)], start=True, stop=True)
                    mm.then_inc(q[l, "row_ready"], 1)
                pe.wait_ge(q[l, "slots_in"], 16)
                for n in range(ST // 4):
                    if n == 4:
                        pe.wait_ge(q[l, "slots_turned"], 1)
                    for k in range(4):
                        mm = pe.transpose(ps[:, n % 4, P * k:P * (k + 1)], xe[:, 4 * n + k, :], eye)
                    mm.then_inc(q[l, "slots_turning"], 1)
                pe.wait_ge(q[l, "slots_turned"], ST // 4)

                def expert_up(e):
                    if e >= 2:
                        pe.wait_ge(q[l, "expert_hidden"], e - 1)
                    for c in range(2):
                        mm = pe.matmul(ps[:, 4 + e % 2, CAP * c:CAP * (c + 1)],
                                       W(l, "w1")[:, FF3 * e + P * c:FF3 * e + P * (c + 1)],
                                       xet[:, CAP * e:CAP * (e + 1)], start=(c == 0), stop=True, skip_group_check=True)
                    mm.then_inc(q[l, "expert_up"], 1)

                def expert_down(e):
                    pe.wait_ge(q[l, "expert_hidden"], e + 1)
                    if e >= 2:
                        pe.wait_ge(q[l, "expert_out"], e - 1)
                    for c in range(2):
                        mm = pe.matmul(ps[:, 6 + e % 2, 0:CAP], W(l, "w2")[:, P * (2 * e + c):P * (2 * e + c + 1)],
                                       hid[:, e % 2, CAP * c:CAP * (c + 1)], start=(c == 0), stop=(c == 1))
                    mm.then_inc(q[l, "expert_down"], 1)

                for e in range(E3):
                    expert_up(e)
                    if e:
                        expert_down(e - 1)
                expert_down(E3 - 1)
                pe.wait_ge(q[l, "expert_out"], E3)
                for n in range(ST // 4):
                    if n == 4:
                        pe.wait_ge(q[l, "slots_turned"], ST // 4 + 1)
                    for k in range(4):
                        mm = pe.transpose(ps[:, n % 4, P * k:P * (k + 1)], xet[:, P * (4 * n + k):P * (4 * n + k + 1)],
                                          eye)
                    mm.then_inc(q[l, "slots_turning"], 1)
                pe.wait_ge(q[l, "slots_turned"], 2 * (ST // 4))

            def attention_layer(l):
                kind = KIND[l]
                ua, ub, st = units[l]
                pe.wait_ge(s_w[l], 48 if l == 2 else 32)
                pe.wait_ge(xnt_ready[before[l]], NB + 1)
                names = {1: ("wq", "wk"), 2: ("wq", "wk", "wqs", "wks"), 3: ("wq", "wk")}[l]

                def queries_keys(b):
                    pe.wait_ge(q[l, "xb_ready"], start[l, "xb_ready"] + b + 1)
                    pe.wait_ge(q[l, "exp_done"], start[l, "exp_done"] + b * NUB[l] + 2)
                    for c, n in enumerate(names):
                        pe.matmul(ps[:, c, :], W(l, n), xb[:, :], start=True, stop=True)\
                          .then_inc(q[l, "proj_ready"], 1)

                def values_gate(b):
                    pe.wait_ge(q[l, "tail_done"], start[l, "tail_done"] + b + 1)
                    for j in range(TB):
                        mm = pe.matmul(ps[:, PV, P * j:P * (j + 1)], xb[:, P * j:P * (j + 1)], W(l, "wv"),
                                       start=(j == 0), stop=True, skip_group_check=True)
                    mm.then_inc(q[l, "proj_ready"], 1)
                    if l != 3:
                        gate(l, YB, b, q[l, "proj_ready"])

                def heads(b):
                    if l != layers[-1]:
                        pe.wait_ge(xnt_ready[l], b + 1)

                    def scores_a(u):
                        if u == 0:
                            pe.wait_ge(q[l, "stacks_ready"], start[l, "stacks_ready"] + 16 * 2 * NSTK[l] * (b + 1))
                            if l in (1, 3):
                                pe.wait_ge(q[l, "rows_ready"], 16 * NROWS[l])
                            pe.wait_ge(q[l, "evac_done"], start[l, "evac_done"] + len(names) * (b + 1))
                        pe.wait_ge(q[l, "a_free"], start[l, "a_free"] + b * NUA[l] + u + 1)
                        base, begun = 2 * (u % 2), set()
                        for h, j, col, n in ua[u]:
                            p0, s = head(h)
                            bank, c0 = base + col // 512, col % 512
                            o_ = ps[:, bank, c0:c0 + n]
                            lhs = stack[0][p0:p0 + KA[l], s, P * j:P * (j + 1)]
                            first_ = bank not in begun
                            begun.add(bank)
                            if l == 1:
                                pe.matmul(o_, lhs, stack[1][p0:p0 + KA[l], s, 0:n], start=first_, stop=True,
                                          skip_group_check=True)
                                mm = pe.matmul(o_[:, n - P:n], eyeb, W("c16", "mask_a"), start=False, stop=True,
                                               skip_group_check=True)
                            else:
                                cut = P * (j + 1)
                                mm = pe.matmul(o_[:, 0:cut], lhs, stack[1][p0:p0 + KA[l], s, 0:cut], start=first_,
                                               stop=True, skip_group_check=True)
                                if cut < T:
                                    pe.matmul(o_[:, cut:T], lhs, stack[2][p0:p0 + KA[l], s, cut:T], start=False,
                                              stop=True, skip_group_check=True)
                                mm = pe.matmul(o_[:, cut - P:cut], slope[:, P * h:P * (h + 1)],
                                               W("c16", "back_a"), start=False, stop=True, skip_group_check=True)
                        mm.then_inc(q[l, "a_ready"], 1)

                    def turn_max():
                        pe.wait_ge(q[l, "a_free"], start[l, "a_free"] + NUA[l] * (b + 1) + 2)
                        for j in range(TB):
                            mm = pe.transpose(ps[0:NH, 0, P * j:P * (j + 1)], mx[:, j, :], eye)
                        mm.then_inc(q[l, "max_turned"], 1)

                    def scores_b(u):
                        if u == 0:
                            if l == 2:
                                pe.wait_ge(q[l, "stacks_ready"], start[l, "stacks_ready"] + 16 * 2 * NSTK[l] * (b + 1))
                                pe.wait_ge(q[l, "evac_done"], start[l, "evac_done"] + len(names) * (b + 1))
                            else:
                                pe.wait_ge(q[l, "max_in"], start[l, "max_in"] + 32 * (b + 1))
                                pe.wait_ge(q[l, "max_parts"], start[l, "max_parts"] + b + 1)
                        pe.wait_ge(q[l, "exp_done"], start[l, "exp_done"] + b * NUB[l] + u + 1)
                        base, begun = 2 * (u % 2), set()
                        stage, number, regions = ub[u]
                        plain = stage is None
                        if l == 2 and stage == 0 and number == 0:
                            pe.wait_ge(q[l, "rotated_ready"], 64 * (b + 1))
                        for h, c, col, n in regions:
                            p0, s = head(h)
                            bank, c0 = base + col // 512, col % 512
                            o_ = ps[:, bank, c0:c0 + n]
                            first_ = bank not in begun
                            begun.add(bank)
                            rows_ = KROWS if l == 2 else KALL
                            if plain:
                                mm = pe.matmul(o_, stack[0][p0:p0 + rows_, s, P * c:P * (c + 1)],
                                               stack[1][p0:p0 + rows_, s, :], start=True, stop=True)
                                continue
                            qs = stack[2 if l == 2 else 0][p0:p0 + rows_, s, :]
                            ks = stack[3 if l == 2 else 1][p0:p0 + rows_, s, P * c:P * (c + 1)]
                            if l == 1:
                                pe.matmul(o_, ks, qs[:, P * c:T], start=first_, stop=True, skip_group_check=True)
                                mm = pe.matmul(o_[:, 0:P], eyeb, W("c16", "mask_b"), start=False, stop=True,
                                               skip_group_check=True)
                            elif l == 2:
                                mm = pe.matmul(o_, ks, qs, start=True, stop=True)
                            else:
                                pe.matmul(o_[:, P * c:T], ks, qs[:, P * c:T], start=True, stop=True,
                                          skip_group_check=True)
                                if c:
                                    kn = stack[2][p0:p0 + rows_, s, P * c:P * (c + 1)]
                                    pe.matmul(o_[:, 0:P * c], kn, qs[:, 0:P * c], start=False, stop=True,
                                              skip_group_check=True)
                                mm = pe.matmul(o_[:, P * c:P * (c + 1)], slope[:, P * h:P * (h + 1)],
                                               W("c16", "back_b"), start=False, stop=True, skip_group_check=True)
                        mm.then_inc(q[l, "b_ready"], 1)

                    def values(s, part):
                        g, what, end, parts = st[s]
                        first_ = part == 0 and (s == 0 or st[s - 1][0] != g)
                        if part == 0:
                            pe.wait_ge(q[l, "exp_done"], start[l, "exp_done"] + b * NUB[l] + end + 2)
                        if first_:
                            pe.wait_ge(q[l, "pv_free"], start[l, "pv_free"] + b * QUADS + g + 1)
                            if s == 0:
                                pe.wait_ge(q[l, "values_ready"], start[l, "values_ready"] + b + 1)
                        if what == "x":
                            regions = [(0, 0, 0, 512, pt[g % 2]), (1, 128, 512, 384, pt[g % 2]), (3, 384, 896, 128, pt[g % 2])]
                        elif what == "y":
                            regions = [(2, 256, 0, 256, pty)]
                        else:
                            regions = [(2 * what + n, 0, 512 * n, 512, pt[s % 2]) for n in range(2)]
                        for c, q0, col, n, buf in regions[part:part + 1]:
                            for i in range(4):
                                h = 4 * g + i
                                lhs = vx[:, c, VW * h:VW * h + 32]
                                slot = by_parity(range(4)).index(i) if what == "y" else i
                                mm = pe.matmul(ps[32 * i:32 * i + 32, PV, q0:q0 + n], lhs, buf[:, slot, col:col + n],
                                               start=first_, stop=True, skip_group_check=True)
                        if part == parts - 1:
                            mm.then_inc(q[l, "pv_done"], 1)

                    def denominators(g):
                        pe.wait_ge(q[l, "head_copied"], start[l, "head_copied"] + b * QUADS + g + 1)
                        for j in range(TB):
                            mm = pe.transpose(ps[:, PV, P * j:P * (j + 1)], ot[:, P * j:P * (j + 1)], eye)
                        mm.then_inc(q[l, "den_ready"], 1)

                    for what, n in schedule(l):
                        if what == "f":
                            if l == 2 and n == 0:
                                mixture_bias(l, b)
                            up(l, b, n)
                            if n:
                                down(l, b, n - 1)
                        elif what == "fl":
                            down(l, b, NF[l] - 1)
                        elif what == "a":
                            scores_a(n)
                        elif what == "mx":
                            turn_max()
                        elif what == "b":
                            scores_b(n)
                        elif what == "pv":
                            values(n[0], n[1])
                        else:
                            denominators(n)
                    pe.wait_ge(q[l, "pv_free"], start[l, "pv_free"] + QUADS * (b + 1) + 1)
                    for j in range(TB):
                        mm = pe.transpose(ps[:, PV, P * j:P * (j + 1)], on[:, j, :], eye)
                    mm.then_inc(q[l, "heads_turned"], 1)

                def projection(b):
                    pe.wait_ge(q[l, "heads_ready"], start[l, "heads_ready"] + b + 1)
                    for j in range(TB):
                        mm = pe.matmul(ps[:, PV, P * j:P * (j + 1)], ot[:, P * j:P * (j + 1)], W(l, "wp"),
                                       start=(j == 0), stop=True, skip_group_check=True)
                    mm.then_inc(q[l, "attn_ready"], 1)

                queries_keys(0)
                values_gate(0)
                with pe.Fori(0, NB - 1) as b:
                    heads(b)
                    queries_keys(b + 1)
                    projection(b)
                    values_gate(b + 1)
                    if l != layers[-1]:
                        turn_xn(l, b)
                heads(NB - 1)
                projection(NB - 1)
                if l != layers[-1]:
                    turn_xn(l, NB - 1)

            pe.sem_inc(q[0, "y_ready"], 1)
            pe.sem_inc(q[0, "pv_done"], 2)
            pe.wait_ge(s_c32, 16)
            for b in range(NB):
                pe.wait_ge(xn_ready["pre"], b + 1)
                for j in range(TB):
                    mm = pe.transpose(ps[:, b, P * j:P * (j + 1)], xn[:, TB * b + j, :], eye)
                mm.then_inc(xn_turned["pre"], 1)
            pe.wait_ge(s_c16, 16)
            for l in layers:
                if l == 0:
                    layer0()
                else:
                    if l == 3:
                        pe_route()
                    attention_layer(l)

        @block.scalar
        def _(act):
            al = sem("scalar_own")
            own = Links(act, al)

            def take_xnt(l, b):
                act.wait_ge(xn_turned[l], b + 1)
                act.activation(xnt[:, span(b)], ps[:, MI, :], ACT.Copy).then_inc(xnt_ready[l], 1)

            def gate_exp(l, b):
                act.wait_ge(q[l, "gate_diff"], start[l, "gate_diff"] + b + 1)
                if l == 2:
                    act.activation(cw2[:, :, 0:9], cw[:, :, 0:9], ACT.Exp).then_inc(q[l, "gate_exp"], 1)
                else:
                    act.activation(gd[:, 1, :], gd[:, 0, :], ACT.Exp).then_inc(q[l, "gate_exp"], 1)

            def hidden(l, b, f):
                act.wait_ge(q[l, "up_ready"], start[l, "up_ready"] + b * NF[l] + f + 1)
                if l == 1:
                    act.activation(act_t[:, :], ps[:, UP, :], ACT.Tanh, scale=0.5).then_inc(q[l, "tanh_done"], 1)
                    return
                n = 3 if l == 0 else 2
                act.wait_ge(q[l, "y_ready"], start[l, "y_ready"] + b * NY[l] + (upto(l, f - n) if f >= n else 0) + 1)
                act.activation(hidden_buffer(l, f), ps[:, up_bank(l, f), :], ACT.Gelu, bias=W(l, "b1")[:, f:f + 1])\
                   .then_inc(q[l, "hidden_ready"], 1)

            def gate_tanh(l, b):
                if l == 3:
                    act.wait_ge(q[l, "gathered"], 16 * TB * (b + 1))
                else:
                    act.wait_ge(q[l, "y_free"], start[l, "y_free"] + NE[l] * (b + 1) + 1)
                act.activation(act_t[:, :], gs[:, bass.ds(b * TB, TB), :] if l == 3 else facc[:, :, :], ACT.Tanh, scale=0.5).then_inc(q[l, "fgate_ready"], 1)

            def layer0():
                l = 0
                act.wait_ge(s_w[0], 32)
                act.activation(small[:, 16:48], W(l, "a_log"), ACT.Exp).then_inc(q[l, "a_exp"], 1)
                act.wait_ge(dn_set, 1)
                with act.Fori(0, NB) as b:
                    own.enter(b, "act0")
                    for g in range(2):
                        act.wait_ge(q[l, "proj_ready"], start[l, "proj_ready"] + NPROJ[l] * b + g + 1)
                        act.activation(l0["xp"][:, g, KC - 1:], ps[:, g, :], ACT.Identity,
                                       bias=W(l, "in_b")[:, g:g + 1]).then_inc(q[l, "xp_ready"], 1)
                    for g in range(2):
                        act.wait_ge(q[l, "proj_ready"], start[l, "proj_ready"] + NPROJ[l] * b + g + 3)
                        act.activation(l0["zs"][:, g, :], ps[:, 2 + g, :], ACT.Identity,
                                       bias=small[:, 10 + g:11 + g], scale=0.5).then_inc(q[l, "zbias_ready"], 1)
                    act.wait_ge(q[l, "zbias_ready"], 2 * b + 2)
                    act.activation(l0["tmp"][:, :, :], l0["zs"][:, :, :], ACT.Tanh).then_inc(q[l, "z_tanh"], 1)
                    for n in range(AHEAD[0]):
                        hidden(l, b, n)
                    for g in range(2):
                        act.wait_ge(q[l, "conv_ready"], 2 * b + g + 1)
                        act.activation(l0["xconv"][:, g, :], l0["xc"][:, g, :], ACT.Tanh)\
                           .then_inc(q[l, "conv_tanh"], 1)
                    gate_exp(l, b)
                    for g in range(2):
                        act.wait_ge(q[l, "dt_abs"], 2 * b + g + 1)
                        own.add(act.activation(l0["dtx"][:, g, :], l0["dt"][:, g, :], ACT.Abs))
                    own.wait(1)
                    own.add(act.activation(l0["dtx"][:, 0, :], l0["dtx"][:, 0, :], ACT.Exp, scale=-1.0))
                    own.wait(2)
                    own.add(act.activation(l0["dtx"][:, 1, :], l0["dtx"][:, 1, :], ACT.Exp, scale=-1.0))
                    own.wait(3)
                    own.add(act.activation(l0["dtx"][:, 0, :], l0["dtx"][:, 0, :], ACT.Ln, bias=1.0))
                    own.wait(4)
                    act.activation(l0["dtx"][:, 1, :], l0["dtx"][:, 1, :], ACT.Ln, bias=1.0)\
                       .then_inc(q[l, "dt_ln"], 1)
                    for n in range(*AHEAD):
                        hidden(l, b, n)
                    act.wait_ge(q[l, "dt_ready"], b + 1)

                    def decay(s):
                        for g in range(2):
                            act.wait_ge(q[l, "da_free"], 2 * NST * b + 2 * s + g + 1)
                            act.activation(l0[f"da{s % 2}"][:, g, :], l0["dt"][:, g, :], ACT.Exp,
                                           scale=small[:, 16 + NST * g + s:17 + NST * g + s])\
                               .then_inc(q[l, "da_ready"], 1)

                    decay(0)
                    for what, n in schedule(l):
                        if what == "s" and n + 1 < NST:
                            decay(n + 1)
                        elif what == "f":
                            hidden(l, b, n)
                    gate_tanh(l, b)
                    if l != layers[-1]:
                        take_xnt(l, b)
                    own.close("act0")

            def act_route():
                l = 3
                act.wait_ge(q[l, "logits_shifted"], 1)
                act.activation(r_w[:, :, :], r_w[:, :, :], ACT.Exp).then_inc(q[l, "logits_exp"], 1)
                act.wait_ge(q[l, "stack_turned"], 1)
                act.activation(r_partst, ps[0:3 * PART, 0:4, :], ACT.Copy).then_inc(q[l, "stack_parts"], 1)
                for n in range(ST // 4):
                    act.wait_ge(q[l, "slots_turning"], n + 1)
                    act.activation(xet[:, T * n:T * (n + 1)], ps[:, n % 4, :], ACT.Copy)\
                       .then_inc(q[l, "slots_turned"], 1)
                for e in range(E3):
                    act.wait_ge(q[l, "expert_up"], e + 1)
                    if e >= 2:
                        act.wait_ge(q[l, "expert_down"], e - 1)
                    for c in range(2):
                        ins = act.activation(hid[:, e % 2, CAP * c:CAP * (c + 1)],
                                             ps[:, 4 + e % 2, CAP * c:CAP * (c + 1)], ACT.Gelu_apprx_tanh,
                                             bias=W(l, "b1")[:, 2 * e + c:2 * e + c + 1])
                    ins.then_inc(q[l, "expert_hidden"], 1)
                for n in range(ST // 4):
                    act.wait_ge(q[l, "slots_turning"], ST // 4 + n + 1)
                    act.activation(xe[:, 4 * n:4 * n + 4, :], ps[:, n % 4, :], ACT.Copy)\
                       .then_inc(q[l, "slots_turned"], 1)

            def attention_layer(l):
                rs = float(DH) ** -0.5
                _, ub, st = units[l]
                act.wait_ge(s_w[l], 48 if l == 2 else 32)
                if l == 3:
                    act_route()

                def queries_keys(b):
                    act.wait_ge(q[l, "pv_done"], start[l, "pv_done"] + b * NS[l] + 2)
                    for c in range(EV[l]):
                        act.wait_ge(q[l, "proj_ready"], start[l, "proj_ready"] + NPROJ[l] * b + c + 1)
                        isq = c % 2 == 0
                        if l == 3:
                            ins = act.activation(vf[c], ps[:, c, :], ACT.Identity, scale=rs if isq else 1.0,
                                                 bias=small[:, 48:49] if isq else W(l, "bk"))
                        else:
                            ins = act.activation(vf[c], ps[:, c, :], ACT.Copy, scale=rs if isq else 1.0)
                        ins.then_inc(q[l, "evac_done"], 1)

                def heads(b):
                    def probabilities(u):
                        act.wait_ge(q[l, "b_ready"], start[l, "b_ready"] + b * NUB[l] + u + 1)
                        s, n, regions = ub[u]
                        if s is None:
                            for h, j, col, _ in regions:
                                bank = ps[:, 2 * (u % 2) + col // 512, :]
                                ins = act.activation(bank, bank, ACT.Exp, accum_out=dens[:, j, h:h + 1])
                            ins.then_inc(q[l, "exp_done"], 1)
                            return
                        g, what = st[s][:2]
                        if n == 0 and what == "x":
                            if g >= 2:
                                act.wait_ge(q[l, "pv_done"], start[l, "pv_done"] + b * NS[l] + s - 1)
                        elif n == 0:
                            act.wait_ge(q[l, "pv_done"], start[l, "pv_done"] + b * NS[l] + s + 1)
                        src = ps[:, 2 * (u % 2):2 * (u % 2) + 2, :]
                        if what == "y":
                            dst, src = pty[:, :, :], src.rearrange("p k (i c) -> p (k i) c", c=256)
                        elif what == "x":
                            dst = pt[g % 2][:, n, :].rearrange("p (k c) -> p k c", k=2)
                        else:
                            dst = pt[s % 2][:, n, :].rearrange("p (k c) -> p k c", k=2)
                        act.activation(dst, src, ACT.Exp).then_inc(q[l, "exp_done"], 1)

                    for what, n in schedule(l):
                        if what == "f":
                            hidden(l, b, n)
                        elif what == "b":
                            probabilities(n)
                    act.wait_ge(q[l, "heads_turned"], start[l, "heads_turned"] + b + 1)
                    act.activation(ot[:, :], ps[:, PV, :], ACT.Copy).then_inc(q[l, "heads_ready"], 1)

                queries_keys(0)
                if l != 3:
                    gate_exp(l, 0)
                with act.Fori(0, NB - 1) as b:
                    heads(b)
                    queries_keys(b + 1)
                    gate_tanh(l, b)
                    if l != layers[-1]:
                        take_xnt(l, b)
                    if l != 3:
                        gate_exp(l, b + 1)
                heads(NB - 1)
                gate_tanh(l, NB - 1)
                if l != layers[-1]:
                    take_xnt(l, NB - 1)

            act.sem_inc(q[0, "hidden_ready"], 1)
            act.sem_inc(q[0, "exp_done"], 2)
            for n in ("pre",) + tuple(layers):
                act.sem_inc(xnt_ready[n], 1)
            for b in range(NB):
                act.wait_ge(xn_turned["pre"], b + 1)
                act.activation(xnt[:, T * b:T * (b + 1)], ps[:, b, :], ACT.Copy).then_inc(xnt_ready["pre"], 1)
            for l in layers:
                layer0() if l == 0 else attention_layer(l)

        @block.vector
        def _(dve):
            own = Links(dve, dl)
            tt, stt, ts, cp = dve.tensor_tensor, dve.scalar_tensor_tensor, dve.tensor_scalar, dve.tensor_copy

            def moments(src, l, n):
                wait_done(dve, 0)
                for j in range(TB):
                    own.add(dve.bn_stats(stat[:, j, :], src(j)))
                own.wait()
                wait_done(dve, 0)
                for j in range(TB):
                    ins = dve.bn_aggr(mv[:, j, :], stat[:, j, :])
                ins.then_inc(var_ready[l], 1)
                dve.wait_ge(rstd_ready[l], n)

            def normed(b, l, n):
                moments(lambda j: x[:, bass.ds(b * TB + j, 1), :].rearrange("p o d -> p (o d)"), l, n)
                for j in range(TB):
                    own.add(ts(xn[:, bass.ds(b * TB + j, 1), :].rearrange("p o d -> p (o d)"),
                               x[:, bass.ds(b * TB + j, 1), :].rearrange("p o d -> p (o d)"),
                               mv[:, j, 0:1], rstd[:, j:j + 1], ALU.subtract, ALU.mult))
                own.wait()
                ts(xs[:, :, :], xn[:, bass.ds(b * TB, TB), :], 1.0, None, ALU.mult).then_inc(xn_ready[l], 1)

            def gates(l, b, count):
                n = NE[l]
                dve.wait_ge(q[l, "proj_ready"], start[l, "proj_ready"] + count)
                src = ps[:, YB, 0:16 * TB].rearrange("p (j e) -> p j e", e=16)[:, :, 0:n]
                if l == 0:
                    tt(lg[:, :, 0:n], src, W(l, "gate_b").unsqueeze(1).to_broadcast([P, TB, n]), ALU.add)\
                        .then_inc(q[l, "gate_seen"], 1)
                else:
                    cp(lg[:, :, 0:n], src).then_inc(q[l, "gate_seen"], 1)
                dve.wait_ge(q[l, "gate_seen"], start[l, "gate_seen"] + b + 1)
                wait_done(dve, 0)
                for j in range(TB):
                    own.add(dve.max(m8[:, j, :], lg[:, j, 0:8]))
                own.wait()
                wait_done(dve, 0)
                for j in range(TB):
                    own.add(dve.max_index(i8[:, j, :], m8[:, j, :], lg[:, j, 0:8]))
                if l == 2:
                    own.add(tt(cw[:, :, 0:8], lg[:, :, 0:8], m8[:, :, 0:1].to_broadcast([P, TB, 8]), ALU.subtract))
                    tt(cw[:, :, 8:9], m8[:, :, 1:2], m8[:, :, 0:1], ALU.subtract).then_inc(q[l, "gate_diff"], 1)
                else:
                    tt(gd[:, 0, :], m8[:, :, 1], m8[:, :, 0], ALU.subtract).then_inc(q[l, "gate_diff"], 1)
                own.wait()
                own.link(cp(fi[:, :, :], i8[:, :, :]))

            def weights(l, b):
                n = NE[l]
                dve.wait_ge(q[l, "gate_exp"], start[l, "gate_exp"] + b + 1)
                io = iota[:, 0:n].unsqueeze(1).to_broadcast([P, TB, n])
                if l == 2:
                    own.add(dve.tensor_reduce(gd[:, 1, :], cw2[:, :, 0:8], AX.X, ALU.add))
                    own.add(ts(gd[:, 2, :], cw2[:, :, 8], 1.0, None, ALU.add))
                    own.wait()
                    own.link(dve.reciprocal(gd[:, 3, :], gd[:, 1, :]))
                    own.add(tt(gd[:, 4, :], gd[:, 2, :], gd[:, 3, :], ALU.mult))
                    own.add(tt(cw[:, :, 0:n], io, fi[:, :, 0:1].to_broadcast([P, TB, n]), ALU.is_equal))
                    own.link(tt(cw2[:, :, 0:n], io, fi[:, :, 1:2].to_broadcast([P, TB, n]), ALU.is_equal))
                    own.link(tt(cw[:, :, 0:n], cw[:, :, 0:n], cw2[:, :, 0:n], ALU.add))
                    tt(cw[:, :, 0:n], cw[:, :, 0:n], gd[:, 4, :].unsqueeze(2).to_broadcast([P, TB, n]), ALU.mult)\
                        .then_inc(q[l, "cw_ready"], 1)
                else:
                    own.add(tt(cw[:, :, 0:n], io, fi[:, :, 0:1].to_broadcast([P, TB, n]), ALU.is_equal))
                    own.add(tt(cw2[:, :, 0:n], io, fi[:, :, 1:2].to_broadcast([P, TB, n]), ALU.is_equal))
                    own.link(ts(gd[:, 2, :], gd[:, 1, :], 1.0, None, ALU.add))
                    own.link(dve.reciprocal(gd[:, 3, :], gd[:, 2, :]))
                    own.add(tt(cw[:, :, 0:n], cw[:, :, 0:n], gd[:, 3, :].unsqueeze(2).to_broadcast([P, TB, n]), ALU.mult))
                    own.link(tt(gd[:, 4, :], gd[:, 1, :], gd[:, 3, :], ALU.mult))
                    own.link(tt(cw2[:, :, 0:n], cw2[:, :, 0:n], gd[:, 4, :].unsqueeze(2).to_broadcast([P, TB, n]), ALU.mult))
                    tt(cw[:, :, 0:n], cw[:, :, 0:n], cw2[:, :, 0:n], ALU.add).then_inc(q[l, "cw_ready"], 1)
                if l == 1:
                    return
                dve.wait_ge(q[l, "cwt_turned"], start[l, "cwt_turned"] + b + 1)
                cp(cwt[0:n, :], ps[0:n, MI, :]).then_inc(q[l, "cwt_ready"], 1)
                dve.wait_ge(q[l, "bias_ready"], start[l, "bias_ready"] + b + 1)
                cp(facc[:, :, :], ps[:, MI, :].rearrange("p (j d) -> p j d", j=TB)).then_inc(q[l, "bias_seen"], 1)

            def gated(b, f):
                l = 1
                dve.wait_ge(q[l, "tanh_done"], b * NF[l] + f + 1)
                own.link(stt(act_g[:, :], act_t[:, :], 1.0, ps[:, UP, :], ALU.add, ALU.mult))
                dve.wait_ge(q[l, "y_ready"], start[l, "y_ready"] + b * NY[l] + (upto(l, f - 2) if f >= 2 else 0) + 1)
                dst = hidh[:, :] if len(CH1[f]) == 2 else hid[:, f % 2, :]
                stt(dst, act_g[:, :], 0.5, ps[:, MI, :], ALU.mult, ALU.mult).then_inc(q[l, "hidden_ready"], 1)

            def mix(l, b, f):
                for n, (e, _, _, _, _, last) in enumerate(DG[l][f]):
                    if not last:
                        continue
                    dve.wait_ge(q[l, "y_ready"], start[l, "y_ready"] + b * NY[l] + upto(l, f - 1) + n + 2)
                    if l == 1 and e == 0:
                        pass
                    elif e == 0:
                        dve.wait_ge(q[l, "bias_seen"], start[l, "bias_seen"] + b + 1)
                    else:
                        dve.wait_ge(q[l, "y_free"], start[l, "y_free"] + b * NE[l] + e + 1)
                    if e == 0:
                        dve.wait_ge(q[l, "cw_ready"], start[l, "cw_ready"] + b + 1)
                    for j in range(TB):
                        yj = ps[:, YB, P * j:P * (j + 1)]
                        if l == 1 and e == 0:
                            ins = ts(facc[:, j, :], yj, cw[:, j, e:e + 1], None, ALU.mult)
                        else:
                            ins = stt(facc[:, j, :], yj, cw[:, j, e:e + 1], facc[:, j, :], ALU.mult, ALU.add)
                    ins.then_inc(q[l, "y_free"], 1)

            def combine(l, b):
                dve.wait_ge(q[l, "fgate_ready"], start[l, "fgate_ready"] + b + 1)
                mixture = gs[:, bass.ds(b * TB, TB), :] if l == 3 else facc[:, :, :]
                own.link(stt(facc[:, :, :], act_t[:, :].rearrange("p (j d) -> p j d", j=TB), 1.0, mixture,
                             ALU.add, ALU.mult))
                own.link(tt(sa[:, :, :], sa[:, :, :], facc[:, :, :], ALU.mult))
                xv = x[:, bass.ds(b * TB, TB), :]
                ins = stt(xv, sa[:, :, :], 0.5, xv, ALU.mult, ALU.add)
                if l != layers[-1]:
                    own.link(ins)
                    normed(b, l, (b + 1) if l == 0 else 2 * b + 2)
                else:
                    ins.then_inc(q[l, "layer_done"], 1)

            def spread_rows(v):
                return v.unsqueeze(1).to_broadcast([P, TB, v.shape[1]])

            def layer0():
                l = 0
                dve.wait_ge(s_w[0], 32)
                dve.sem_inc(q[l, "da_free"], 4)
                dve.sem_inc(q[l, "hc_ready"], 4)
                own.add(dve.memset(l0["xp"][:, :, 0:KC - 1], 0.0))
                own.add(ts(small[:, 0:8], W(l, "conv_w"), 0.5, None, ALU.mult))
                own.add(ts(small[:, 8:10], W(l, "conv_b"), 0.5, None, ALU.mult))
                own.add(ts(small[:, 10:12], W(l, "in_b")[:, 2:4], 0.5, None, ALU.mult))
                dve.wait_ge(q[l, "a_exp"], 1)
                ts(small[:, 16:48], small[:, 16:48], -1.0, None, ALU.mult).then_inc(dn_set, 1)
                own.straight()
                with dve.Fori(0, NB) as b:
                    own.enter(b, 0)
                    dve.wait_ge(xnt_ready[before[l]], b + 2)
                    ts(xb[:, :], xnt[:, span(b)], 1.0, None, ALU.mult).then_inc(q[l, "xb_ready"], 1)
                    for g in range(2):
                        dve.wait_ge(q[l, "xp_ready"], 2 * b + g + 1)
                        own.add(ts(l0["xc"][:, g, :], l0["xp"][:, g, 0:T], small[:, KC * g:KC * g + 1],
                                   small[:, 8 + g:9 + g], ALU.mult, ALU.add))
                    n0 = own.n
                    for k in range(1, KC):
                        for g in range(2):
                            own.wait(n0 + 2 * (k - 1) - 1 + g)
                            ins = stt(l0["xc"][:, g, :], l0["xp"][:, g, k:k + T], small[:, KC * g + k:KC * g + k + 1],
                                      l0["xc"][:, g, :], ALU.mult, ALU.add)
                            if k == KC - 1:
                                ins.then_inc(q[l, "conv_ready"], 1)
                            else:
                                own.add(ins)
                    gates(l, b, NPROJ[l] * (b + 1))
                    for g in range(2):
                        dve.wait_ge(q[l, "conv_tanh"], 2 * b + g + 1)
                        stt(l0["xconv"][:, g, :], l0["xconv"][:, g, :], 1.0, l0["xc"][:, g, :], ALU.add, ALU.mult)\
                            .then_inc(q[l, "xconv_ready"], 1)
                    weights(l, b)
                    dve.wait_ge(q[l, "z_tanh"], b + 1)
                    own.add(stt(l0["zs"][:, :, :], l0["tmp"][:, :, :], 1.0, l0["zs"][:, :, :], ALU.add, ALU.mult))
                    for g in range(2):
                        dve.wait_ge(q[l, "dtbc_ready"], 3 * b + g + 1)
                        ts(l0["dt"][:, g, :], ps[:, g, :], W(l, "dt_b")[:, g:g + 1], None, ALU.add)\
                            .then_inc(q[l, "dt_abs"], 1)
                    dve.wait_ge(q[l, "dtbc_ready"], 3 * b + 3)
                    n = 2 * NST
                    own.link(ts(l0["bcf"][0:n, :], ps[0:n, 2, :], W(l, "bc_b")[0:n, :], None, ALU.add))
                    own.link(cp(l0["bcs"][0:n, :], l0["bcf"][0:n, :]))
                    own.link(tt(l0["bcf"][0:n, :], l0["bcf"][0:n, :], l0["bcs"][0:n, :], ALU.subtract))
                    own.link(cp(l0["bcm"][0:n, :], l0["bcf"][0:n, :]))
                    own.add(cp(l0["bcs"][n:2 * n, :], l0["bcm"][0:n, :]))
                    tt(l0["bcs"][2 * n:3 * n, :], l0["bcf"][0:n, :], l0["bcm"][0:n, :], ALU.subtract)\
                        .then_inc(q[l, "bcs_ready"], 1)
                    dve.wait_ge(q[l, "dt_ln"], b + 1)
                    for g in range(2):
                        own.add(stt(l0["dt"][:, g, :], l0["dt"][:, g, :], 0.0, l0["dtx"][:, g, :], ALU.max, ALU.add))
                    own.wait()
                    own.add(tt(l0["dtx"][:, 0, :], l0["dt"][:, 0, :], l0["xconv"][:, 0, :], ALU.mult))
                    tt(l0["dtx"][:, 1, :], l0["dt"][:, 1, :], l0["xconv"][:, 1, :], ALU.mult)\
                        .then_inc(q[l, "dt_ready"], 1)
                    for g in range(2):
                        ts(l0["y"][:, g, :], l0["xconv"][:, g, :], W(l, "d")[:, g:g + 1], None, ALU.mult)\
                            .then_inc(q[l, "y_begun"], 1)
                    dve.wait_ge(q[l, "dt_ready"], b + 1)

                    def step(s):
                        dve.wait_ge(q[l, "bc_rows"], b * NST + s + 1)
                        k = 2 * (s % 2)
                        for g in range(2):
                            own.add(tt(l0["ub"][:, g, :], l0["dtx"][:, g, :], ps[:, k, :], ALU.mult))
                        n0 = own.n
                        at_ = 2 * NST * b + 2 * s
                        for g in range(2):
                            dve.wait_ge(q[l, "da_ready"], at_ + g + 1)
                            own.wait(n0 - 1 + g)
                            dve.tensor_tensor_scan(l0["hs"][:, g, :], l0[f"da{s % 2}"][:, g, :], l0["ub"][:, g, :],
                                                   0.0, ALU.mult, ALU.add).then_inc(q[l, "da_free"], 1)
                        for g in range(2):
                            dve.wait_ge(q[l, "state_added"], at_ + g + 1)
                            dve.wait_ge(q[l, "da_free"], at_ + g + 5)
                            tt(l0["hc"][:, g, :], l0["hs"][:, g, :], ps[:, k + 1, :], ALU.mult)\
                                .then_inc(q[l, "hc_ready"], 1)

                    for n in range(*AHEAD):
                        mix(l, b, n - LAG[l])
                    for what, n in schedule(l):
                        if what == "s":
                            step(n)
                        elif what == "f":
                            mix(l, b, n - LAG[l])
                        else:
                            for f in range(NF[l] - LAG[l], NF[l]):
                                mix(l, b, f)
                    dve.wait_ge(q[l, "state_added"], 2 * NST * (b + 1) + 2)
                    tt(l0["y"][:, :, :], l0["y"][:, :, :], l0["zs"][:, :, :], ALU.mult).then_inc(q[l, "yg_ready"], 1)
                    dve.wait_ge(q[l, "attn_ready"], start[l, "attn_ready"] + b + 1)
                    tt(sa[:, :, :], ps[:, PV, :].rearrange("p (j d) -> p j d", j=TB), spread_rows(W(l, "out_b")),
                       ALU.add).then_inc(q[l, "tail_done"], 1)
                    dve.wait_ge(q[l, "tail_done"], start[l, "tail_done"] + b + 2)
                    combine(l, b)
                    own.close(0)

            def dve_route():
                l = 3
                own.add(dve.memset(r_parts[:, :, :], 0.0))
                own.add(dve.memset(r_hot[:, :, :], 0.0))
                own.add(dve.memset(r_v[:, 1, :], 0.0))
                dve.wait_ge(q[l, "logits_ready"], 1)
                own.link(cp(r_lg[:, :, :], ps[:, YB, 0:NT * E3].rearrange("p (i e) -> p i e", e=E3)))
                for i in range(NT):
                    own.add(dve.max(r_m8[:, i, :], r_lg[:, i, :]))
                own.wait()
                for i in range(NT):
                    own.add(dve.max_index(r_i8[:, i, :], r_m8[:, i, :], r_lg[:, i, :]))
                tt(r_w[:, :, :], r_lg[:, :, :], r_m8[:, :, 0:1].to_broadcast([P, NT, E3]), ALU.subtract)\
                    .then_inc(q[l, "logits_shifted"], 1)
                own.wait()
                own.link(cp(r_fi[:, :, :], r_i8[:, :, :]))
                io = iota[:, 0:E3].unsqueeze(1).to_broadcast([P, NT, E3])
                own.add(tt(r_hot1[:, :, :], io, r_fi[:, :, 0:1].to_broadcast([P, NT, E3]), ALU.is_equal))
                dve.wait_ge(q[l, "logits_exp"], 1)
                own.link(dve.tensor_reduce(r_v[:, 8, :], r_w[:, :, :], AX.X, ALU.add))
                own.link(dve.reciprocal(r_v[:, 0, :], r_v[:, 8, :]))
                for k in range(3):
                    own.add(cp(r_hot[:, :, PART * k:PART * k + E3], r_hot1[:, :, :]))
                own.link(tt(r_w[:, :, :], r_hot1[:, :, :], r_v[:, 0, :].unsqueeze(2).to_broadcast([P, NT, E3]),
                            ALU.mult))
                high = r_b16[:, 0, :].rearrange("p (i e) -> p i e", e=E3)
                mid = r_b16[:, 1, :].rearrange("p (i e) -> p i e", e=E3)
                own.link(cp(high, r_w[:, :, :]))
                own.add(cp(r_parts[:, :, 0:E3], high))
                own.link(tt(r_w[:, :, :], r_w[:, :, :], high, ALU.subtract))
                own.link(cp(mid, r_w[:, :, :]))
                own.add(cp(r_parts[:, :, PART:PART + E3], mid))
                own.wait()
                tt(r_parts[:, :, 2 * PART:2 * PART + E3], r_w[:, :, :], mid, ALU.subtract)\
                    .then_inc(q[l, "stack_built"], 1)
                dve.wait_ge(q[l, "stack_turned"], 2)
                cp(r_hott.rearrange("p (k c) -> p k c", k=4), ps[0:3 * PART, 4:8, :]).then_inc(q[l, "stack_hot"], 1)

                def slots(g):
                    dve.wait_ge(q[l, "ranked"], TB * (g + 1))
                    t = slice(TB * g, TB * (g + 1))
                    v = [r_v[:, k, t] for k in range(9)]
                    drop = W("c32", "drop")[:, t]
                    own.add(tt(v[4], v[1], v[2], ALU.add))
                    own.link(stt(v[5], r_fi[:, t, 0], float(CAP), drop, ALU.mult, ALU.subtract))
                    own.link(tt(v[4], v[4], v[3], ALU.add))
                    own.add(tt(v[5], v[5], v[4], ALU.add))
                    own.link(ts(v[6], v[4], float(CAP), None, ALU.is_lt))
                    own.link(tt(v[5], v[5], v[6], ALU.mult))
                    own.link(tt(v[5], v[5], drop, ALU.add))
                    cp(r_idx[:, t], v[5]).then_inc(q[l, "index_ready"], 1)

                for i in range(NT):
                    dve.wait_ge(q[l, "row_ready"], i + 1)
                    if i:
                        dve.wait_ge(q[l, "ranked"], i)
                    row = ps[:, 4 * (i % 2):4 * (i % 2) + 4, :].rearrange("p k c -> p (k c)")
                    mine = r_v[:, 0, i:i + 1]
                    if i:
                        own.add(ts(r_junk[:, 0:P * i], row[:, 0:P * i], mine, 0.0, ALU.is_ge, ALU.add,
                                   accum_out=r_v[:, 1, i:i + 1]))
                    own.add(ts(r_junk[:, P * i:NT * P], row[:, P * i:NT * P], mine, 0.0, ALU.is_gt, ALU.add,
                               accum_out=r_v[:, 2, i:i + 1]))
                    own.wait()
                    stt(r_junk[:, NT * P:], row[:, P * i:P * (i + 1)], mine, W("c32", "lower"), ALU.is_equal, ALU.mult,
                        accum_out=r_v[:, 3, i:i + 1]).then_inc(q[l, "ranked"], 1)
                    if i % TB == TB - 1:
                        slots(i // TB)
                for e in range(E3):
                    dve.wait_ge(q[l, "expert_down"], e + 1)
                    ts(xet[:, CAP * e:CAP * (e + 1)], ps[:, 6 + e % 2, 0:CAP], W(l, "b2")[:, e:e + 1], None, ALU.add)\
                        .then_inc(q[l, "expert_out"], 1)
                own.straight()

            def attention_layer(l):
                ua, ub, st = units[l]
                dve.wait_ge(s_w[l], 48 if l == 2 else 32)
                if l == 1:
                    own.add(dve.memset(lg[:, :, E1:8], NEG))
                if l == first:
                    own.add(dve.memset(vx[:, :, :], 0.0))
                    own.wait()
                elif l == 1:
                    own.add(dve.memset(vx[:, :, :], 0.0))
                    own.wait()
                own.add(dve.memset(vx[:, :, 0:NH * VW].rearrange("p j (h d) -> p j h d", d=VW)[:, :, :, DH:VW],
                                   0.0 if l == 2 else 1.0))
                if l == 3:
                    own.add(ts(small[:, 48:49], W(l, "bq"), float(DH) ** -0.5, None, ALU.mult))
                own.wait()
                own.straight()
                if l == 3:
                    dve_route()

                def queries_keys(b):
                    dve.wait_ge(xnt_ready[before[l]], b + 2)
                    ts(xb[:, :], xnt[:, span(b)], 1.0, None, ALU.mult).then_inc(q[l, "xb_ready"], 1)

                    def parts(v, k):
                        rest = act_g[:, :] if l == 2 else vf[v]
                        if l == 2 and k:
                            dve.wait_ge(q[l, "parts_ready"], start[l, "parts_ready"] + 4 * b + k)
                        own.link(cp(part[k][:, 0, :], vf[v]))
                        own.link(tt(rest, vf[v], part[k][:, 0, :], ALU.subtract))
                        own.link(cp(part[k][:, 1, :], rest))
                        tt(part[k][:, 2, :], rest, part[k][:, 1, :], ALU.subtract).then_inc(q[l, "parts_ready"], 1)

                    if l == 2:
                        for k in range(4):
                            dve.wait_ge(q[l, "evac_done"], start[l, "evac_done"] + EV[l] * b + k + 1)
                            if k >= 2:
                                dve.wait_ge(q[l, "parts_ready"], start[l, "parts_ready"] + 4 * b + k)
                                own.add(tt(act_g[:, :], vf[k - 2], rope[0], ALU.mult))
                                own.link(tt(vf[k], vf[k], rope[1], ALU.mult))
                                own.link(tt(vf[k], vf[k], act_g[:, :], ALU.add))
                            parts(k, k)
                    else:
                        for k in range(2):
                            dve.wait_ge(q[l, "evac_done"], start[l, "evac_done"] + EV[l] * b + k + 1)
                            parts(k, k)

                def values_gate(b):
                    dve.wait_ge(q[l, "proj_ready"], start[l, "proj_ready"] + NPROJ[l] * b + EV[l] + 1)
                    pv_in = ps[:, PV, :].rearrange("p (j h d) -> p j h d", j=TB, d=DH)
                    for j in range(TB):
                        if l == 3:
                            ins = tt(vx[:, j, 0:NH * VW].rearrange("p (h d) -> p h d", d=VW)[:, :, 0:DH], pv_in[:, j], W(l, "bv").rearrange("p (h d) -> p h d", d=DH),
                                     ALU.add)
                        else:
                            ins = cp(vx[:, j, 0:NH * VW].rearrange("p (h d) -> p h d", d=VW)[:, :, 0:DH], pv_in[:, j])
                        if j == TB - 1:
                            ins.then_inc(q[l, "values_ready"], 1)
                    if l != 3:
                        gates(l, b, NPROJ[l] * (b + 1))
                        weights(l, b)

                def heads(b):
                    def column(h):
                        return (h % 2) * (NH // 2) + h // 2

                    def maxima(u):
                        dve.wait_ge(q[l, "a_ready"], start[l, "a_ready"] + b * NUA[l] + u + 1)
                        base = 2 * (u % 2)
                        flat = ps[:, base:base + 2, :].rearrange("p k c -> p (k c)")
                        if l == 3:
                            h, j = ua[u][0][0], ua[u][0][1]
                            ins = dve.tensor_reduce(mx[:, j:j + 2, column(h)], ps[:, base:base + 2, :], AX.X, ALU.max,
                                                    negate=True)
                        elif len(ua[u]) == 4:
                            g = ua[u][0][0] // 4
                            dst = mx[:, 1, :].rearrange("p (a s) -> p a s", a=2)[:, :, 2 * g:2 * g + 2]
                            ins = dve.tensor_reduce(dst, ps[:, base:base + 2, :].rearrange("p k (i c) -> p k i c", c=256),
                                                    AX.X, ALU.max, negate=True)
                        else:
                            for h, j, col, n in ua[u]:
                                c = column(h)
                                ins = dve.tensor_reduce(mx[:, j, c:c + 1], flat[:, col:col + n], AX.X, ALU.max,
                                                        negate=True)
                        ins.then_inc(q[l, "a_free"], 1)

                    for what, n in schedule(l):
                        if what == "f":
                            if l == 1:
                                gated(b, n)
                            if n:
                                mix(l, b, n - 1)
                        elif what == "fl":
                            mix(l, b, NF[l] - 1)
                        elif what == "a":
                            maxima(n)
                        elif what == "mx":
                            dve.wait_ge(q[l, "max_turned"], start[l, "max_turned"] + b + 1)
                            own.link(cp(nm[:, 0, :], ps[0:NH, 0, :]))
                            tt(nm[:, 1, :], ps[0:NH, 0, :], nm[:, 0, :], ALU.subtract).then_inc(q[l, "max_parts"], 1)
                        elif what == "pv":
                            s, _, last = n
                            if last and (s + 1 == NS[l] or st[s + 1][0] != st[s][0]):
                                dve.wait_ge(q[l, "pv_done"], start[l, "pv_done"] + b * NS[l] + s + 3)
                                cp(ot[:, :], ps[:, PV, :]).then_inc(q[l, "head_copied"], 1)
                        elif what == "bc":
                            dve.wait_ge(q[l, "den_ready"], start[l, "den_ready"] + b * QUADS + n + 1)
                            four = ps[:, PV, :].rearrange("p (j i c) -> p j i c", j=TB, i=4)
                            own.link(dve.reciprocal(rcp[:, :, :], dens[:, :, 4 * n:4 * (n + 1)] if l == 2
                                                    else four[:, :, :, DH]))
                            tt(on[:, :, 32 * n:32 * (n + 1)].rearrange("p j (i c) -> p j i c", i=4), four[:, :, :, 0:DH],
                               rcp[:, :, :].unsqueeze(3).to_broadcast([P, TB, 4, DH]), ALU.mult)\
                                .then_inc(q[l, "pv_free"], 1)

                def projection(b):
                    dve.wait_ge(q[l, "attn_ready"], start[l, "attn_ready"] + b + 1)
                    pj = ps[:, PV, :].rearrange("p (j d) -> p j d", j=TB)
                    xv = xn[:, bass.ds(b * TB, TB), :]
                    tt(sa[:, :, :], pj, xv if l == 2 else spread_rows(W(l, "bp")), ALU.add)\
                        .then_inc(q[l, "tail_done"], 1)
                    dve.wait_ge(q[l, "tail_done"], start[l, "tail_done"] + b + 2)
                    if l == 1:
                        own.link(tt(sa[:, :, :], sa[:, :, :], xv, ALU.add))
                    if l != 3:
                        moments(lambda j: sa[:, j, :], l, 2 * b + 1 if l != layers[-1] else b + 1)
                        for j in range(TB):
                            own.add(ts(sa[:, j, :], sa[:, j, :], mv[:, j, 0:1], rstd[:, j:j + 1], ALU.subtract, ALU.mult))
                        own.wait()
                        own.link(tt(sa[:, :, :], sa[:, :, :], spread_rows(W(l, "gamma")), ALU.mult))
                        own.link(tt(sa[:, :, :], sa[:, :, :], spread_rows(W(l, "beta")), ALU.add))
                    combine(l, b)

                queries_keys(0)
                values_gate(0)
                own.straight()
                with dve.Fori(0, NB - 1) as b:
                    own.enter(b, l)
                    heads(b)
                    queries_keys(b + 1)
                    projection(b)
                    values_gate(b + 1)
                    own.close(l, NB - 1)
                heads(NB - 1)
                projection(NB - 1)
                own.straight()

            dve.sem_inc(q[0, "tail_done"], 1)
            dve.sem_inc(q[0, "y_free"], 1)
            dve.sem_inc(q[0, "pv_free"], 1)
            dve.sem_inc(q[0, "a_free"], 2)
            dve.wait_ge(s_x, 16)
            for t in range(NT):
                own.add(dve.bn_stats(stat0[:, t, :], x[:, t, :]))
            own.wait()
            for t in range(NT):
                ins = dve.bn_aggr(mv0[:, t, :], stat0[:, t, :])
            ins.then_inc(var_ready["pre"], 1)
            dve.wait_ge(rstd_ready["pre"], 1)
            for t in range(NT):
                ins = ts(xn[:, t, :], x[:, t, :], mv0[:, t, 0:1], rstd0[:, t:t + 1], ALU.subtract, ALU.mult)
                if t % TB == TB - 1:
                    ins.then_inc(xn_ready["pre"], 1)
            own.straight()
            for l in layers:
                layer0() if l == 0 else attention_layer(l)

        @block.gpsimd
        def _(pool):
            own = Links(pool, pl)
            own.add(pool.memset(half[:, :], -0.5))

            def serve(l, n, key):
                pool.wait_ge(var_ready[l], n)
                wait_done(pool, 1)
                own.link(pool.tensor_scalar(vare[:, :], mv[:, :, 1], EPS, None, ALU.add))
                pool.tensor_tensor(rstd[:, :], vare[:, :], half[:, :], ALU.pow).then_inc(rstd_ready[l], 1)

            def pool_route():
                l = 3
                pool.wait_ge(xnt_ready[before[l]], NB + 1)
                pool.memset(xe[:, :, :], 0.0).then_inc(q[l, "zeros_ready"], 1)
                pool.wait_ge(q[l, "zeros_out"], 32)
                for i in range(NT):
                    if i % TB == 0:
                        pool.wait_ge(q[l, "index_ready"], i // TB + 1)
                    pool.indirect_dma_start(slots_d, bass.IndirectOffsetOnAxis(ap=r_idx[:, i:i + 1], axis=0),
                                            xn[:, i, :], None).then_inc(q[l, "scattered"], 16)
                pool.wait_ge(q[l, "slots_out"], 16)
                for i in range(NT):
                    if i and i % TB == 0:
                        pool.wait_ge(q[l, "gathered"], 16 * i)
                    pool.indirect_dma_start(gs[:, i, :], None, slots_d,
                                            bass.IndirectOffsetOnAxis(ap=r_idx[:, i:i + 1], axis=0))\
                        .then_inc(q[l, "gathered"], 16)

            own.wait()
            pool.wait_ge(var_ready["pre"], 1)
            own.link(pool.tensor_scalar(vare0, mv0[:, :, 1], EPS, None, ALU.add))
            pool.tensor_tensor(rstd0, vare0, half[:, 0:1].to_broadcast([P, NT]), ALU.pow)\
                .then_inc(rstd_ready["pre"], 1)
            own.straight()
            for l in layers:
                n = (l in (1, 2)) + (l != layers[-1])
                if l == 3:
                    pool_route()
                if n or l == 0:
                    if l == 0:
                        pool.sem_inc(q[l, "state_added"], 2)
                    with pool.Fori(0, NB) as b:
                        own.enter(b, "pool%d" % n)
                        if l == 0:
                            pool.wait_ge(q[l, "y_begun"], 2 * (b + 1))
                            for s in range(NST):
                                for g in range(2):
                                    if s:
                                        pool.wait_ge(q[l, "state_added"], 2 * NST * b + 2 * s + g + 1)
                                    pool.wait_ge(q[l, "hc_ready"], 2 * NST * b + 2 * s + g + 5)
                                    pool.tensor_tensor(l0["y"][:, g, :], l0["y"][:, g, :], l0["hc"][:, g, :], ALU.add)\
                                        .then_inc(q[l, "state_added"], 1)
                        for k in range(n):
                            serve(l, n * b + k + 1, "pool")
                        own.close("pool%d" % n)

        @block.sync
        def _(sp):
            def load_weights(l):
                base = wb if l % 2 else wa
                cut = at[f"l{l}"]["w1"][0]
                n = wide[f"l{l}"]
                src = blobs[f"l{l}"]
                sp.dma_start(base[:, 0:cut], src[:, 0:cut]).then_inc(s_w[l], 16)
                sp.dma_start(base[:, cut:n], src[:, cut:n]).then_inc(s_w[l], 16)
                if l == 2:
                    sp.dma_start(wa[:, n:n + 2 * T], blobs["rope"]).then_inc(s_w[l], 16)

            def sp_route():
                l = 3
                slots = slots_d[0:SLOTS, :].rearrange("(n p) d -> p n d", p=P)
                sp.wait_ge(q[l, "zeros_ready"], 1)
                sp.dma_start(slots, xe[:, :, :]).then_inc(q[l, "zeros_out"], 16)
                sp.wait_ge(xn_ready[before[l]], NB)
                sp.dma_start(slots_d[SLOTS:, :].rearrange("(n p) d -> p n d", p=P), xn[:, :, :])\
                  .then_inc(q[l, "zeros_out"], 16)
                sp.wait_ge(q[l, "scattered"], 16 * NT)
                sp.dma_start(xe[:, :, :], slots).then_inc(q[l, "slots_in"], 16)
                sp.wait_ge(q[l, "slots_turned"], 2 * (ST // 4))
                sp.dma_start(slots, xe[:, :, :]).then_inc(q[l, "slots_out"], 16)

            sp.dma_start(x[:, :, :], x_in_v).then_inc(s_x, 16)
            sp.dma_start(c32[:, :], blobs["c32"]).then_inc(s_c32, 16)
            sp.dma_start(c16[:, :], blobs["c16"]).then_inc(s_c16, 16)
            if 0 in layers:
                sp.dma_start(l0["sel"], blobs["sel"].rearrange("p (s m) -> p s m", m=P)).then_inc(s_sel, 16)
            load_weights(layers[0])
            if len(layers) > 1:
                load_weights(layers[1])
            for i, l in enumerate(layers):
                if i:
                    sp.wait_ge(xn_ready[l - 1], NB)
                    if i + 1 < len(layers):
                        load_weights(l + 1)
                if l == 3:
                    sp_route()
                if l in (1, 3):
                    for s, k in ((0, 0), (1, 1)) if l == 1 else ((0, 2), (1, 3), (2, 4)):
                        for par in range(2):
                            sp.dma_start(stack[s][64 * par + AROW:64 * par + AROW + 6, :, :], blobs["rows"][k, par])\
                              .then_inc(q[l, "rows_ready"], 16)
                if l == 3:
                    sp.dma_start(slope, blobs["slope"]).then_inc(q[l, "rows_ready"], 16)
                def stacks(b):
                    order = range(len(OPERANDS[l]))
                    reads = 0
                    for n in range(len(order) + 1):
                        if n < len(order):
                            k = order[n]
                            sp.wait_ge(q[l, "parts_ready"], start[l, "parts_ready"] + len(order) * b + n + 1)
                            for j, pn in enumerate(KPARTS if k % 2 else QPARTS):
                                sp.dma_start(parts_d[k, :, j], part[k][:, pn, :]).then_inc(q[l, f"parts{k}_out"], 16)
                        if not n:
                            continue
                        k = order[n - 1]
                        sp.wait_ge(q[l, f"parts{k}_out"], start[l, f"parts{k}_out"] + 16 * NG * (b + 1))
                        for s in ((1, 2) if (l == 3 and k == 1) else (k,)):
                            for par in range(2):
                                sp.dma_start(stack[s][64 * par:64 * par + KROWS, :, :],
                                             parts_d[k, par::2].rearrange("p j d t -> (j d) p t"))\
                                  .then_inc(q[l, "rotated_ready" if s >= NSTK[l] else "stacks_ready"], 16)
                                reads += s < NSTK[l]
                    assert reads == 2 * NSTK[l]
                    sp.wait_ge(q[l, "stacks_ready"], start[l, "stacks_ready"] + 16 * 2 * NSTK[l] * (b + 1))
                    wait_done(sp, 2)
                    if l == 2:
                        sp.wait_ge(q[l, "rotated_ready"], 64 * (b + 1))
                        wait_done(sp, 2)

                def maxima(b):
                    sp.wait_ge(q[l, "max_parts"], start[l, "max_parts"] + b + 1)
                    sp.dma_start(max_d.rearrange("k a s t -> (a s) k t"), nm[:, :, :])\
                      .then_inc(q[l, "max_out"], 16)
                    sp.wait_ge(q[l, "max_out"], start[l, "max_out"] + 16 * (b + 1))
                    for par in range(2):
                        sp.dma_start(stack[0][64 * par + MROW:64 * par + KALL, :, :], max_d[:, par])\
                          .then_inc(q[l, "max_in"], 16)
                    sp.wait_ge(q[l, "max_in"], start[l, "max_in"] + 32 * (b + 1))
                    wait_done(sp, 2)

                def result(b):
                    sp.wait_ge(q[l, "layer_done"], b + 1)
                    sp.dma_start(out_v[:, bass.ds(b * TB, TB), :], x[:, bass.ds(b * TB, TB), :])\
                      .then_inc(s_out, 16)

                if l:
                    stacks(0)
                    with sp.Fori(0, NB - 1) as b:
                        if l != 2:
                            maxima(b)
                        stacks(b + 1)
                        if l == layers[-1]:
                            result(b)
                    if l != 2:
                        maxima(NB - 1)
                    if l == layers[-1]:
                        result(NB - 1)
                elif l == layers[-1]:
                    with sp.Fori(0, NB) as b:
                        result(b)
            sp.wait_ge(s_out, 16 * NB)


def kernel(**inputs):
    import concourse.bacc as bacc
    from concourse.bass_utils import run_bass_kernel_spmd

    host = {n: np.ascontiguousarray(a) for n, a in inputs.items()}
    packed = layouts(host)
    packed.update(constants())
    at = {n: where for n, (where, _) in packed.items()}
    arrays = {f"in_{n}": a for n, (_, a) in packed.items()}
    arrays["in_x"] = host["L0_attn_x"]
    nc = bacc.Bacc("TRN2", target_bir_lowering=False, num_devices=1)
    aps = {n: nc.dram_tensor(n, a.shape, mybir.dt.from_np(a.dtype), kind="ExternalInput").ap()
           for n, a in arrays.items()}
    shape = host["L0_attn_x"].shape
    out = nc.dram_tensor("out_x", shape, F32, kind="ExternalOutput").ap()
    program(nc, aps["in_x"], {n[3:]: v for n, v in aps.items() if n != "in_x"}, at, out)
    r = run_bass_kernel_spmd(nc, [arrays], core_ids=[0])
    return r.results[0]["out_x"]
```
